# Optimizing a Trainium2 kernel written in Bass

```python
import numpy as np
import jax
import jax.numpy as jnp

def _softmax(x, axis=-1):
    return jax.nn.softmax(x, axis=axis)

def _gelu(x):
    return jax.nn.gelu(x, approximate=True)

def _silu(x):
    return jax.nn.silu(x)

def _sigmoid(x):
    return jax.nn.sigmoid(x)

def _layernorm(x, axis=-1, eps=1e-05):
    m = jnp.mean(x, axis=axis, keepdims=True)
    v = jnp.var(x, axis=axis, keepdims=True)
    return (x - m) / jnp.sqrt(v + eps)

def _scatter_add(tgt, idx, src, axis=0):
    return tgt.at[idx].add(src)

def _segment_sum(src, seg, n):
    return jax.ops.segment_sum(src, seg, n)
kernel_name = 'mk_gps_d2_gnn_r8_fdaf3f'

def setup_inputs(seed: int=0):
    np.random.seed(seed)
    _w = jnp.asarray

    def _rec_inputs():
        import jax
        import jax.numpy as jnp
        _gk = jax.random.key(seed)
        x = 7.22e-05 + 1 * jax.random.normal(jax.random.fold_in(_gk, 1), (2048, 512), jnp.float32)
        src = jax.random.randint(jax.random.fold_in(_gk, 2), (32768,), 0, 2048, jnp.int32)
        dst = jnp.minimum((2048 * jax.random.uniform(jax.random.fold_in(_gk, 3), (32768,)) ** 2.0).astype(jnp.int32), 16383)
        _o = jnp.argsort(dst, stable=True)
        src = src[_o]
        dst = dst[_o]
        edge_attr_16 = -0.000585658 + 0.999949 * jax.random.normal(jax.random.fold_in(_gk, 12), (32768, 16), jnp.float32)
        edge_attr_64 = -5.3897e-05 + 0.999841 * jax.random.normal(jax.random.fold_in(_gk, 13), (32768, 64), jnp.float32)
        return (x, src, dst, edge_attr_16, edge_attr_64)
    x, src, dst, edge_attr_16, edge_attr_64 = _rec_inputs()

    def _L0_gnn_setup():
        import jax, jax.numpy as jnp
        import numpy as np
        B = 32
        N = 512
        HID = 512
        H = 8
        E = 32768
        ED = 16
        key = jax.random.key(seed)
        ks = jax.random.split(key, 12)
        x = jax.random.normal(ks[0], (B * N, HID), jnp.float32)
        batch = jnp.repeat(jnp.arange(B, dtype=jnp.int64), N)
        g = jax.random.randint(ks[1], (E,), 0, B)
        src = g * N + jax.random.randint(ks[2], (E,), 0, N)
        dst = g * N + jax.random.randint(ks[3], (E,), 0, N)
        edge_index = jnp.stack([src, dst]).astype(jnp.int64)
        edge_attr = jax.random.normal(ks[4], (E, ED), jnp.float32)
        s = 1.0 / np.sqrt(HID).astype(np.float32)
        Wq = jax.random.normal(ks[5], (HID, HID), jnp.float32) * s
        Wk = jax.random.normal(ks[6], (HID, HID), jnp.float32) * s
        Wv = jax.random.normal(ks[7], (HID, HID), jnp.float32) * s
        Wo = jax.random.normal(ks[8], (HID, HID), jnp.float32) * s
        We = jax.random.normal(ks[9], (ED, H), jnp.float32) * (1.0 / np.sqrt(ED).astype(np.float32))
        bq = jnp.zeros((HID,), jnp.float32)
        bk = jnp.zeros((HID,), jnp.float32)
        bv = jnp.zeros((HID,), jnp.float32)
        bo = jnp.zeros((HID,), jnp.float32)
        be = jnp.zeros((H,), jnp.float32)
        return dict(x=x, batch=batch, edge_index=edge_index, edge_attr=edge_attr, Wq=Wq, bq=bq, Wk=Wk, bk=bk, Wv=Wv, bv=bv, Wo=Wo, bo=bo, We=We, be=be, num_graphs=B)
    _L0_gnn_all = _L0_gnn_setup()
    _L0_gnn_in = {k: v for k, v in _L0_gnn_all.items() if k in ('Wq', 'bq', 'Wk', 'bk', 'Wv', 'bv', 'Wo', 'bo', 'We', 'be')}
    del _L0_gnn_all

    def _L0_mix_setup():
        import jax, jax.numpy as jnp
        import numpy as np
        HEADS = 8
        DIM_HEAD = 64
        EPS = 0.0001

        def softmax_kernel(data, proj, is_query):
            data_normalizer = data.shape[-1] ** (-0.25)
            ratio = proj.shape[0] ** (-0.5)
            data_dash = jnp.einsum('bhnd,md->bhnm', data_normalizer * data, proj)
            diag = (data * data).sum(-1) * 0.5 * data_normalizer ** 2
            diag = diag[..., None]
            if is_query:
                stab = jnp.max(data_dash, axis=-1, keepdims=True)
            else:
                stab = jnp.max(data_dash)
            return ratio * (jnp.exp(data_dash - diag - stab) + EPS)

        def linear_attention(q, k, v):
            k_cumsum = k.sum(axis=-2)
            d_inv = 1.0 / jnp.einsum('bhnm,bhm->bhn', q, k_cumsum)
            context = jnp.einsum('bhnm,bhne->bhme', k, v)
            return jnp.einsum('bhme,bhnm,bhn->bhne', context, q, d_inv)
        key = jax.random.key(seed)
        ks = jax.random.split(key, 6)
        b, n, dim = (8, 512, 512)
        m, dh = (266, DIM_HEAD)
        x = jax.random.normal(ks[0], (b, n, dim), dtype=jnp.float32)
        s = dim ** (-0.5)
        Wq = jax.random.normal(ks[1], (dim, dim), dtype=jnp.float32) * s
        Wk = jax.random.normal(ks[2], (dim, dim), dtype=jnp.float32) * s
        Wv = jax.random.normal(ks[3], (dim, dim), dtype=jnp.float32) * s
        Wo = jax.random.normal(ks[4], (dim, dim), dtype=jnp.float32) * s
        bo = jnp.zeros((dim,), dtype=jnp.float32)
        proj = jax.random.normal(ks[5], (m, dh), dtype=jnp.float32)
        return {'x': x, 'Wq': Wq, 'Wk': Wk, 'Wv': Wv, 'Wo': Wo, 'bo': bo, 'proj': proj}
    _L0_mix_all = _L0_mix_setup()
    _L0_mix_in = {k: v for k, v in _L0_mix_all.items() if k in ('Wq', 'Wk', 'Wv', 'Wo', 'bo', 'proj')}
    del _L0_mix_all

    def _L0_ffn_setup():
        import jax, jax.numpy as jnp
        import numpy as np
        E, TOPK, H, DK, DV, D = (4, 2, 8, 64, 64, 512)
        B, L = (4, 1024)
        VDIM = H * DV

        def _silu(x):
            return x * jax.nn.sigmoid(x)

        def _l2norm(x):
            return x * jax.lax.rsqrt(jnp.sum(x * x, axis=-1, keepdims=True) + 1e-06)

        def _forward(h, Wq, Wgate, Wk, Wv, Wb, Wa, A_log, dt_bias, Wg, o_norm_weight, Wo):
            Bs, Ls, _ = h.shape
            scores = jax.nn.softmax((h @ Wgate).astype(jnp.float32), axis=-1)
            rw, sel = jax.lax.top_k(scores, TOPK)
            rw = rw / jnp.sum(rw, axis=-1, keepdims=True)
            bi = jnp.arange(Bs)[:, None, None]
            li = jnp.arange(Ls)[None, :, None]
            w_full = jnp.zeros((Bs, Ls, E), jnp.float32).at[bi, li, sel].set(rw)
            m = jnp.transpose(w_full > 0, (2, 0, 1))
            q = _l2norm(_silu(h @ Wq).reshape(Bs, Ls, H, DK))
            k = _l2norm(_silu(h @ Wk).reshape(Bs, Ls, H, DK))
            v = _silu(h @ Wv).reshape(Bs, Ls, H, DV)
            beta = jax.nn.sigmoid(h @ Wb)
            g = -jnp.exp(A_log) * jax.nn.softplus((h @ Wa).astype(jnp.float32) + dt_bias)
            beta_e = beta[None] * m[..., None]
            g_e = jnp.where(m[..., None], g[None], 0.0)
            scale = DK ** (-0.5)
            xs = (jnp.moveaxis(q, 1, 0), jnp.moveaxis(k, 1, 0), jnp.moveaxis(v, 1, 0), jnp.moveaxis(beta_e, 2, 0), jnp.moveaxis(g_e, 2, 0))

            def step(S, x):
                qt, kt, vt, bt, gt = x
                S = S * jnp.exp(gt)[..., None, None]
                kv = jnp.einsum('bhk,ebhkv->ebhv', kt, S)
                delta = (vt[None] - kv) * bt[..., None]
                S = S + kt[None, :, :, :, None] * delta[..., None, :]
                ot = jnp.einsum('bhk,ebhkv->ebhv', qt * scale, S)
                return (S, ot)
            S0 = jnp.zeros((E, Bs, H, DK, DV), jnp.float32)
            _, o = jax.lax.scan(step, S0, xs)
            o = jnp.moveaxis(o, 0, 2)
            core = jnp.einsum('ble,eblhv->blhv', w_full, o)
            gate = _silu((h @ Wg).reshape(Bs, Ls, H, DV))
            core = core * jax.lax.rsqrt(jnp.mean(core * core, axis=-1, keepdims=True) + 1e-05)
            core = core * o_norm_weight * gate
            return core.reshape(Bs, Ls, VDIM) @ Wo
        key = jax.random.key(seed)
        ks = jax.random.split(key, 12)
        std = 0.02
        h = jax.random.normal(ks[0], (B, L, D), jnp.float32)
        Wq = jax.random.normal(ks[1], (D, H * DK), jnp.float32) * std
        Wgate = jax.random.normal(ks[2], (D, E), jnp.float32) * std
        Wk = jax.random.normal(ks[3], (D, H * DK), jnp.float32) * std
        Wv = jax.random.normal(ks[4], (D, VDIM), jnp.float32) * std
        Wb = jax.random.normal(ks[5], (D, H), jnp.float32) * std
        Wa = jax.random.normal(ks[6], (D, H), jnp.float32) * std
        Wg = jax.random.normal(ks[7], (D, VDIM), jnp.float32) * std
        Wo = jax.random.normal(ks[8], (VDIM, D), jnp.float32) * std
        A = jax.random.uniform(ks[9], (H,), jnp.float32, 0.0001, 16.0)
        A_log = jnp.log(A)
        dt = jnp.exp(jax.random.uniform(ks[10], (H,), jnp.float32) * (np.float32(np.log(0.1)) - np.float32(np.log(0.001))) + np.float32(np.log(0.001)))
        dt = jnp.maximum(dt, 0.0001)
        dt_bias = dt + jnp.log(-jnp.expm1(-dt))
        o_norm_weight = jnp.ones((DV,), jnp.float32)
        return {'hidden_states': h, 'Wq': Wq, 'Wgate': Wgate, 'Wk': Wk, 'Wv': Wv, 'Wb': Wb, 'Wa': Wa, 'A_log': A_log, 'dt_bias': dt_bias, 'Wg': Wg, 'o_norm_weight': o_norm_weight, 'Wo': Wo}
    _L0_ffn_all = _L0_ffn_setup()
    _L0_ffn_in = {k: v for k, v in _L0_ffn_all.items() if k in ('Wq', 'Wgate', 'Wk', 'Wv', 'Wb', 'Wa', 'A_log', 'dt_bias', 'Wg', 'o_norm_weight', 'Wo')}
    del _L0_ffn_all

    def _L1_gnn_setup():
        import jax, jax.numpy as jnp
        import numpy as np
        N, E, H, ED = (6250, 50000, 512, 64)
        BN_EPS = 1e-05

        def _bn(h, g, b):
            mu = jnp.mean(h, axis=0)
            var = jnp.mean(jnp.square(h - mu), axis=0)
            return (h - mu) * jax.lax.rsqrt(var + BN_EPS) * g + b
        key = jax.random.key(seed)
        ks = jax.random.split(key, 8)
        s = lambda d: 1.0 / np.sqrt(d)
        return {'x': jax.random.normal(ks[0], (N, H), jnp.float32), 'edge_attr': jax.random.normal(ks[1], (E, ED), jnp.float32), 'edge_index': jax.random.randint(ks[2], (2, E), 0, N, jnp.int32), 'W_e': jax.random.normal(ks[3], (ED, H), jnp.float32) * s(ED), 'b_e': jnp.zeros((H,), jnp.float32), 'W1': jax.random.normal(ks[4], (H, 2 * H), jnp.float32) * s(H), 'b1': jnp.zeros((2 * H,), jnp.float32), 'g1': jnp.ones((2 * H,), jnp.float32), 'beta1': jnp.zeros((2 * H,), jnp.float32), 'W2': jax.random.normal(ks[5], (2 * H, H), jnp.float32) * s(2 * H), 'b2': jnp.zeros((H,), jnp.float32), 'g2': jnp.ones((H,), jnp.float32), 'beta2': jnp.zeros((H,), jnp.float32), 'eps': jnp.zeros((), jnp.float32)}
    _L1_gnn_all = _L1_gnn_setup()
    _L1_gnn_in = {k: v for k, v in _L1_gnn_all.items() if k in ('W_e', 'b_e', 'W1', 'b1', 'g1', 'beta1', 'W2', 'b2', 'g2', 'beta2', 'eps')}
    del _L1_gnn_all

    def _L1_mix_setup():
        import jax, jax.numpy as jnp
        import numpy as np
        NUM_HEADS = 8
        EPS = 1e-06
        key = jax.random.key(seed)
        k1, k2, k3, k4 = jax.random.split(key, 4)
        B, N, C = (16, 512, 512)
        x = jax.random.normal(k1, (B, N, C), dtype=jnp.float32)
        W_qkv = jax.random.normal(k2, (3 * C, C), dtype=jnp.float32) * C ** (-0.5)
        W_proj = jax.random.normal(k3, (C, C), dtype=jnp.float32) * C ** (-0.5)
        b_proj = jax.random.normal(k4, (C,), dtype=jnp.float32) * 0.02
        return {'x': x, 'W_qkv': W_qkv, 'W_proj': W_proj, 'b_proj': b_proj}
    _L1_mix_all = _L1_mix_setup()
    _L1_mix_in = {k: v for k, v in _L1_mix_all.items() if k in ('W_qkv', 'W_proj', 'b_proj')}
    del _L1_mix_all

    def _L1_ffn_setup():
        import jax, jax.numpy as jnp
        import numpy as np
        EPS = 1e-06
        SINKHORN_ITERS = 8
        TEMPERATURE = 1.0
        B, N, D = (4, 1024, 512)
        E, OUT = (8, 512)
        H = 1

        def _sinkhorn(logits):
            t = jnp.log(jnp.clip(logits, EPS)) / TEMPERATURE
            for _ in range(SINKHORN_ITERS):
                t = t - jax.nn.logsumexp(t, axis=-2, keepdims=True)
                t = t - jax.nn.logsumexp(t, axis=-1, keepdims=True)
            return jnp.exp(t)
        key = jax.random.key(seed)
        k1, k2, k3 = jax.random.split(key, 3)
        x = jax.random.normal(k1, (B, N, D), dtype=jnp.float32)
        gate_weight = jax.random.normal(k2, (H, D, E), dtype=jnp.float32)
        experts = jax.random.normal(k3, (E, D, OUT), dtype=jnp.float32) * 0.02
        return {'x': x, 'gate_weight': gate_weight, 'experts': experts}
    _L1_ffn_all = _L1_ffn_setup()
    _L1_ffn_in = {k: v for k, v in _L1_ffn_all.items() if k in ('gate_weight', 'experts')}
    del _L1_ffn_all
    return {'x': x, 'src': src, 'dst': dst, 'edge_attr_16': edge_attr_16, 'edge_attr_64': edge_attr_64, 'L0_gnn_Wq': _L0_gnn_in['Wq'], 'L0_gnn_bq': _L0_gnn_in['bq'], 'L0_gnn_Wk': _L0_gnn_in['Wk'], 'L0_gnn_bk': _L0_gnn_in['bk'], 'L0_gnn_Wv': _L0_gnn_in['Wv'], 'L0_gnn_bv': _L0_gnn_in['bv'], 'L0_gnn_Wo': _L0_gnn_in['Wo'], 'L0_gnn_bo': _L0_gnn_in['bo'], 'L0_gnn_We': _L0_gnn_in['We'], 'L0_gnn_be': _L0_gnn_in['be'], 'L0_mix_Wq': _L0_mix_in['Wq'], 'L0_mix_Wk': _L0_mix_in['Wk'], 'L0_mix_Wv': _L0_mix_in['Wv'], 'L0_mix_Wo': _L0_mix_in['Wo'], 'L0_mix_bo': _L0_mix_in['bo'], 'L0_mix_proj': _L0_mix_in['proj'], 'L0_ffn_Wq': _L0_ffn_in['Wq'], 'L0_ffn_Wgate': _L0_ffn_in['Wgate'], 'L0_ffn_Wk': _L0_ffn_in['Wk'], 'L0_ffn_Wv': _L0_ffn_in['Wv'], 'L0_ffn_Wb': _L0_ffn_in['Wb'], 'L0_ffn_Wa': _L0_ffn_in['Wa'], 'L0_ffn_A_log': _L0_ffn_in['A_log'], 'L0_ffn_dt_bias': _L0_ffn_in['dt_bias'], 'L0_ffn_Wg': _L0_ffn_in['Wg'], 'L0_ffn_o_norm_weight': _L0_ffn_in['o_norm_weight'], 'L0_ffn_Wo': _L0_ffn_in['Wo'], 'L1_gnn_W_e': _L1_gnn_in['W_e'], 'L1_gnn_b_e': _L1_gnn_in['b_e'], 'L1_gnn_W1': _L1_gnn_in['W1'], 'L1_gnn_b1': _L1_gnn_in['b1'], 'L1_gnn_g1': _L1_gnn_in['g1'], 'L1_gnn_beta1': _L1_gnn_in['beta1'], 'L1_gnn_W2': _L1_gnn_in['W2'], 'L1_gnn_b2': _L1_gnn_in['b2'], 'L1_gnn_g2': _L1_gnn_in['g2'], 'L1_gnn_beta2': _L1_gnn_in['beta2'], 'L1_gnn_eps': _L1_gnn_in['eps'], 'L1_mix_W_qkv': _L1_mix_in['W_qkv'], 'L1_mix_W_proj': _L1_mix_in['W_proj'], 'L1_mix_b_proj': _L1_mix_in['b_proj'], 'L1_ffn_gate_weight': _L1_ffn_in['gate_weight'], 'L1_ffn_experts': _L1_ffn_in['experts']}

def reference(x, src, dst, edge_attr_16, edge_attr_64, L0_gnn_Wq, L0_gnn_bq, L0_gnn_Wk, L0_gnn_bk, L0_gnn_Wv, L0_gnn_bv, L0_gnn_Wo, L0_gnn_bo, L0_gnn_We, L0_gnn_be, L0_mix_Wq, L0_mix_Wk, L0_mix_Wv, L0_mix_Wo, L0_mix_bo, L0_mix_proj, L0_ffn_Wq, L0_ffn_Wgate, L0_ffn_Wk, L0_ffn_Wv, L0_ffn_Wb, L0_ffn_Wa, L0_ffn_A_log, L0_ffn_dt_bias, L0_ffn_Wg, L0_ffn_o_norm_weight, L0_ffn_Wo, L1_gnn_W_e, L1_gnn_b_e, L1_gnn_W1, L1_gnn_b1, L1_gnn_g1, L1_gnn_beta1, L1_gnn_W2, L1_gnn_b2, L1_gnn_g2, L1_gnn_beta2, L1_gnn_eps, L1_mix_W_qkv, L1_mix_W_proj, L1_mix_b_proj, L1_ffn_gate_weight, L1_ffn_experts):
    import jax
    import jax.numpy as jnp

    def _L0_gnn_ref(x, batch, edge_index, edge_attr, Wq, bq, Wk, bk, Wv, bv, Wo, bo, We, be, num_graphs):
        import jax, jax.numpy as jnp
        import numpy as np
        B = 32
        N = 512
        HID = 512
        H = 8
        E = 32768
        ED = 16
        n_total, hid = x.shape
        n = n_total // num_graphs
        hd = hid // H
        scale = 1.0 / jnp.sqrt(jnp.asarray(hd, x.dtype))
        q = (x @ Wq + bq).reshape(num_graphs, n, H, hd)
        k = (x @ Wk + bk).reshape(num_graphs, n, H, hd)
        v = (x @ Wv + bv).reshape(num_graphs, n, H, hd)
        attn = jnp.einsum('bnhd,bmhd->bnmh', q, k) * scale
        eb = edge_attr @ We + be
        b_idx = edge_index[0] // n
        loc_src = edge_index[0] % n
        loc_dst = edge_index[1] % n
        attn = attn.at[b_idx, loc_src, loc_dst].add(eb)
        attn = jax.nn.softmax(attn, axis=2)
        out = jnp.einsum('bnmh,bmhd->bnhd', attn, v).reshape(n_total, hid)
        return out @ Wo + bo

    def _L0_mix_ref(x, Wq, Wk, Wv, Wo, bo, proj):
        import jax, jax.numpy as jnp
        import numpy as np
        HEADS = 8
        DIM_HEAD = 64
        EPS = 0.0001

        def softmax_kernel(data, proj, is_query):
            data_normalizer = data.shape[-1] ** (-0.25)
            ratio = proj.shape[0] ** (-0.5)
            data_dash = jnp.einsum('bhnd,md->bhnm', data_normalizer * data, proj)
            diag = (data * data).sum(-1) * 0.5 * data_normalizer ** 2
            diag = diag[..., None]
            if is_query:
                stab = jnp.max(data_dash, axis=-1, keepdims=True)
            else:
                stab = jnp.max(data_dash)
            return ratio * (jnp.exp(data_dash - diag - stab) + EPS)

        def linear_attention(q, k, v):
            k_cumsum = k.sum(axis=-2)
            d_inv = 1.0 / jnp.einsum('bhnm,bhm->bhn', q, k_cumsum)
            context = jnp.einsum('bhnm,bhne->bhme', k, v)
            return jnp.einsum('bhme,bhnm,bhn->bhne', context, q, d_inv)
        b, n, dim = x.shape
        h, dh = (HEADS, DIM_HEAD)
        q = (x @ Wq).reshape(b, n, h, dh).transpose(0, 2, 1, 3)
        k = (x @ Wk).reshape(b, n, h, dh).transpose(0, 2, 1, 3)
        v = (x @ Wv).reshape(b, n, h, dh).transpose(0, 2, 1, 3)
        qp = softmax_kernel(q, proj, is_query=True)
        kp = softmax_kernel(k, proj, is_query=False)
        out = linear_attention(qp, kp, v)
        out = out.transpose(0, 2, 1, 3).reshape(b, n, h * dh)
        return out @ Wo + bo

    def _L0_ffn_ref(hidden_states, Wq, Wgate, Wk, Wv, Wb, Wa, A_log, dt_bias, Wg, o_norm_weight, Wo):
        import jax, jax.numpy as jnp
        import numpy as np
        E, TOPK, H, DK, DV, D = (4, 2, 8, 64, 64, 512)
        B, L = (4, 1024)
        VDIM = H * DV

        def _silu(x):
            return x * jax.nn.sigmoid(x)

        def _l2norm(x):
            return x * jax.lax.rsqrt(jnp.sum(x * x, axis=-1, keepdims=True) + 1e-06)

        def _forward(h, Wq, Wgate, Wk, Wv, Wb, Wa, A_log, dt_bias, Wg, o_norm_weight, Wo):
            Bs, Ls, _ = h.shape
            scores = jax.nn.softmax((h @ Wgate).astype(jnp.float32), axis=-1)
            rw, sel = jax.lax.top_k(scores, TOPK)
            rw = rw / jnp.sum(rw, axis=-1, keepdims=True)
            bi = jnp.arange(Bs)[:, None, None]
            li = jnp.arange(Ls)[None, :, None]
            w_full = jnp.zeros((Bs, Ls, E), jnp.float32).at[bi, li, sel].set(rw)
            m = jnp.transpose(w_full > 0, (2, 0, 1))
            q = _l2norm(_silu(h @ Wq).reshape(Bs, Ls, H, DK))
            k = _l2norm(_silu(h @ Wk).reshape(Bs, Ls, H, DK))
            v = _silu(h @ Wv).reshape(Bs, Ls, H, DV)
            beta = jax.nn.sigmoid(h @ Wb)
            g = -jnp.exp(A_log) * jax.nn.softplus((h @ Wa).astype(jnp.float32) + dt_bias)
            beta_e = beta[None] * m[..., None]
            g_e = jnp.where(m[..., None], g[None], 0.0)
            scale = DK ** (-0.5)
            xs = (jnp.moveaxis(q, 1, 0), jnp.moveaxis(k, 1, 0), jnp.moveaxis(v, 1, 0), jnp.moveaxis(beta_e, 2, 0), jnp.moveaxis(g_e, 2, 0))

            def step(S, x):
                qt, kt, vt, bt, gt = x
                S = S * jnp.exp(gt)[..., None, None]
                kv = jnp.einsum('bhk,ebhkv->ebhv', kt, S)
                delta = (vt[None] - kv) * bt[..., None]
                S = S + kt[None, :, :, :, None] * delta[..., None, :]
                ot = jnp.einsum('bhk,ebhkv->ebhv', qt * scale, S)
                return (S, ot)
            S0 = jnp.zeros((E, Bs, H, DK, DV), jnp.float32)
            _, o = jax.lax.scan(step, S0, xs)
            o = jnp.moveaxis(o, 0, 2)
            core = jnp.einsum('ble,eblhv->blhv', w_full, o)
            gate = _silu((h @ Wg).reshape(Bs, Ls, H, DV))
            core = core * jax.lax.rsqrt(jnp.mean(core * core, axis=-1, keepdims=True) + 1e-05)
            core = core * o_norm_weight * gate
            return core.reshape(Bs, Ls, VDIM) @ Wo
        return _forward(hidden_states, Wq, Wgate, Wk, Wv, Wb, Wa, A_log, dt_bias, Wg, o_norm_weight, Wo)

    def _L1_gnn_ref(x, edge_attr, edge_index, W_e, b_e, W1, b1, g1, beta1, W2, b2, g2, beta2, eps):
        import jax, jax.numpy as jnp
        import numpy as np
        N, E, H, ED = (6250, 50000, 512, 64)
        BN_EPS = 1e-05

        def _bn(h, g, b):
            mu = jnp.mean(h, axis=0)
            var = jnp.mean(jnp.square(h - mu), axis=0)
            return (h - mu) * jax.lax.rsqrt(var + BN_EPS) * g + b
        src, dst = (edge_index[0], edge_index[1])
        msg = jax.nn.relu(x[src] + edge_attr @ W_e + b_e)
        aggr = jax.ops.segment_sum(msg, dst, num_segments=x.shape[0])
        h = (1.0 + eps) * x + aggr
        h = jax.nn.silu(_bn(h @ W1 + b1, g1, beta1))
        h = h @ W2 + b2
        return jax.nn.silu(_bn(h, g2, beta2))

    def _L1_mix_ref(x, W_qkv, W_proj, b_proj):
        import jax, jax.numpy as jnp
        import numpy as np
        NUM_HEADS = 8
        EPS = 1e-06
        B, N, C = x.shape
        H = NUM_HEADS
        E = C // H
        scale = E ** (-0.5)
        qkv = (x @ W_qkv.T).reshape(B, N, 3, H, E)
        q, k, v = (qkv[:, :, 0], qkv[:, :, 1], qkv[:, :, 2])
        q_ = jax.nn.relu(q) + scale
        k_ = jax.nn.relu(k) + scale
        kv = jnp.einsum('bnhe,bnhf->bhef', k_, v)
        k_sum = jnp.sum(k_, axis=1)
        z = 1.0 / (jnp.einsum('bnhe,bhe->bnh', q_, k_sum) + EPS)
        out = jnp.einsum('bnhe,bhef->bnhf', q_, kv) * z[..., None]
        out = out.reshape(B, N, C)
        return out @ W_proj.T + b_proj

    def _L1_ffn_ref(x, gate_weight, experts):
        import jax, jax.numpy as jnp
        import numpy as np
        EPS = 1e-06
        SINKHORN_ITERS = 8
        TEMPERATURE = 1.0
        B, N, D = (4, 1024, 512)
        E, OUT = (8, 512)
        H = 1

        def _sinkhorn(logits):
            t = jnp.log(jnp.clip(logits, EPS)) / TEMPERATURE
            for _ in range(SINKHORN_ITERS):
                t = t - jax.nn.logsumexp(t, axis=-2, keepdims=True)
                t = t - jax.nn.logsumexp(t, axis=-1, keepdims=True)
            return jnp.exp(t)
        b, n, d = x.shape
        e = experts.shape[0]
        m = n // e
        xh = x[:, None, :, :]
        gate_logits = jnp.einsum('bhnd,hde->bhne', xh, gate_weight)
        gates = _sinkhorn(gate_logits)
        g_t = jnp.swapaxes(gates, -1, -2)
        vals, idx = jax.lax.top_k(g_t, m)
        gate_values = jnp.transpose(vals, (2, 0, 1, 3))[..., None]
        routed = jnp.take_along_axis(xh[:, :, None, :, :], idx[..., None], axis=3)
        routed = jnp.transpose(routed, (2, 0, 1, 3, 4))
        expert_w = experts[:, None, :, :]
        outputs = jnp.einsum('ebhmi,ehio->ebhmo', routed, expert_w)
        outputs = outputs * gate_values
        bh_idx = idx.reshape(b, 1, e * m)
        bh_vals = jnp.transpose(outputs, (1, 2, 0, 3, 4)).reshape(b, 1, e * m, outputs.shape[-1])

        def scat(i1, v1):
            return jnp.zeros((n, v1.shape[-1]), dtype=v1.dtype).at[i1].set(v1)
        routed_back = jax.vmap(jax.vmap(scat))(bh_idx, bh_vals)
        return routed_back[:, 0]
    edge_index = jnp.stack([src, dst])
    batch0 = jnp.zeros((2048,), jnp.int32)
    xn = _layernorm(x, axis=-1)
    x = x + _L0_gnn_ref(xn, batch0, edge_index, edge_attr_16, L0_gnn_Wq, L0_gnn_bq, L0_gnn_Wk, L0_gnn_bk, L0_gnn_Wv, L0_gnn_bv, L0_gnn_Wo, L0_gnn_bo, L0_gnn_We, L0_gnn_be, 32) + _L0_mix_ref(xn[None], L0_mix_Wq, L0_mix_Wk, L0_mix_Wv, L0_mix_Wo, L0_mix_bo, L0_mix_proj)[0]
    x = x + _L0_ffn_ref(_layernorm(x, axis=-1)[None], L0_ffn_Wq, L0_ffn_Wgate, L0_ffn_Wk, L0_ffn_Wv, L0_ffn_Wb, L0_ffn_Wa, L0_ffn_A_log, L0_ffn_dt_bias, L0_ffn_Wg, L0_ffn_o_norm_weight, L0_ffn_Wo)[0]
    xn = _layernorm(x, axis=-1)
    x = x + _L1_gnn_ref(xn, edge_attr_64, edge_index, L1_gnn_W_e, L1_gnn_b_e, L1_gnn_W1, L1_gnn_b1, L1_gnn_g1, L1_gnn_beta1, L1_gnn_W2, L1_gnn_b2, L1_gnn_g2, L1_gnn_beta2, L1_gnn_eps) + _L1_mix_ref(xn[None], L1_mix_W_qkv, L1_mix_W_proj, L1_mix_b_proj)[0]
    x = x + _L1_ffn_ref(_layernorm(x, axis=-1)[None], L1_ffn_gate_weight, L1_ffn_experts)[0]
    return x

_drawn_inputs = setup_inputs


def setup_inputs(seed=0):
    import zlib

    import numpy as np

    out = dict(_drawn_inputs(seed))
    spreads = {'L0_gnn_bq': (0.0, 0.1),
     'L0_gnn_bk': (0.0, 0.8),
     'L0_gnn_bv': (0.0, 0.1),
     'L0_gnn_bo': (0.0, 0.1),
     'L0_gnn_be': (0.0, 0.295),
     'L0_mix_bo': (0.0, 0.1),
     'L0_ffn_o_norm_weight': (1.0, 0.545),
     'L1_gnn_b_e': (0.0, 0.1),
     'L1_gnn_b1': (0.0, 0.8),
     'L1_gnn_g1': (1.0, 0.2),
     'L1_gnn_beta1': (0.0, 0.1),
     'L1_gnn_b2': (0.0, 0.8),
     'L1_gnn_g2': (1.0, 0.2),
     'L1_gnn_beta2': (0.0, 0.1)}
    factors = {'L0_mix_Wq': 8.0, 'L0_mix_Wk': 8.0, 'L0_mix_proj': 8.0, 'L0_ffn_Wa': 4.284}
    for name, (base, spread) in spreads.items():
        noise = np.random.default_rng([zlib.crc32(name.encode()), seed]).standard_normal(out[name].shape)
        drawn = base * np.exp(spread * noise) if base else spread * noise
        out[name] = jnp.asarray(drawn.astype(out[name].dtype))
    for name, factor in factors.items():
        out[name] = (out[name] * factor).astype(out[name].dtype)
    return out
```

```python
import numpy as np
import concourse.bass as bass
from concourse import mybir
from contextlib import ExitStack

F32 = mybir.dt.float32
I32 = mybir.dt.int32
ALU = mybir.AluOpType
ACT = mybir.ActivationFunctionType
AX = mybir.AxisListType

P = 128
N, D = 2048, 512
NT = N // P
KC = D // P
H, HD = 8, 64
G = 64
E = 32768
EC = E // P
ET = EC + NT
R0 = H + 2
R1 = 64 + 3
M = 266
MC = [(0, 128), (128, 128), (256, 10)]
EX = 4
SL = 2 * N
ST = SL // P
FE, CAP = 8, N // 8
LEVELS = [1, 2, 4, 8, 16, 32, 64]
EPS_LN = 1e-5
LIMIT = 8000
RESET = -1.0e4


def constants():
    r = np.arange(P)[:, None]
    c = np.arange(P)[None, :]
    parts = {
        "ident": (r == c),
        "ones": np.ones((P, P)),
        "before": (r < c),
        "upto": (r <= c),
        "after": (r > c),
        "lower": (r >= c),
        "iota": np.broadcast_to(c, (P, P)),
    }
    for b in LEVELS:
        parts[f"block{b}"] = ((r // b) % 2 == 1) & (c // b == r // b - 1)
    parts["tile_start"] = np.broadcast_to(np.arange(ET)[None, :] * P, (P, ET))
    sel = np.zeros((P, KC, H))
    for k in range(KC):
        for p in range(P):
            sel[p, k, 2 * k + p // HD] = 1
    parts["head_of_row"] = sel.reshape(P, -1)
    parts["parity"] = np.stack([(np.arange(P) < HD), (np.arange(P) >= HD)], 1)
    parts["earlier"] = np.broadcast_to((np.arange(EX)[None, :] < np.arange(EX)[:, None]).reshape(1, -1), (P, EX * EX))
    at, n = {}, 0
    for name, a in parts.items():
        at[name] = (n, a.shape[1])
        n += a.shape[1]
    return np.ascontiguousarray(np.concatenate([np.asarray(a, np.float32) for a in parts.values()], 1)), at


class Lane:

    def __init__(self, flow, name, engine):
        self.flow, self.name, self.engine, self.sem, self.count, self.seen = flow, name, engine, None, 0, {}

    def wait(self, *events):
        for e in events:
            if e is None:
                continue
            if isinstance(e, list):
                self.wait(*e)
                continue
            sem, value, stage = e
            if value is None:
                value = self.flow.totals[sem] if stage == self.flow.number else 0
            if self.seen.get(sem, 0) < value:
                self.seen[sem] = value
                self.engine.wait_ge(sem, value)

    def __call__(self, build, *after):
        self.wait(*after)
        self.count += 1
        build(self.engine).then_inc(self.sem, 1)
        return (self.sem, self.count, self.flow.number)


class Flow:

    def __init__(self, nc, ctx):
        self.nc, self.ctx = nc, ctx
        self.lanes = [Lane(self, *x) for x in (("pe", nc.tensor), ("act", nc.scalar), ("dve", nc.vector),
                                               ("pool", nc.gpsimd), ("sp", nc.sync))]
        self.number, self.rings, self.totals, self.idle = 0, {}, {}, {True: [], False: []}

    def stage(self, name):
        ends = [(lane.sem, lane.count, self.number) for lane in self.lanes if lane.count]
        ends += [(sem, None, self.number) for sem in self.rings.values()]
        for lane in self.lanes:
            lane.wait(ends)
        for lane in self.lanes:
            if lane.sem is None or lane.count > LIMIT:
                lane.sem = self.ctx.enter_context(self.nc.semaphore(f"{lane.name}_from_{name}"))
                lane.count = 0
        for (software, _), sem in self.rings.items():
            self.idle[software].append(sem)
        self.number, self.rings, self.name = self.number + 1, {}, name

    def dma(self, lane, ring, build, *after):
        lane.wait(*after)
        ring = (lane.name == "pool", ring)
        if ring not in self.rings:
            idle = self.idle[ring[0]]
            if not idle:
                idle.append(self.ctx.enter_context(self.nc.semaphore(f"ring{len(self.totals)}")))
                self.totals[idle[-1]] = 0
            self.rings[ring] = idle.pop()
        sem = self.rings[ring]
        self.totals[sem] += 16
        build(lane.engine).then_inc(sem, 16)
        return (sem, None, self.number)


def interleave(steps, width):
    steps = list(steps)
    live = []
    while steps or live:
        if steps and len(live) < width:
            live.append(steps.pop(0))
        for g in list(live):
            if next(g, StopIteration) is StopIteration:
                live.remove(g)


def mid(ap, n):
    return ap.unsqueeze(2).broadcast_to([ap.shape[0], ap.shape[1], n])


def rep(ap, n):
    return ap.unsqueeze(1).broadcast_to([ap.shape[0], n, ap.shape[1]])


def program(nc, I, const_at, out, stop=99):
    ctx = ExitStack()
    with ctx:
        f = Flow(nc, ctx)
        pe, act, dve, pool, sp = f.lanes
        bank = [ctx.enter_context(nc.psum_tensor(f"bank{i}", [P, 512], F32)) for i in range(8)]

        def scratch(name, shape, dt=F32):
            return nc.dram_tensor(name, shape, dt, kind="Internal").ap()

        sorted_bias = scratch("sorted_bias", (P * ET, R0))
        sorted_edge = scratch("sorted_edge", (P * ET, R1))
        xn_rows = scratch("xn_rows", (N, D))
        gate_rows = scratch("gate_rows", (N, D))
        slot_qkv = scratch("slot_qkv", (SL, 3 * D))
        slot_gates = scratch("slot_gates", (SL, 2 * H))
        slot_out = scratch("slot_out", (SL, D))
        expert_in = scratch("expert_in", (N, D))
        expert_out = scratch("expert_out", (N, D))

        f.stage("start")
        cw = sum(w for _, w in const_at.values())
        C = ctx.enter_context(nc.sbuf_tensor("C", [P, cw], F32))
        X = ctx.enter_context(nc.sbuf_tensor("X", [P, NT, D], F32))
        bucket0 = ctx.enter_context(nc.sbuf_tensor("bucket0", [P, ET], I32))
        bucket1 = ctx.enter_context(nc.sbuf_tensor("bucket1", [P, ET], I32))
        neg_half = ctx.enter_context(nc.sbuf_tensor("neg_half", [P, P], F32))

        def const(name):
            a, w = const_at[name]
            return C[:, a:a + w]

        ident, ones = const("ident"), const("ones")
        f.dma(sp, "const", lambda e: e.dma_start(C[:, :], I["const"]))
        f.dma(sp, "x", lambda e: e.dma_start(X[:, :, :], I["x"].rearrange("(t p) d -> p t d", p=P)))
        pool(lambda e: e.memset(neg_half[:, :], -0.5))

        def tensors(s):
            def sb(name, shape, dt=F32):
                return s.enter_context(nc.sbuf_tensor(f"{f.name}_{name}", shape, dt))
            return sb

        def rows(ap):
            return ap.rearrange("(c p) n -> p c n", p=P)

        def vec_row(ap, parts, n):
            return ap.rearrange("(a n) -> a n", a=1).broadcast_to([parts, n])

        def rsqrt(dst, src, eps, scale, *after):
            a = dve(lambda e: e.tensor_scalar(dst, src, scale, eps, ALU.mult, ALU.add), *after)
            n = dst.shape[1]
            return pool(lambda e: e.tensor_tensor(dst, dst, neg_half[0:dst.shape[0], 0:n], ALU.pow), a)

        def sort_edges(name, key, local_fields, width, table, bucket_of_tile, fill):
            f.stage(name)
            with ExitStack() as s:
                sb = tensors(s)
                ends = sb("ends", [P, E // P], I32)
                bkt = sb("bkt", [P, EC])
                hot = sb("hot", [P, NT, EC])
                run = sb("run", [P, NT, EC])
                rec = sb("rec", [P, EC, width])
                pad = sb("pad", [P, 17, width])
                small = sb("small", [P, 8, NT])
                ints = sb("ints", [P, 2, NT], I32)
                tmp = sb("tmp", [P, EC], I32)
                pos = sb("pos", [P, EC])
                posi = sb("posi", [P, 2, EC], I32)
                tl = sb("tl", [P, ET])
                a = pool(lambda e: e.memset(pad[:, :, :], 0.0))
                a = pool(lambda e: e.memset(pad[:, :, local_fields:local_fields + 1], -1.0), a)
                blank = [f.dma(sp, "blank", lambda e, i=i: e.dma_start(
                    table[i * 17 * P:(i + 1) * 17 * P, :].rearrange("(p n) w -> p n w", p=P), pad[:, :, :]), a)
                    for i in range(ET // 17)]
                got = f.dma(sp, "key", lambda e: e.dma_start(ends[:, :], key.rearrange("(p c) -> p c", p=P)))
                filled = fill(sb, rec, ends, tmp, got)
                b = dve(lambda e: e.tensor_single_scalar(tmp[:, :], ends[:, :], 7, ALU.logical_shift_right), got, filled)
                b = dve(lambda e: e.tensor_copy(bkt[:, :], tmp[:, :]), b)
                for i in range(NT):
                    b1 = dve(lambda e: e.tensor_single_scalar(hot[:, i, :], bkt[:, :], float(i), ALU.is_equal), b)
                flat = hot[:, :, :].rearrange("p b c -> p (b c)")
                b = dve(lambda e: e.tensor_tensor_scan(run[:, :, :].rearrange("p b c -> p (b c)"), flat, flat, 0.0,
                                                       ALU.add, ALU.max), b1)
                b = dve(lambda e: e.tensor_copy(small[:, 0, :], run[:, :, EC - 1]), b)
                c1 = dve(lambda e: e.tensor_copy(small[:, 1, 0:1], small[:, 0, 0:1]), b)
                c2 = dve(lambda e: e.tensor_tensor(small[:, 1, 1:NT], small[:, 0, 1:NT], small[:, 0, 0:NT - 1],
                                                   ALU.subtract), b)
                pe(lambda e: e.matmul(bank[0][:, 0:NT], const("before"), small[:, 1, :], start=True, stop=True), c1, c2)
                c = pe(lambda e: e.matmul(bank[1][:, 0:NT], ones, small[:, 1, :], start=True, stop=True))
                c = dve(lambda e: e.tensor_scalar(small[:, 2, :], bank[1][:, 0:NT], 127.0, None, ALU.add), c)
                c = dve(lambda e: e.tensor_copy(ints[:, 0, :], small[:, 2, :]), c)
                c = dve(lambda e: e.tensor_scalar(ints[:, 1, :], ints[:, 0, :], 7, 7, ALU.logical_shift_right,
                                                  ALU.logical_shift_left), c)
                c = dve(lambda e: e.tensor_copy(small[:, 3, :], ints[:, 1, :]), c)
                c = dve(lambda e: e.tensor_tensor_scan(small[:, 4, :], small[:, 3, :], small[:, 3, :], 0.0,
                                                       ALU.add, ALU.max), c)
                d = dve(lambda e: e.tensor_tensor(small[:, 5, :], small[:, 4, :], small[:, 3, :], ALU.subtract), c)
                d = dve(lambda e: e.tensor_tensor(small[:, 5, :], small[:, 5, :], bank[0][:, 0:NT], ALU.add), d)
                d = dve(lambda e: e.tensor_tensor(small[:, 5, :], small[:, 5, :], small[:, 0, :], ALU.subtract), d)
                d = dve(lambda e: e.tensor_tensor(small[:, 5, :], small[:, 5, :], small[:, 1, :], ALU.add), d)
                d = dve(lambda e: e.tensor_scalar(small[:, 5, :], small[:, 5, :], -1.0, None, ALU.add), d)
                for i in range(NT):
                    d1 = dve(lambda e: e.scalar_tensor_tensor(run[:, i, :], run[:, i, :], small[:, 5, i:i + 1],
                                                              hot[:, i, :], ALU.add, ALU.mult), d)
                d = dve(lambda e: e.tensor_reduce(pos[:, :], run[:, :, :].rearrange("p b c -> p c b"), AX.X, ALU.add), d1)
                d = dve(lambda e: e.tensor_copy(posi[:, 0, :], pos[:, :]), d)
                d1 = dve(lambda e: e.tensor_single_scalar(posi[:, 1, :], posi[:, 0, :], 7, ALU.logical_shift_right), d)
                d2 = dve(lambda e: e.tensor_single_scalar(posi[:, 0, :], posi[:, 0, :], 127, ALU.bitwise_and), d1)
                d2 = dve(lambda e: e.tensor_copy(pos[:, :], posi[:, 0, :]), d2)
                d2 = dve(lambda e: e.scalar_tensor_tensor(pos[:, :], pos[:, :], float(ET), posi[:, 1, :], ALU.mult,
                                                          ALU.add), d2)
                d2 = dve(lambda e: e.tensor_copy(posi[:, 0, :], pos[:, :]), d2)
                t = dve(lambda e: e.tensor_scalar(tl[:, :], const("tile_start"), small[:, 4, 0:1], None, ALU.is_ge), c)
                for i in range(1, NT):
                    t = dve(lambda e: e.scalar_tensor_tensor(tl[:, :], const("tile_start"), small[:, 4, i:i + 1],
                                                             tl[:, :], ALU.is_ge, ALU.add), t)
                t = dve(lambda e: e.tensor_scalar(tl[:, :], tl[:, :], NT - 1.0, float(D), ALU.min, ALU.mult), t)
                dve(lambda e: e.tensor_copy(bucket_of_tile[:, :], tl[:, :]), t)
                pool.wait(blank, d2, filled)
                for c in range(EC):
                    f.dma(pool, "scatter", lambda e: e.indirect_dma_start(
                        out=table, out_offset=bass.IndirectOffsetOnAxis(ap=posi[:, 0, c:c + 1], axis=0),
                        in_=rec[:, c, :], in_offset=None))
                f.stage(name + "_end")

        def fill_bias(sb, rec, src, tmp, got):
            ea = sb("ea", [P, EC, 16])
            dst = sb("dst", [P, EC], I32)
            eaT = sb("eaT", [P, 2, P])
            we = sb("we", [P, 8, H])
            be = sb("be", [P, H])
            l1 = f.dma(sp, "ea", lambda e: e.dma_start(ea[:, :, :], I["edge_attr_16"].rearrange("(p c) w -> p c w", p=P)))
            l2 = f.dma(sp, "dst", lambda e: e.dma_start(dst[:, :], I["dst"].rearrange("(p c) -> p c", p=P)))
            z = dve(lambda e: e.memset(we[:, :, :], 0.0))
            lw = [f.dma(act, "we", lambda e: e.dma_start(we[16 * j:16 * j + 16, j, :], I["L0_gnn_We"]), z) for j in range(8)]
            lb = f.dma(act, "be", lambda e: e.dma_start(be[:, :], vec_row(I["L0_gnn_be"], P, H)))
            done = []
            freeT, freeS = {}, {}
            for j in range(EC // 8):
                s = j % 2
                t = pe(lambda e: e.transpose(bank[s][:, 0:P], ea[:, 8 * j:8 * j + 8, :].rearrange("p a b -> p (a b)"),
                                             ident), l1, freeT.get(s))
                freeT[s] = t = act(lambda e: e.activation(eaT[:, s, :], bank[s][:, 0:P], ACT.Copy), t)
                t = pe(lambda e: e.matmul(bank[2 + s][:, 0:64], eaT[:, s, :], we[:, :, :].rearrange("p a b -> p (a b)"),
                                          start=True, stop=True), t, lw, freeS.get(s))
                freeS[s] = dve(lambda e: e.tensor_tensor(
                    rec[:, 8 * j:8 * j + 8, 0:H], bank[2 + s][:, 0:64].rearrange("p (a b) -> p a b", b=H),
                    rep(be[:, :], 8), ALU.add), t, lb)
            done.append(freeS[0])
            done.append(freeS[1])
            t = dve(lambda e: e.tensor_single_scalar(tmp[:, :], src[:, :], P - 1, ALU.bitwise_and), got)
            t = dve(lambda e: e.tensor_copy(rec[:, :, H], tmp[:, :]), t)
            t = dve(lambda e: e.tensor_single_scalar(tmp[:, :], dst[:, :], G - 1, ALU.bitwise_and), l2, t)
            done.append(dve(lambda e: e.tensor_copy(rec[:, :, H + 1], tmp[:, :]), t))
            return done

        def fill_conv(sb, rec, dst, tmp, got):
            src = sb("src", [P, EC], I32)
            done = [f.dma(act, "ea", lambda e: e.dma_start(rec[:, :, 0:64], I["edge_attr_64"].rearrange(
                "(p c) w -> p c w", p=P)))]
            l2 = f.dma(act, "src", lambda e: e.dma_start(src[:, :], I["src"].rearrange("(p c) -> p c", p=P)))
            done.append(dve(lambda e: e.memset(rec[:, :, 64:65], 1.0)))
            t = dve(lambda e: e.tensor_single_scalar(tmp[:, :], dst[:, :], P - 1, ALU.bitwise_and), got)
            t = dve(lambda e: e.tensor_copy(rec[:, :, 65], tmp[:, :]), t)
            done.append(t)
            done.append(dve(lambda e: e.tensor_copy(rec[:, :, 66:67].bitcast(I32).rearrange("p c w -> p (c w)"),
                                                    src[:, :]), l2))
            return done

        sort_edges("sort0", I["src"], H, R0, sorted_bias, bucket0, fill_bias)
        sort_edges("sort1", I["dst"], 65, R1, sorted_edge, bucket1, fill_conv)

        def layernorm(xnT, xn, store=None):
            with ExitStack() as s:
                sb = tensors(s)
                st = sb("st", [P, NT, 6])
                mv = sb("mv", [P, NT, 2])
                rs = sb("rs", [P, NT])
                for t in range(NT):
                    a = dve(lambda e: e.bn_stats(st[:, t, :], X[:, t, :]))
                    a = dve(lambda e: e.bn_aggr(mv[:, t, :], st[:, t, :]), a)
                a = rsqrt(rs[:, :], mv[:, :, 1], EPS_LN, 1.0, a)
                freed, copied = {}, {}
                for t in range(NT):
                    b = t % 2
                    n = dve(lambda e: e.tensor_scalar(xn[:, b, :], X[:, t, :], mv[:, t, 0:1], rs[:, t:t + 1],
                                                      ALU.subtract, ALU.mult), a, freed.get(b))
                    freed[b] = []
                    if store is not None:
                        freed[b].append(f.dma(sp, f"rows{b}", lambda e: e.dma_start(store[t * P:(t + 1) * P, :],
                                                                                    xn[:, b, :]), n))
                    for c in range(KC):
                        m = pe(lambda e: e.transpose(bank[b][:, c * P:(c + 1) * P], xn[:, b, c * P:(c + 1) * P], ident),
                               n, copied.get(b))
                    freed[b].append(m)
                    copied[b] = act(lambda e: e.activation(xnT[:, :, t * P:(t + 1) * P],
                                                           bank[b][:, :].rearrange("p (c n) -> p c n", c=KC), ACT.Copy), m)
                f.stage(f.name + "n")

        def project_back(o, oT, w, acc_bank, t_bank, t, *after):
            for c in range(KC):
                a = pe(lambda e: e.transpose(t_bank[:, c * P:(c + 1) * P], o[:, c * P:(c + 1) * P], ident), *after)
            yield
            a = act(lambda e: e.activation(oT, t_bank[:, :], ACT.Copy), a)
            yield
            for c in range(KC):
                b = pe(lambda e: e.matmul(acc_bank[:, :], oT[:, c * P:(c + 1) * P], w[:, c, :], start=c == 0,
                                          stop=c == KC - 1), a)
            yield
            yield dve(lambda e: e.tensor_tensor(X[:, t, :], X[:, t, :], acc_bank[:, :], ALU.add), b)

        f.stage("ln0")
        layer0 = ExitStack()
        xnT = layer0.enter_context(nc.sbuf_tensor("xnT0", [P, KC, N], F32))
        biased = ExitStack()
        bias = biased.enter_context(nc.sbuf_tensor("bias", [P, NT, D], F32))
        with ExitStack() as s:
            xn = s.enter_context(nc.sbuf_tensor("xn0", [P, 2, D], F32))
            layernorm(xnT, xn)

        def sum_edges(name, width, table, bucket_of_tile, acc, local, rhs, width_pipe):
            per = 16
            with ExitStack() as s:
                sb = tensors(s)
                rec = sb("rec", [P, 2, per, width])
                hot = sb("hot", [P, 4, P])
                make = rhs(sb)
                flat = acc[:, :, :].rearrange("p t d -> p (t d)")
                table_p = table.rearrange("(p n) w -> p n w", p=P)
                loaded, ended = {}, {}
                acc_done = [None]

                def load(g):
                    b = g % 2
                    loaded[g] = f.dma(sp, f"rec{b}", lambda e: e.dma_start(
                        rec[:, b, :, :], table_p[:, g * per:(g + 1) * per, :]),
                        [ended[i] for i in range((g - 2) * per, (g - 1) * per)] if g >= 2 else None)

                def tile(i):
                    g, k, q = i // per, i % per, i % 4
                    if k == 0:
                        load(g)
                    r = rec[:, g % 2, k, :]
                    before = ended.get(i - 4)
                    h = dve(lambda e: e.tensor_scalar(hot[:, q, :], const("iota"), r[:, local:local + 1], None,
                                                      ALU.is_equal), loaded[g], before)
                    yield
                    m = None
                    for m in make(i, q, r, loaded[g], before):
                        if m is None:
                            yield
                    yield
                    a = pe(lambda e: e.matmul(bank[q][:, :], hot[:, q, :], m[0], start=True, stop=True), h, m[1], before)
                    yield
                    at = dve.engine.value_load(bucket_of_tile[0:1, i:i + 1], min_val=0, max_val=(NT - 1) * D)
                    acc_done[0] = dve(lambda e: e.tensor_tensor(flat[:, bass.ds(at, D)], flat[:, bass.ds(at, D)],
                                                                bank[q][:, :], ALU.add), a, acc_done[0])
                    ended[i] = [acc_done[0], m[1]]

                interleave((tile(i) for i in range(ET)), width_pipe)
                f.stage(f.name + "s")

        def bias_rhs(sb):
            col = sb("col", [P, 4, G])
            prod = sb("prod", [P, 4, H, G])

            def make(i, q, r, loaded, before):
                c = dve(lambda e: e.tensor_scalar(col[:, q, :], const("iota")[:, 0:G], r[:, H + 1:H + 2], None,
                                                  ALU.is_equal), loaded, before)
                yield None
                yield (prod[:, q, :, :].rearrange("p h j -> p (h j)"),
                       pool(lambda e: e.tensor_tensor(prod[:, q, :, :], rep(col[:, q, :], H), mid(r[:, 0:H], G),
                                                      ALU.mult), c, before))
            return make

        f.stage("bias")
        pool(lambda e: e.memset(bias[:, :, :], 0.0))
        f.stage("biasz")
        if stop >= 1:
            sum_edges("bias", R0, sorted_bias, bucket0, bias, H, bias_rhs, 4)

        f.stage("att")
        with ExitStack() as s:
            sb = tensors(s)
            wq, wk, wv, wo = (sb(n, [P, KC, D]) for n in ("wq", "wk", "wv", "wo"))
            loads = [f.dma(sp, "w", lambda e: e.dma_start(w[:, :, :], rows(I[f"L0_gnn_W{n}"])))
                     for w, n in ((wq, "q"), (wk, "k"), (wv, "v"), (wo, "o"))]
            bq, bk = sb("bq", [P, KC]), sb("bk", [P, KC])
            bkp = sb("bkp", [P, 2, KC])
            bv = sb("bv", [G, D])
            bo = sb("bo", [P, 2, D])
            with nc.allow_non_contiguous_dma(reason="small bias columns"):
                loads.append(f.dma(act, "b", lambda e: e.dma_start(bq[:, :], I["L0_gnn_bq"].rearrange("(c p) -> p c", p=P))))
                loads.append(f.dma(act, "b", lambda e: e.dma_start(bk[:, :], I["L0_gnn_bk"].rearrange("(c p) -> p c", p=P))))
            loads.append(f.dma(act, "b", lambda e: e.dma_start(bv[:, :], vec_row(I["L0_gnn_bv"], G, D))))
            loads.append(f.dma(act, "b", lambda e: e.dma_start(bo[:, 0, :], vec_row(I["L0_gnn_bo"], P, D))))
            loads.append(f.dma(act, "b", lambda e: e.dma_start(bo[:, 1, :], vec_row(I["L0_mix_bo"], P, D))))
            par = const("parity")
            for j in range(2):
                bkd = dve(lambda e: e.tensor_scalar(bkp[:, j, :], bk[:, :], par[:, j:j + 1], None, ALU.mult), loads)
            bod = dve(lambda e: e.tensor_tensor(bo[:, 0, :], bo[:, 0, :], bo[:, 1, :], ALU.add), loads)
            qT = sb("qT", [P, 2, KC, P])
            kT = sb("kT", [P, 2, 2, KC, P])
            v = sb("v", [G, 2, 2, D])
            sc = sb("sc", [P, 2, D])
            pT = sb("pT", [G, 2, H, P])
            o = sb("o", [P, 2, D])
            oT = sb("oT", [P, 2, D])
            mx = sb("mx", [P, 2, 3, H])
            ended = {}

            def att_tile(t):
                q = t % 2
                B = bank[4 * q:4 * q + 4]
                was = ended.get(t - 2)
                nodes = slice(t * P, (t + 1) * P)
                bx = pool(lambda e: e.tensor_tensor(X[:, t, :], X[:, t, :], bo[:, 0, :], ALU.add), bod)
                for w, b in ((wq, B[0]), (wk, B[1])):
                    for m in range(KC):
                        for c in range(KC):
                            a = pe(lambda e: e.matmul(b[:, m * P:(m + 1) * P], w[:, c, m * P:(m + 1) * P],
                                                      xnT[:, c, nodes], start=c == 0, stop=c == KC - 1), loads, was)
                    yield
                for g in range(2):
                    for c in range(KC):
                        av = pe(lambda e: e.matmul(B[2 + g][0:G, :], xnT[:, c, t * P + g * G:t * P + (g + 1) * G],
                                                   wv[:, c, :], start=c == 0, stop=c == KC - 1))
                B0 = B[0][:, :].rearrange("p (c n) -> p c n", c=KC)
                B1 = B[1][:, :].rearrange("p (c n) -> p c n", c=KC)
                qd = dve(lambda e: e.tensor_tensor(qT[:, q, :, :], B0, mid(bq[:, :], P), ALU.add), a, was)
                for j in range(2):
                    kd = dve(lambda e: e.scalar_tensor_tensor(kT[:, q, j, :, :], B1, par[:, j:j + 1],
                                                              mid(bkp[:, j, :], P), ALU.mult, ALU.add), bkd)
                for g in range(2):
                    vd = dve(lambda e: e.tensor_tensor(v[:, q, g, :], B[2 + g][0:G, :], bv[:, :], ALU.add), av)
                yield
                for h in range(H):
                    for g in range(2):
                        cols = slice(g * G, (g + 1) * G)
                        a = pe(lambda e: e.matmul(B[0][cols, h * G:(h + 1) * G], qT[:, q, h // 2, cols],
                                                  kT[:, q, h % 2, h // 2, cols], start=True, stop=True), kd)
                yield
                s3 = sc[:, q, :].rearrange("p (h j) -> p h j", h=H)
                a = dve(lambda e: e.scalar_tensor_tensor(sc[:, q, :], B[0][:, :], HD ** -0.5, bias[:, t, :],
                                                         ALU.mult, ALU.add), a)
                a = dve(lambda e: e.tensor_reduce(mx[:, q, 0, :], s3, AX.X, ALU.max), a)
                yield
                a = dve(lambda e: e.tensor_tensor(s3, s3, mid(mx[:, q, 0, :], G), ALU.subtract), a)
                x = act(lambda e: e.activation(sc[:, q, :], sc[:, q, :], ACT.Exp), a)
                yield
                for h in range(H):
                    a = pe(lambda e: e.transpose(B[1 + h // 4][0:G, (h % 4) * P:(h % 4 + 1) * P],
                                                 s3[:, h, :], ident), x, vd)
                b = dve(lambda e: e.tensor_reduce(mx[:, q, 1, :], s3, AX.X, ALU.add), x)
                b = dve(lambda e: e.reciprocal(mx[:, q, 2, :], mx[:, q, 1, :]), b)
                yield
                for j in range(2):
                    a = act(lambda e: e.activation(pT[:, q, 4 * j:4 * j + 4, :].rearrange("p h n -> p (h n)"),
                                                   B[1 + j][0:G, :], ACT.Copy), a)
                yield
                for h in range(H):
                    for g in range(2):
                        cols = slice(g * G, (g + 1) * G)
                        m = pe(lambda e: e.matmul(B[3][cols, h * HD:(h + 1) * HD], pT[:, q, h, cols],
                                                  v[:, q, g, h * HD:(h + 1) * HD], start=True, stop=True), a, vd)
                yield
                a = dve(lambda e: e.tensor_tensor(o[:, q, :].rearrange("p (h j) -> p h j", h=H),
                                                  B[3][:, :].rearrange("p (h j) -> p h j", h=H),
                                                  mid(mx[:, q, 2, :], HD), ALU.mult), m, b)
                yield
                for r in project_back(o[:, q, :], oT[:, q, :], wo, B[1], B[0], t, a, bx):
                    yield
                ended[t] = r

            if stop >= 1:
                interleave((att_tile(t) for t in range(NT)), 2)
            f.stage("att_end")
        biased.close()

        def write_out():
            f.dma(sp, "out", lambda e: e.dma_start(out.rearrange("(t p) d -> p t d", p=P), X[:, :, :]))
            f.stage("end")

        if stop <= 1:
            layer0.close()
            write_out()
            return
        f.stage("perf")
        with ExitStack() as s:
            sb = tensors(s)
            tT = sb("tT", [P, KC, N])
            va = sb("va", [P, NT, H, HD + 1])
            w = sb("w", [P, KC, D])
            wv = sb("wv", [P, KC, D])
            prj = sb("prj", [P, 2, M])
            diag = sb("diag", [P, NT, H])
            mk = sb("mk", [P, NT, H])
            sq = sb("sq", [P, 2, D])
            ctx_t = sb("ctx_t", [HD + 1, M])
            cx = sb("cx", [P, H, 3, HD + 1])
            ex = sb("ex", [P, 4, M])
            qf = sb("qf", [P, 4, 3, P])
            o = sb("o", [P, 2, D])
            oT = sb("oT", [P, 2, D])
            t1 = sb("t1", [P, 4, 4])
            rc = sb("rc", [P, 2, 4])
            row = sb("row", [P, 4])
            dn = HD ** -0.25

            z = dve(lambda e: e.memset(prj[:, :, :], 0.0))
            with nc.allow_non_contiguous_dma(reason="projection laid out transposed"):
                lp = [f.dma(act, "prj", lambda e: e.dma_start(prj[j * HD:(j + 1) * HD, j, :], I["L0_mix_projT"]), z)
                      for j in range(2)]
            prj2 = prj[:, :, :].rearrange("p a b -> p (a b)")
            pd = dve(lambda e: e.tensor_scalar(prj2, prj2, dn, None, ALU.mult), lp)
            lk = f.dma(sp, "w", lambda e: e.dma_start(w[:, :, :], rows(I["L0_mix_Wk"])))
            lv = f.dma(sp, "wv", lambda e: e.dma_start(wv[:, :, :], rows(I["L0_mix_Wv"])))
            vo = dve(lambda e: e.memset(va[:, :, :, HD:HD + 1], 1.0))

            def to_features(loaded):
                freed, sqfree, copied = {}, {}, []
                for m in range(KC):
                    for nb in range(4):
                        b = bank[(m * 4 + nb) % 4]
                        cols = slice(nb * 512, (nb + 1) * 512)
                        for c in range(KC):
                            a = pe(lambda e: e.matmul(b[:, :], w[:, c, m * P:(m + 1) * P], xnT[:, c, cols],
                                                      start=c == 0, stop=c == KC - 1), loaded, freed.get((m * 4 + nb) % 4))
                        freed[(m * 4 + nb) % 4] = a = act(lambda e: e.activation(tT[:, m, cols], b[:, :], ACT.Copy), a)
                last = a
                head_of_row = const("head_of_row").rearrange("p (c h) -> p c h", c=KC)
                dg = bank[4]
                for t in range(NT):
                    q = t % 2
                    a = pool(lambda e: e.tensor_tensor(sq[:, q, :].rearrange("p (c n) -> p c n", c=KC),
                                                       tT[:, :, t * P:(t + 1) * P], tT[:, :, t * P:(t + 1) * P],
                                                       ALU.mult), last, sqfree.get(q))
                    for c in range(KC):
                        b = pe(lambda e: e.matmul(dg[:, t * H:(t + 1) * H], sq[:, q, c * P:(c + 1) * P],
                                                  head_of_row[:, c, :], start=c == 0, stop=c == KC - 1), a)
                    sqfree[q] = b
                return [last, dve(lambda e: e.tensor_scalar(diag[:, :, :].rearrange("p t h -> p (t h)"),
                                                            dg[:, 0:NT * H], -0.5 * dn * dn, None, ALU.mult), b)]

            def scores(b, t, h, *after):
                return pe(lambda e: e.matmul(b[:, 0:M], tT[:, h // 2, t * P:(t + 1) * P], prj[:, h % 2, :],
                                             start=True, stop=True), *after)

            ready = to_features(lk)
            freed = {}
            for t in range(NT):
                b = bank[5 + t % 2]
                for c in range(KC):
                    a = pe(lambda e: e.matmul(b[:, :], xnT[:, c, t * P:(t + 1) * P], wv[:, c, :], start=c == 0,
                                              stop=c == KC - 1), lv, freed.get(t % 2))
                freed[t % 2] = vd = act(lambda e: e.activation(va[:, t, :, 0:HD], b[:, :].rearrange(
                    "p (h d) -> p h d", h=H), ACT.Copy), a)
            freed = {}
            for n in range(NT * H):
                t, h = n // H, n % H
                a = scores(bank[n % 4], t, h, ready, pd, freed.get(n % 4))
                freed[n % 4] = mkd = dve(lambda e: e.tensor_reduce(mk[:, t, h:h + 1], bank[n % 4][:, 0:M], AX.X,
                                                                   ALU.max), a)
            a = dve(lambda e: e.tensor_reduce(row[:, 0:1], mk[:, :, :].rearrange("p t h -> p (t h)"), AX.X, ALU.max), mkd)
            a = pe(lambda e: e.transpose(bank[7][0:1, 0:P], row[:, 0:1], ident), a)
            a = dve(lambda e: e.tensor_reduce(row[0:1, 1:2], bank[7][0:1, 0:P], AX.X, ALU.max), a)
            a = pe(lambda e: e.matmul(bank[7][:, P:P + 1], ones[0:1, :], row[0:1, 1:2], start=True, stop=True), a)
            a = dve(lambda e: e.tensor_copy(row[:, 2:3], bank[7][:, P:P + 1]), a)
            shift = dve(lambda e: e.tensor_scalar(mk[:, :, :], diag[:, :, :], row[:, 2:3], None, ALU.subtract), a)
            freed, used, cfree = {}, {}, None
            for h in range(H):
                held = bank[6 + h % 2]
                pend = []
                for t in range(NT):
                    n = h * NT + t
                    q = n % 4
                    a = scores(bank[q], t, h, freed.get(q), shift)
                    freed[q] = a = act(lambda e: e.activation(ex[:, q, :], bank[q][:, 0:M], ACT.Exp,
                                                              bias=mk[:, t, h:h + 1]), a, used.get(q))
                    a = pool(lambda e: e.tensor_scalar(ex[:, q, :], ex[:, q, :], 1e-4, None, ALU.add), a)
                    pend.append((t, q, a))
                    if len(pend) > 2 or t == NT - 1:
                        for t_, q_, a_ in (pend if t == NT - 1 else pend[:1]):
                            used[q_] = b = pe(lambda e: e.matmul(held[0:HD + 1, 0:M], va[:, t_, h, :], ex[:, q_, :],
                                                                 start=t_ == 0, stop=t_ == NT - 1), a_, vd, vo)
                        pend = pend[1:]
                c = dve(lambda e: e.tensor_copy(ctx_t[:, :], held[0:HD + 1, 0:M]), b, cfree)
                for j, (m0, mn) in enumerate(MC):
                    cfree = pe(lambda e: e.transpose(bank[4][0:mn, j * 128:j * 128 + HD + 1], ctx_t[:, m0:m0 + mn],
                                                     ident[0:HD + 1, 0:HD + 1]), c)
                for j, (m0, mn) in enumerate(MC):
                    c = dve(lambda e: e.tensor_copy(cx[0:mn, h, j, :], bank[4][0:mn, j * 128:j * 128 + HD + 1]), cfree)
                cfree = c
            f.stage("perfq")
            lq = f.dma(sp, "w", lambda e: e.dma_start(w[:, :, :], rows(I["L0_mix_Wq"])))
            lo = f.dma(sp, "wv", lambda e: e.dma_start(wv[:, :, :], rows(I["L0_mix_Wo"])))
            ready = to_features(lq)
            f.stage("perfo")
            ended = {}

            def perf_tile(t):
                q = t % 2
                was = ended.get(t - 2)
                B = bank[4 * q:4 * q + 4]
                scored, cleared = {}, {}
                norm = None
                for h in range(H):
                    r = h % 2
                    a = scores(B[r], t, h, was, scored.get(r))
                    k = 2 * q + r
                    b = dve(lambda e: e.tensor_reduce(t1[:, k, 0:1], B[r][:, 0:M], AX.X, ALU.max), a, cleared.get(r))
                    b = dve(lambda e: e.tensor_tensor(t1[:, k, 1:2], diag[:, t, h:h + 1], t1[:, k, 0:1], ALU.subtract), b)
                    yield
                    a = act(lambda e: e.activation(ex[:, k, :], B[r][:, 0:M], ACT.Exp, bias=t1[:, k, 1:2]), b,
                            cleared.get(r))
                    yield
                    for j, (m0, mn) in enumerate(MC):
                        a = pe(lambda e: e.transpose(B[r][0:mn, j * P:(j + 1) * P], ex[:, k, m0:m0 + mn], ident), a)
                    cleared[r] = a
                    yield
                    b1 = dve(lambda e: e.tensor_scalar(qf[:, k, 0:2, :].rearrange("p a b -> p (a b)"), B[r][:, 0:256],
                                                       1e-4, None, ALU.add), a)
                    scored[r] = b = dve(lambda e: e.tensor_scalar(qf[0:MC[2][1], k, 2, :], B[r][0:MC[2][1], 256:384], 1e-4,
                                                                  None, ALU.add), a)
                    yield
                    nb = B[2]
                    at = (h % 4) * (HD + 1)
                    for j, (m0, mn) in enumerate(MC):
                        c = pe(lambda e: e.matmul(nb[:, at:at + HD + 1], qf[0:mn, k, j, :], cx[0:mn, h, j, :],
                                                  start=j == 0, stop=j == 2), b, norm)
                    if h % 4 == 3:
                        n4 = nb[:, 0:4 * (HD + 1)].rearrange("p (h d) -> p h d", h=4)
                        yield
                        d = dve(lambda e: e.reciprocal(rc[:, q, :], n4[:, :, HD]), c, norm)
                        norm = dve(lambda e: e.tensor_tensor(
                            o[:, q, (h - 3) * HD:(h + 1) * HD].rearrange("p (h d) -> p h d", h=4), n4[:, :, 0:HD],
                            mid(rc[:, q, :], HD), ALU.mult), d)
                yield
                for r in project_back(o[:, q, :], oT[:, q, :], wv, B[3], B[0], t, norm, lo):
                    yield
                ended[t] = r

            interleave((perf_tile(t) for t in range(NT)), 2)
            f.stage("perf_end")
        layer0.close()
        if stop <= 2:
            write_out()
            return
        f.stage("ln1")
        layer = ExitStack()
        xnT = layer.enter_context(nc.sbuf_tensor("xnT1", [P, KC, N], F32))
        slot_of = layer.enter_context(nc.sbuf_tensor("slot_of", [P, 2, NT], I32))
        slot_w = layer.enter_context(nc.sbuf_tensor("slot_w", [P, 2, NT], F32))
        with ExitStack() as s:
            xn = s.enter_context(nc.sbuf_tensor("xn1", [P, 2, D], F32))
            layernorm(xnT, xn)

        def slots_of(sel, pos, base, tot, groups, *after):
            n = groups * NT
            pe(lambda e: e.matmul(bank[0][:, 0:n], const("before"), sel, start=True, stop=True), *after)
            a = pe(lambda e: e.matmul(bank[1][:, 0:n], ones, sel, start=True, stop=True))
            b = dve(lambda e: e.tensor_copy(tot, bank[1][:, 0:n]), a)
            c = dve(lambda e: e.tensor_tensor_scan(base, tot, tot, 0.0, ALU.add, ALU.max), b)
            c = dve(lambda e: e.tensor_tensor(base, base, tot, ALU.subtract), c)
            return dve(lambda e: e.tensor_tensor(pos, base, bank[0][:, 0:n], ALU.add), c)

        f.stage("route")
        with ExitStack() as s:
            sb = tensors(s)
            ws = sb("ws", [P, KC, 20])
            lw = [f.dma(sp, "w", lambda e: e.dma_start(ws[:, :, a:b], rows(I[f"L0_ffn_W{n}"])))
                  for n, a, b in (("gate", 0, 4), ("b", 4, 12), ("a", 12, 20))]
            dtb, alog = sb("dtb", [P, H]), sb("alog", [P, H])
            lb = [f.dma(act, "b", lambda e: e.dma_start(dtb[:, :], vec_row(I["L0_ffn_dt_bias"], P, H))),
                  f.dma(act, "b", lambda e: e.dma_start(alog[:, :], vec_row(I["L0_ffn_A_log"], P, H)))]
            sm = sb("sm", [P, NT, 20])
            for t in range(NT):
                for c in range(KC):
                    a = pe(lambda e: e.matmul(bank[2][:, t * 20:(t + 1) * 20], xnT[:, c, t * P:(t + 1) * P],
                                              ws[:, c, :], start=c == 0, stop=c == KC - 1), lw)
            sm2 = sm[:, :, :].rearrange("p t n -> p (t n)")
            a = dve(lambda e: e.tensor_copy(sm2, bank[2][:, 0:NT * 20]), a)
            big = {n: sb(n, [P, EX, NT]) for n in ("lg", "pr", "sel", "w", "prev", "pos", "base", "tot", "first", "tmp",
                                                   "reset")}
            V = {n: t[:, :, :] for n, t in big.items()}
            flat = {n: v.rearrange("p e t -> p (e t)") for n, v in V.items()}
            cmp = sb("cmp", [P, EX, EX, NT])
            equal = sb("equal", [P, EX, EX, NT])
            mx = sb("mx", [P, NT])
            a = dve(lambda e: e.tensor_copy(V["lg"], sm[:, :, 0:EX].rearrange("p t e -> p e t")), a)
            b = dve(lambda e: e.tensor_reduce(mx[:, :], V["lg"].rearrange("p e t -> p t e"), AX.X, ALU.max), a)
            lg = dve(lambda e: e.tensor_tensor(V["lg"], V["lg"], rep(mx[:, :], EX), ALU.subtract), b)
            pr = act(lambda e: e.activation(flat["pr"], flat["lg"], ACT.Exp), lg)
            other = V["lg"].unsqueeze(1).broadcast_to([P, EX, EX, NT])
            own = V["lg"].unsqueeze(2).broadcast_to([P, EX, EX, NT])
            a = dve(lambda e: e.tensor_tensor(cmp[:, :, :, :], other, own, ALU.is_gt), lg)
            b = dve(lambda e: e.tensor_tensor(equal[:, :, :, :], other, own, ALU.is_equal), lg)
            eq3 = equal[:, :, :, :].rearrange("p e i t -> p (e i) t")
            b = dve(lambda e: e.tensor_tensor(eq3, eq3, mid(const("earlier"), NT), ALU.mult), b)
            a = dve(lambda e: e.tensor_tensor(cmp[:, :, :, :], cmp[:, :, :, :], equal[:, :, :, :], ALU.add), a, b)
            for x in range(EX):
                a1 = dve(lambda e: e.tensor_reduce(V["sel"][:, x, :], cmp[:, x, :, :].rearrange("p i t -> p t i"), AX.X,
                                                   ALU.add), a)
            sel = dve(lambda e: e.tensor_scalar(flat["sel"], flat["sel"], 1.5, None, ALU.is_lt), a1)
            a = dve(lambda e: e.tensor_tensor(V["w"], V["pr"], V["sel"], ALU.mult), sel, pr)
            b = dve(lambda e: e.tensor_reduce(mx[:, :], V["w"].rearrange("p e t -> p t e"), AX.X, ALU.add), a)
            b = dve(lambda e: e.reciprocal(mx[:, :], mx[:, :]), b)
            w_ = dve(lambda e: e.tensor_tensor(V["w"], V["w"], rep(mx[:, :], EX), ALU.mult), b)
            a = dve(lambda e: e.memset(V["prev"][:, 0, :], 0.0))
            for x in range(1, EX):
                a = dve(lambda e: e.tensor_tensor(V["prev"][:, x, :], V["prev"][:, x - 1, :], V["sel"][:, x - 1, :],
                                                  ALU.add), a, sel)
            prev = a
            pos = slots_of(flat["sel"], flat["pos"], flat["base"], flat["tot"], EX, sel)
            rs = dve(lambda e: e.tensor_tensor(V["reset"], V["pos"], mid(V["base"][:, :, 0], NT), ALU.is_equal), pos)
            picked = sb("picked", [P, 2, 3, NT])
            a = None
            for j in range(2):
                if j == 0:
                    c = dve(lambda e: e.tensor_tensor(V["first"], V["sel"], V["prev"], ALU.mult), prev)
                    c = dve(lambda e: e.tensor_tensor(V["first"], V["sel"], V["first"], ALU.subtract), c)
                else:
                    c = dve(lambda e: e.tensor_tensor(V["first"], V["sel"], V["prev"], ALU.mult), a)
                a = c
                for k, n in enumerate(("pos", "w", "reset")):
                    a = dve(lambda e: e.tensor_tensor(V["tmp"], V["first"], V[n], ALU.mult), c, a, pos, w_, rs)
                    a = dve(lambda e: e.tensor_reduce(picked[:, j, k, :], V["tmp"].rearrange("p e t -> p t e"), AX.X,
                                                      ALU.add), a)
            for j in range(2):
                dve(lambda e: e.tensor_copy(slot_of[:, j, :], picked[:, j, 0, :]), a)
                pk = dve(lambda e: e.tensor_copy(slot_w[:, j, :], picked[:, j, 1, :]), a)
            gt = sb("gt", [P, 6, NT, H])
            ga = sb("ga", [P, 2, NT, 2 * H])
            al = sb("al", [P, 2, NT])
            a = act(lambda e: e.activation(gt[:, 0, :, :], sm[:, :, 4:12], ACT.Exp, scale=-1.0), pk)
            a = dve(lambda e: e.tensor_scalar(gt[:, 0, :, :], gt[:, 0, :, :], 1.0, None, ALU.add), a)
            beta = dve(lambda e: e.reciprocal(gt[:, 0, :, :], gt[:, 0, :, :]), a)
            a = act(lambda e: e.activation(alog[:, :], alog[:, :], ACT.Exp), lb)
            na = dve(lambda e: e.tensor_scalar(alog[:, :], alog[:, :], -1.0, None, ALU.mult), a)
            z = dve(lambda e: e.tensor_tensor(gt[:, 1, :, :], sm[:, :, 12:20], rep(dtb[:, :], NT), ALU.add), lb)
            a = dve(lambda e: e.scalar_tensor_tensor(gt[:, 2, :, :], gt[:, 1, :, :], -1.0, gt[:, 1, :, :], ALU.mult,
                                                     ALU.max), z)
            a = act(lambda e: e.activation(gt[:, 3, :, :], gt[:, 2, :, :], ACT.Exp, scale=-1.0), a)
            a = dve(lambda e: e.tensor_scalar(gt[:, 3, :, :], gt[:, 3, :, :], 1.0, None, ALU.add), a)
            a = act(lambda e: e.activation(gt[:, 3, :, :], gt[:, 3, :, :], ACT.Ln), a)
            a = dve(lambda e: e.scalar_tensor_tensor(gt[:, 4, :, :], gt[:, 1, :, :], 0.0, gt[:, 3, :, :], ALU.max,
                                                     ALU.add), a)
            g = dve(lambda e: e.tensor_tensor(gt[:, 4, :, :], gt[:, 4, :, :], rep(alog[:, :], NT), ALU.mult), a, na)
            for j in range(2):
                a = dve(lambda e: e.tensor_scalar(al[:, j, :], picked[:, j, 1, :], 0.0, None, ALU.is_gt), pk)
                dve(lambda e: e.tensor_tensor(ga[:, j, :, 0:H], gt[:, 0, :, :], mid(al[:, j, :], H), ALU.mult), a, beta)
                b = dve(lambda e: e.tensor_tensor(gt[:, 5, :, :], gt[:, 4, :, :], mid(al[:, j, :], H), ALU.mult), a, g)
                g = dve(lambda e: e.scalar_tensor_tensor(ga[:, j, :, H:2 * H], mid(picked[:, j, 2, :], H), RESET,
                                                         gt[:, 5, :, :], ALU.mult, ALU.add), b)
            f.stage("qkv")
            wts = [sb(f"w{n}", [P, KC, D]) for n in "qkvg"]
            lw = [f.dma(sp, "w", lambda e: e.dma_start(wts[i][:, :, :], rows(I[f"L0_ffn_W{n}"])))
                  for i, n in enumerate("qkvg")]
            rw = sb("rw", [P, 2, 3 * D])
            gr = sb("gr", [P, 2, D])
            sq = sb("sq", [P, 2, 2 * D])
            ss = sb("ss", [P, 2, 2 * H])
            ended = {}

            def qkv_tile(t):
                q = t % 2
                B = bank[4 * q:4 * q + 4]
                was = ended.get(t - 2)
                for i in range(4):
                    for c in range(KC):
                        a = pe(lambda e: e.matmul(B[i][:, :], xnT[:, c, t * P:(t + 1) * P], wts[i][:, c, :], start=c == 0,
                                                  stop=c == KC - 1), lw, was)
                    if i < 3:
                        b = act(lambda e: e.activation(rw[:, q, i * D:(i + 1) * D], B[i][:, :], ACT.Silu), a, was)
                    else:
                        g = act(lambda e: e.activation(gr[:, q, :], B[i][:, :], ACT.Silu), a, was)
                    yield
                sg = f.dma(sp, f"gate{q}", lambda e: e.dma_start(gate_rows[t * P:(t + 1) * P, :], gr[:, q, :]), g)
                a = pool(lambda e: e.tensor_tensor(sq[:, q, :], rw[:, q, 0:2 * D], rw[:, q, 0:2 * D], ALU.mult), b)
                yield
                a = dve(lambda e: e.tensor_reduce(ss[:, q, :], sq[:, q, :].rearrange("p (h d) -> p h d", d=HD), AX.X,
                                                  ALU.add), a)
                a = rsqrt(ss[:, q, :], ss[:, q, :], 1e-6, 1.0, a)
                yield
                a = dve(lambda e: e.tensor_scalar(ss[:, q, 0:H], ss[:, q, 0:H], HD ** -0.5, None, ALU.mult), a)
                qk = rw[:, q, 0:2 * D].rearrange("p (h d) -> p h d", d=HD)
                a = dve(lambda e: e.tensor_tensor(qk, qk, mid(ss[:, q, :], HD), ALU.mult), a)
                yield
                pool.wait(a)
                for j in range(2):
                    off = bass.IndirectOffsetOnAxis(ap=slot_of[:, j, t:t + 1], axis=0)
                    s1 = f.dma(pool, f"slots{q}", lambda e: e.indirect_dma_start(
                        out=slot_qkv, out_offset=off, in_=rw[:, q, :], in_offset=None))
                    f.dma(pool, "slotg", lambda e: e.indirect_dma_start(
                        out=slot_gates, out_offset=off, in_=ga[:, j, t, :], in_offset=None))
                ended[t] = [s1, sg, a]

            interleave((qkv_tile(t) for t in range(NT)), 2)
            f.stage("qkv_end")

        f.stage("delta")
        with ExitStack() as s:
            sb = tensors(s)
            state = sb("state", [HD, 2, H, HD])
            decayed = sb("decayed", [HD, H, HD])
            B8 = [P, 2, H, P]
            rw = sb("rw", [P, 2, 3 * D])
            gt = sb("gt", [P, 2, 2 * H])
            eg = sb("eg", [P, 2, 3, H])
            bg = sb("bg", [P, 2, H])
            dec, A, Bm, Xm, Tm, Zm = (sb(n, B8) for n in ("dec", "A", "Bm", "Xm", "Tm", "Zm"))
            kT, qT, qdT = (sb(n, [HD, 2, H, P]) for n in ("kT", "qT", "qdT"))
            kd, kb, vb, qd, u = (sb(n, [P, 2, D]) for n in ("kd", "kb", "vb", "qd", "u"))
            st0 = pool(lambda e: e.memset(state[:, :, :, :], 0.0))
            cur = {"state": st0, "read": None, "decayed": None, "n": 0}
            ended = {}

            def heads(ap, w=HD):
                return ap.rearrange("p (h d) -> p h d", d=w)

            def per_bank(pair):
                return [(b, slice(4 * j, 4 * j + 4)) for j, b in enumerate(pair)]

            def delta_tile(t):
                q = t % 2
                B = bank[4 * q:4 * q + 4]
                lo, hi = B[0:2], B[2:4]
                was = ended.get(t - 2)
                sl = slice(t * P, (t + 1) * P)
                l1 = f.dma(sp, f"rw{q}", lambda e: e.dma_start(rw[:, q, :], slot_qkv[sl, :]), was)
                l2 = f.dma(sp, f"gt{q}", lambda e: e.dma_start(gt[:, q, :], slot_gates[sl, :]))
                Q, K, Vv = (rw[:, q, i * D:(i + 1) * D] for i in range(3))
                beta, g = gt[:, q, 0:H], gt[:, q, H:2 * H]
                for i, n in enumerate(("upto", "ones", "after")):
                    a = pe(lambda e: e.matmul(B[0][:, i * H:(i + 1) * H], const(n), g, start=True, stop=True), l2, was)
                x = act(lambda e: e.activation(eg[:, q, :, :].rearrange("p a h -> p (a h)"), B[0][:, 0:3 * H], ACT.Exp), a, was)
                gu = pool(lambda e: e.tensor_tensor(Zm[:, q, :, :], rep(const("after"), H), mid(g, P), ALU.mult), l2, was)
                yield
                for b, hs in per_bank(hi):
                    a = pe(lambda e: e.matmul(b[:, :], const("upto"), Zm[:, q, hs, :].rearrange("p h n -> p (h n)"),
                                              start=True, stop=True), gu)
                for b, hs in per_bank(hi):
                    ed = act(lambda e: e.activation(dec[:, q, hs, :].rearrange("p h n -> p (h n)"), b[:, :], ACT.Exp), a)
                bb = dve(lambda e: e.tensor_tensor(bg[:, q, :], beta, eg[:, q, 0, :], ALU.mult), x, l2)
                d = {}
                d["vb"] = dve(lambda e: e.tensor_tensor(heads(vb[:, q, :]), heads(Vv), mid(beta, HD), ALU.mult), l1)
                d["qd"] = pool(lambda e: e.tensor_tensor(heads(qd[:, q, :]), heads(Q), mid(eg[:, q, 0, :], HD), ALU.mult), x, l1)
                d["kb"] = dve(lambda e: e.tensor_tensor(heads(kb[:, q, :]), heads(K), mid(bg[:, q, :], HD), ALU.mult), bb)
                d["kd"] = pool(lambda e: e.tensor_tensor(heads(kd[:, q, :]), heads(K), mid(eg[:, q, 2, :], HD), ALU.mult))
                yield
                prior = x
                for src, dst, need in ((K, kT, l1), (Q, qT, l1), (qd[:, q, :], qdT, d["qd"])):
                    pair = lo if dst is not qT else hi
                    for h in range(H):
                        a = pe(lambda e: e.transpose(pair[h // 4][0:HD, (h % 4) * P:(h % 4 + 1) * P],
                                                     src[:, h * HD:(h + 1) * HD], ident), need, prior, ed)
                    yield
                    for b, hs in per_bank(pair):
                        prior = act(lambda e: e.activation(dst[:, q, hs, :].rearrange("p h n -> p (h n)"), b[0:HD, :],
                                                           ACT.Copy), a, was)
                    if dst is kT:
                        kk = prior
                for h in range(H):
                    a = pe(lambda e: e.matmul(hi[h // 4][:, (h % 4) * P:(h % 4 + 1) * P], kT[:, q, h, :], kT[:, q, h, :],
                                              start=True, stop=True), kk, prior)
                yield
                for h in range(H):
                    ad = dve(lambda e: e.scalar_tensor_tensor(A[:, q, h, :], hi[h // 4][:, (h % 4) * P:(h % 4 + 1) * P],
                                                              beta[:, h:h + 1], dec[:, q, h, :], ALU.mult, ALU.mult), a, ed, was)
                for h in range(H):
                    a = pe(lambda e: e.matmul(lo[h // 4][:, (h % 4) * P:(h % 4 + 1) * P], qT[:, q, h, :], kT[:, q, h, :],
                                              start=True, stop=True), prior)
                yield
                for b, hs in per_bank(lo):
                    md = dve(lambda e: e.tensor_tensor(dec[:, q, hs, :], dec[:, q, hs, :],
                                                       b[:, :].rearrange("p (h n) -> p h n", h=4), ALU.mult), a, ad)
                md = pool(lambda e: e.tensor_tensor(dec[:, q, :, :], dec[:, q, :, :], rep(const("lower"), H), ALU.mult), md)
                nb = pool(lambda e: e.tensor_tensor(Bm[:, q, :, :], A[:, q, :, :], rep(const("block1"), H), ALU.mult), ad, was)
                xd = pool(lambda e: e.tensor_tensor(Xm[:, q, :, :], rep(ident, H), Bm[:, q, :, :], ALU.subtract), nb, was)
                yield
                for h in range(H):
                    a = pe(lambda e: e.transpose(hi[h // 4][:, (h % 4) * P:(h % 4 + 1) * P], Xm[:, q, h, :], ident), xd, ad)
                yield
                for b, hs in per_bank(hi):
                    td = act(lambda e: e.activation(Tm[:, q, hs, :].rearrange("p h n -> p (h n)"), b[:, :], ACT.Copy), a, was)
                zused, bused = md, xd
                for b_ in LEVELS[1:]:
                    last = b_ == LEVELS[-1]
                    bd = pool(lambda e: e.tensor_tensor(Bm[:, q, :, :], A[:, q, :, :], rep(const(f"block{b_}"), H), ALU.mult),
                              bused)
                    yield
                    for h in range(H):
                        bused = pe(lambda e: e.matmul(lo[h // 4][:, (h % 4) * P:(h % 4 + 1) * P], Bm[:, q, h, :],
                                                      Tm[:, q, h, :], start=True, stop=True), bd, td, xd, zused)
                    yield
                    for b, hs in per_bank(lo):
                        zd = act(lambda e: e.activation(Zm[:, q, hs, :].rearrange("p h n -> p (h n)"), b[:, :], ACT.Copy),
                                 bused, zused, gu)
                    yield
                    for h in range(H):
                        a = pe(lambda e: e.matmul(hi[h // 4][:, (h % 4) * P:(h % 4 + 1) * P], Xm[:, q, h, :],
                                                  Zm[:, q, h, :], start=True, stop=True), zd, td)
                    if not last:
                        for h in range(H):
                            zused = pe(lambda e: e.matmul(lo[h // 4][:, (h % 4) * P:(h % 4 + 1) * P], Zm[:, q, h, :],
                                                          Xm[:, q, h, :], start=True, stop=True), zd)
                    yield
                    for b, hs in per_bank(hi):
                        td = dve(lambda e: e.tensor_tensor(Tm[:, q, hs, :], Tm[:, q, hs, :],
                                                           b[:, :].rearrange("p (h n) -> p h n", h=4), ALU.subtract), a)
                    if not last:
                        for b, hs in per_bank(lo):
                            xd = dve(lambda e: e.tensor_tensor(Xm[:, q, hs, :], Xm[:, q, hs, :],
                                                               b[:, :].rearrange("p (h n) -> p h n", h=4), ALU.subtract), zused)
                        zused = [zused, xd]
                    else:
                        zused = [zused, a]
                yield
                for h in range(H):
                    a = pe(lambda e: e.transpose(lo[h // 4][:, (h % 4) * P:(h % 4 + 1) * P], dec[:, q, h, :], ident), md, xd, zd)
                yield
                for b, hs in per_bank(lo):
                    mt = act(lambda e: e.activation(Zm[:, q, hs, :].rearrange("p h n -> p (h n)"), b[:, :], ACT.Copy), a, zused)
                for h in range(H):
                    a = pe(lambda e: e.matmul(hi[0][:, h * HD:(h + 1) * HD], Tm[:, q, h, :], vb[:, q, h * HD:(h + 1) * HD],
                                              start=True, stop=True), td, d["vb"])
                yield
                ud = act(lambda e: e.activation(u[:, q, :], hi[0][:, :], ACT.Copy), a, was)
                for h in range(H):
                    a = pe(lambda e: e.matmul(lo[h // 4][0:HD, (h % 4) * P:(h % 4 + 1) * P], kb[:, q, h * HD:(h + 1) * HD],
                                              Tm[:, q, h, :], start=True, stop=True), mt, d["kb"])
                yield
                for b, hs in per_bank(lo):
                    wd = act(lambda e: e.activation(kT[:, q, hs, :].rearrange("p h n -> p (h n)"), b[0:HD, :], ACT.Copy), a)
                yield
                old, new = state[:, cur["n"] % 2, :, :], state[:, (cur["n"] + 1) % 2, :, :]
                cur["n"] += 1
                dc = pool(lambda e: e.tensor_tensor(decayed[:, :, :], old, mid(eg[0:HD, q, 1, :], HD), ALU.mult), cur["state"], x,
                          cur["decayed"])
                for h in range(H):
                    a = pe(lambda e: e.matmul(hi[1][:, h * HD:(h + 1) * HD], kT[:, q, h, :], old[:, h, :], start=True,
                                              stop=True), wd, cur["state"])
                dl = dve(lambda e: e.tensor_tensor(u[:, q, :], u[:, q, :], hi[1][:, :], ALU.subtract), a, ud)
                for h in range(H):
                    a = pe(lambda e: e.matmul(hi[0][0:HD, h * HD:(h + 1) * HD], kd[:, q, h * HD:(h + 1) * HD],
                                              u[:, q, h * HD:(h + 1) * HD], start=True, stop=True), dl, d["kd"])
                ns = dve(lambda e: e.tensor_tensor(new, decayed[:, :, :], hi[0][0:HD, :].rearrange("p (h d) -> p h d", h=H),
                                                   ALU.add), a, dc, cur["read"])
                cur["state"], cur["decayed"] = ns, ns
                for h in range(H):
                    pe(lambda e: e.matmul(lo[0][:, h * HD:(h + 1) * HD], qdT[:, q, h, :], old[:, h, :], start=True,
                                          stop=False))
                    a = pe(lambda e: e.matmul(lo[0][:, h * HD:(h + 1) * HD], Zm[:, q, h, :], u[:, q, h * HD:(h + 1) * HD],
                                              start=False, stop=True))
                cur["read"] = a
                yield
                od = act(lambda e: e.activation(qd[:, q, :], lo[0][:, :], ACT.Copy), a)
                ended[t] = [od, f.dma(sp, f"out{q}", lambda e: e.dma_start(slot_out[sl, :], qd[:, q, :]), od), ns]

            if stop >= 3:
                interleave((delta_tile(t) for t in range(ST)), 2)
            f.stage("delta_end")

        f.stage("merge")
        with ExitStack() as s:
            sb = tensors(s)
            wo = sb("wo", [P, KC, D])
            onw = sb("onw", [P, HD])
            ab = sb("ab", [P, 2, 3, D])
            ss = sb("ss", [P, 2, H])
            oT = sb("oT", [P, 2, D])
            lw = f.dma(sp, "w", lambda e: e.dma_start(wo[:, :, :], rows(I["L0_ffn_Wo"])))
            ln = f.dma(sp, "n", lambda e: e.dma_start(onw[:, :], vec_row(I["L0_ffn_o_norm_weight"], P, HD)))
            ended = {}

            def merge_tile(t):
                q = t % 2
                B = bank[4 * q:4 * q + 4]
                was = ended.get(t - 2)
                pool.wait(was)
                for j in range(2):
                    g = f.dma(pool, f"in{q}", lambda e: e.indirect_dma_start(
                        out=ab[:, q, j, :], out_offset=None, in_=slot_out,
                        in_offset=bass.IndirectOffsetOnAxis(ap=slot_of[:, j, t:t + 1], axis=0)))
                g2 = f.dma(sp, f"gate{q}", lambda e: e.dma_start(ab[:, q, 2, :], gate_rows[t * P:(t + 1) * P, :]), was)
                yield
                o = ab[:, q, 0, :]
                a = dve(lambda e: e.tensor_scalar(o, o, slot_w[:, 0, t:t + 1], None, ALU.mult), g)
                a = dve(lambda e: e.scalar_tensor_tensor(o, ab[:, q, 1, :], slot_w[:, 1, t:t + 1], o, ALU.mult, ALU.add), a)
                b = pool(lambda e: e.tensor_tensor(ab[:, q, 1, :], o, o, ALU.mult), a)
                yield
                b = dve(lambda e: e.tensor_reduce(ss[:, q, :], ab[:, q, 1, :].rearrange("p (h d) -> p h d", d=HD), AX.X,
                                                  ALU.add), b, was)
                b = rsqrt(ss[:, q, :], ss[:, q, :], 1e-5, 1.0 / HD, b)
                o3 = o.rearrange("p (h d) -> p h d", d=HD)
                a = dve(lambda e: e.tensor_tensor(o, o, ab[:, q, 2, :], ALU.mult), g2, a, b)
                a = dve(lambda e: e.tensor_tensor(o3, o3, mid(ss[:, q, :], HD), ALU.mult), a, b)
                a = dve(lambda e: e.tensor_tensor(o3, o3, rep(onw[:, :], H), ALU.mult), a, ln)
                yield
                for r in project_back(o, oT[:, q, :], wo, B[1], B[0], t, a, lw, was):
                    yield
                ended[t] = [r, a]

            if stop >= 3:
                interleave((merge_tile(t) for t in range(NT)), 2)
            f.stage("merge_end")
        layer.close()
        if stop <= 3:
            write_out()
            return
        f.stage("ln2")
        layer = ExitStack()
        xnT = layer.enter_context(nc.sbuf_tensor("xnT2", [P, KC, N], F32))
        with ExitStack() as s:
            xn = s.enter_context(nc.sbuf_tensor("xn2", [P, 2, D], F32))
            layernorm(xnT, xn, xn_rows)
        f.stage("lin")
        with ExitStack() as s:
            sb = tensors(s)
            wq, wk, wv, wo = (sb(n, [P, KC, D]) for n in ("wq", "wk", "wv", "wo"))
            lw = [f.dma(sp, "w", lambda e: e.dma_start(w[:, :, :], rows(I["L1_mix_W_qkvT"])[:, :, i * D:(i + 1) * D]))
                  for i, w in enumerate((wq, wk, wv))]
            lw.append(f.dma(sp, "w", lambda e: e.dma_start(wo[:, :, :], rows(I["L1_mix_W_projT"]))))
            bo = sb("bo", [P, D])
            lb = f.dma(act, "b", lambda e: e.dma_start(bo[:, :], vec_row(I["L1_mix_b_proj"], P, D)))
            HV = HD + 1
            k = sb("k", [P, 2, D])
            va = sb("va", [P, 2, H, HV])
            kv = sb("kv", [P, KC, 2, HV])
            qT = sb("qT", [P, 2, KC, P])
            o = sb("o", [P, 2, D])
            oT = sb("oT", [P, 2, D])
            rc = sb("rc", [P, 2, H])
            z = pool(lambda e: e.memset(kv[:, :, :, :], 0.0))
            on = pool(lambda e: e.memset(va[:, :, :, HD:HV], 1.0))
            ended = {}

            def kv_tile(t):
                q = t % 2
                B = bank[2 * q:2 * q + 2]
                was = ended.get(t - 2)
                for b, w in ((B[0], wk), (B[1], wv)):
                    for c in range(KC):
                        a = pe(lambda e: e.matmul(b[:, :], xnT[:, c, t * P:(t + 1) * P], w[:, c, :], start=c == 0,
                                                  stop=c == KC - 1), lw, was)
                    if w is wk:
                        x = dve(lambda e: e.tensor_scalar(k[:, q, :], b[:, :], 0.0, HD ** -0.5, ALU.max, ALU.add), a, was)
                    else:
                        y = act(lambda e: e.activation(va[:, q, :, 0:HD], b[:, :].rearrange("p (h d) -> p h d", h=H),
                                                       ACT.Copy), a, was)
                    yield
                for p_ in range(KC):
                    a = pe(lambda e: e.matmul(bank[4 + p_][:, 0:2 * HV], k[:, q, p_ * P:(p_ + 1) * P],
                                              va[:, q, 2 * p_:2 * p_ + 2, :].rearrange("p h d -> p (h d)"),
                                              start=t == 0, stop=t == NT - 1), x, y, on)
                ended[t] = a

            interleave((kv_tile(t) for t in range(NT)), 2)
            for p_ in range(KC):
                for j in range(2):
                    half = slice(j * HD, (j + 1) * HD)
                    kd = dve(lambda e: e.tensor_copy(kv[half, p_, j, :], bank[4 + p_][half, j * HV:(j + 1) * HV]),
                             ended[NT - 1], z)
            f.stage("lino")
            ended = {}

            def lin_tile(t):
                q = t % 2
                B = bank[4 * q:4 * q + 4]
                was = ended.get(t - 2)
                bx = pool(lambda e: e.tensor_tensor(X[:, t, :], X[:, t, :], bo[:, :], ALU.add), lb)
                for m in range(KC):
                    for c in range(KC):
                        a = pe(lambda e: e.matmul(B[0][:, m * P:(m + 1) * P], wq[:, c, m * P:(m + 1) * P],
                                                  xnT[:, c, t * P:(t + 1) * P], start=c == 0, stop=c == KC - 1), was)
                yield
                a = dve(lambda e: e.tensor_scalar(qT[:, q, :, :].rearrange("p c n -> p (c n)"), B[0][:, :], 0.0, HD ** -0.5,
                                                  ALU.max, ALU.add), a, was)
                yield
                for p_ in range(KC):
                    b = pe(lambda e: e.matmul(B[1 + p_ // 2][:, (p_ % 2) * 2 * HV:(p_ % 2 + 1) * 2 * HV], qT[:, q, p_, :],
                                              kv[:, p_, :, :].rearrange("p h d -> p (h d)"), start=True, stop=True), a)
                yield
                for j in range(2):
                    n4 = B[1 + j][:, 0:4 * HV].rearrange("p (h d) -> p h d", h=4)
                    a = dve(lambda e: e.tensor_scalar(rc[:, q, 4 * j:4 * j + 4], n4[:, :, HD], 1e-6, None, ALU.add), b, was)
                    a = dve(lambda e: e.reciprocal(rc[:, q, 4 * j:4 * j + 4], rc[:, q, 4 * j:4 * j + 4]), a)
                    a = dve(lambda e: e.tensor_tensor(o[:, q, j * 256:(j + 1) * 256].rearrange("p (h d) -> p h d", h=4),
                                                      n4[:, :, 0:HD], mid(rc[:, q, 4 * j:4 * j + 4], HD), ALU.mult), a)
                yield
                for r in project_back(o[:, q, :], oT[:, q, :], wo, B[3], B[0], t, a, bx):
                    yield
                ended[t] = [r, a]

            interleave((lin_tile(t) for t in range(NT)), 2)
            f.stage("lin_end")
        layer.close()

        f.stage("conv")
        layer = ExitStack()
        acc = layer.enter_context(nc.sbuf_tensor("acc", [P, NT, D], F32))
        epsr = layer.enter_context(nc.sbuf_tensor("epsr", [P, 1], F32))
        a = f.dma(sp, "xn", lambda e: e.dma_start(acc[:, :, :], xn_rows.rearrange("(t p) d -> p t d", p=P)))
        b = f.dma(sp, "eps", lambda e: e.dma_start(epsr[:, :], vec_row(I["L1_gnn_eps"], P, 1)))
        b = dve(lambda e: e.tensor_scalar(epsr[:, :], epsr[:, :], 1.0, None, ALU.add), b)
        for t in range(NT):
            dve(lambda e: e.tensor_scalar(acc[:, t, :], acc[:, t, :], epsr[:, 0:1], None, ALU.mult), a, b)
        f.stage("convs")
        wes = ExitStack()
        we = wes.enter_context(nc.sbuf_tensor("we", [65, D], F32))
        lwe = [f.dma(sp, "we", lambda e: e.dma_start(we[0:64, :], I["L1_gnn_W_e"])),
               f.dma(sp, "we", lambda e: e.dma_start(we[64:65, :], vec_row(I["L1_gnn_b_e"], 1, D)))]

        def message_rhs(sb):
            src = sb("src", [P, 4, D])
            msg = sb("msg", [P, 4, D])
            eT = sb("eT", [65, 4, P])

            def make(i, q, r, loaded, before):
                pool.wait(loaded, before)
                g = f.dma(pool, f"src{q}", lambda e: e.indirect_dma_start(
                    out=src[:, q, :], out_offset=None, in_=xn_rows,
                    in_offset=bass.IndirectOffsetOnAxis(ap=r[:, 66:67].bitcast(I32), axis=0)))
                a = pe(lambda e: e.transpose(bank[4 + q][0:65, 0:P], r[:, 0:65], ident), loaded, before)
                yield None
                a = act(lambda e: e.activation(eT[:, q, :], bank[4 + q][0:65, 0:P], ACT.Copy), a)
                yield None
                a = pe(lambda e: e.matmul(bank[4 + q][:, :], eT[:, q, :], we[:, :], start=True, stop=True), a, lwe)
                yield None
                a = dve(lambda e: e.tensor_tensor(msg[:, q, :], bank[4 + q][:, :], src[:, q, :], ALU.add), a, g)
                yield None
                a = act(lambda e: e.activation(msg[:, q, :], msg[:, q, :], ACT.Relu), a)
                yield (msg[:, q, :], a)
            return make

        if stop >= 5:
            sum_edges("conv", R1, sorted_edge, bucket1, acc, 65, message_rhs, 4)
        wes.close()

        f.stage("mlp")
        NB = N // 512
        with ExitStack() as s:
            sb = tensors(s)
            hT = sb("hT", [P, KC, N])
            freed = {}
            for t in range(NT):
                b = bank[t % 2]
                for c in range(KC):
                    a = pe(lambda e: e.transpose(b[:, c * P:(c + 1) * P], acc[:, t, c * P:(c + 1) * P], ident), freed.get(t % 2))
                freed[t % 2] = act(lambda e: e.activation(hT[:, :, t * P:(t + 1) * P],
                                                          b[:, :].rearrange("p (c n) -> p c n", c=KC), ACT.Copy), a)
            f.stage("mlp1")
            h1 = sb("h1", [P, 2 * KC, N])
            w2 = sb("w2", [P, 2 * KC, D])
            w1 = acc[:, :, :].rearrange("p a b -> p (a b)")[:, 0:KC * 2 * D].rearrange("p (c n) -> p c n", c=KC)
            st = sb("st", [P, 2 * KC, NB, 6])
            mv = sb("mv", [P, 2 * KC, 2])
            vec = sb("vec", [P, 6, 2 * KC])
            l1 = f.dma(sp, "w1", lambda e: e.dma_start(w1, rows(I["L1_gnn_W1"])))
            l2 = f.dma(sp, "w2", lambda e: e.dma_start(w2[:, :, :], rows(I["L1_gnn_W2"])))
            with nc.allow_non_contiguous_dma(reason="small columns"):
                lb = [f.dma(act, "v", lambda e: e.dma_start(vec[:, i, 0:w], I["L1_gnn_" + n].rearrange("(c p) -> p c", p=P)))
                      for i, (n, w) in enumerate((("b1", 8), ("g1", 8), ("beta1", 8), ("b2", 4), ("g2", 4), ("beta2", 4)))]

            def norm_layer(tag, n_out, w, src, n_in, dst, v, loaded):
                freed, i = {}, 0
                for m in range(n_out):
                    for nb in range(NB):
                        b = bank[i % 4]
                        cols = slice(nb * 512, (nb + 1) * 512)
                        for c in range(n_in):
                            a = pe(lambda e: e.matmul(b[:, :], w[:, c, m * P:(m + 1) * P], src[:, c, cols],
                                                      start=c == 0, stop=c == n_in - 1), loaded, freed.get(i % 4))
                        freed[i % 4] = a = act(lambda e: e.activation(dst[:, m, cols], b[:, :], ACT.Identity,
                                                                      bias=vec[:, v, m:m + 1]), a, lb)
                        a = dve(lambda e: e.bn_stats(st[:, m, nb, :], dst[:, m, cols]), a)
                        i += 1
                    a = dve(lambda e: e.bn_aggr(mv[:, m, :], st[:, m, :, :].rearrange("p a b -> p (a b)")), a)
                f.stage(tag + "n")
                r = rsqrt(mv[:, 0:n_out, 1], mv[:, 0:n_out, 1], 1e-5, 1.0)
                sc = dve(lambda e: e.tensor_tensor(mv[:, 0:n_out, 1], mv[:, 0:n_out, 1], vec[:, v + 1, 0:n_out], ALU.mult), r)
                a = dve(lambda e: e.tensor_tensor(mv[:, 0:n_out, 0], mv[:, 0:n_out, 0], mv[:, 0:n_out, 1], ALU.mult), sc)
                a = dve(lambda e: e.tensor_tensor(mv[:, 0:n_out, 0], vec[:, v + 2, 0:n_out], mv[:, 0:n_out, 0],
                                                  ALU.subtract), a)
                for m in range(n_out):
                    a = act(lambda e: e.activation(dst[:, m, :], dst[:, m, :], ACT.Silu, bias=mv[:, m, 0:1],
                                                   scale=mv[:, m, 1:2]), a)
                f.stage(tag + "e")

            norm_layer("bn1", 2 * KC, w1, hT, KC, h1, 0, l1)
            norm_layer("bn2", KC, w2, h1, 2 * KC, hT, 3, None)
            freed = {}
            for t in range(NT):
                b = bank[t % 2]
                for c in range(KC):
                    a = pe(lambda e: e.transpose(b[:, c * P:(c + 1) * P], hT[:, c, t * P:(t + 1) * P], ident), freed.get(t % 2))
                freed[t % 2] = dve(lambda e: e.tensor_tensor(X[:, t, :], X[:, t, :], b[:, :], ALU.add), a)
            f.stage("mlp_end")
        layer.close()
        if stop <= 5:
            write_out()
            return

        f.stage("ln3")
        layer = ExitStack()
        xnT = layer.enter_context(nc.sbuf_tensor("xnT3", [P, KC, N], F32))
        slot_of = layer.enter_context(nc.sbuf_tensor("slot_of3", [P, NT], I32))
        slot_w = layer.enter_context(nc.sbuf_tensor("slot_w3", [P, NT], F32))
        with ExitStack() as s:
            sb = tensors(s)
            xn = sb("xn", [P, 2, D])
            zero = sb("zero", [P, D])
            a = pool(lambda e: e.memset(zero[:, :], 0.0))
            for t in range(NT):
                f.dma(sp, "zero", lambda e: e.dma_start(expert_in[t * P:(t + 1) * P, :], zero[:, :]), a)
            layernorm(xnT, xn, xn_rows)
        f.stage("sink")
        with ExitStack() as s:
            sb = tensors(s)
            wg = sb("wg", [P, KC, FE])
            lw = f.dma(sp, "w", lambda e: e.dma_start(wg[:, :, :], rows(I["L1_ffn_gate_weight"][0])))
            big = {n: sb(n, [P, FE, NT]) for n in ("g", "sel", "w", "later", "pos", "base", "tot", "win", "tmp")}
            V = {n: t[:, :, :] for n, t in big.items()}
            flat = {n: v.rearrange("p e t -> p (e t)") for n, v in V.items()}
            r8 = sb("r8", [P, FE])
            r16 = sb("r16", [P, NT])
            gT = sb("gT", [FE, N])
            top = sb("top", [FE, 2, 8])
            for t in range(NT):
                for c in range(KC):
                    a = pe(lambda e: e.matmul(bank[2][:, t * FE:(t + 1) * FE], xnT[:, c, t * P:(t + 1) * P], wg[:, c, :],
                                              start=c == 0, stop=c == KC - 1), lw)
            a = dve(lambda e: e.tensor_scalar(V["g"], bank[2][:, 0:NT * FE].rearrange("p (t e) -> p e t", e=FE), 1e-6, None,
                                              ALU.max), a)
            for it in range(8):
                a = dve(lambda e: e.tensor_reduce(r8[:, :], V["g"], AX.X, ALU.add), a)
                a = pe(lambda e: e.matmul(bank[3][:, 0:FE], ones, r8[:, :], start=True, stop=True), a)
                a = dve(lambda e: e.reciprocal(r8[:, :], bank[3][:, 0:FE]), a)
                a = dve(lambda e: e.tensor_tensor(V["g"], V["g"], mid(r8[:, :], NT), ALU.mult), a)
                a = dve(lambda e: e.tensor_reduce(r16[:, :], V["g"].rearrange("p e t -> p t e"), AX.X, ALU.add), a)
                a = dve(lambda e: e.reciprocal(r16[:, :], r16[:, :]), a)
                a = dve(lambda e: e.tensor_tensor(V["g"], V["g"], rep(r16[:, :], FE), ALU.mult), a)
            gd = a
            freed = {}
            for t in range(NT):
                a = pe(lambda e: e.transpose(bank[t % 2][0:FE, 0:P], V["g"][:, :, t], ident), gd, freed.get(t % 2))
                freed[t % 2] = a = dve(lambda e: e.tensor_copy(gT[:, t * P:(t + 1) * P], bank[t % 2][0:FE, 0:P]), a)
            for i in range(CAP // 8):
                a = dve(lambda e: e.max(top[:, i % 2, :], gT[:, :]), a)
                a = dve(lambda e: e.match_replace(gT[:, :], top[:, i % 2, :], gT[:, :], -1.0), a)
            a = dve(lambda e: e.tensor_scalar(gT[:, :], gT[:, :], 0.0, None, ALU.is_lt), a)
            for t in range(NT):
                b = pe(lambda e: e.transpose(bank[4][:, t * FE:(t + 1) * FE], gT[:, t * P:(t + 1) * P],
                                             ident[0:FE, 0:FE]), a)
            sel = dve(lambda e: e.tensor_copy(V["sel"], bank[4][:, 0:NT * FE].rearrange("p (t e) -> p e t", e=FE)), b)
            pos = slots_of(flat["sel"], flat["pos"], flat["base"], flat["tot"], FE, sel)
            a = dve(lambda e: e.memset(V["later"][:, FE - 1, :], 0.0))
            for x in range(FE - 2, -1, -1):
                a = dve(lambda e: e.tensor_tensor(V["later"][:, x, :], V["later"][:, x + 1, :], V["sel"][:, x + 1, :],
                                                  ALU.max), a, sel)
            a = dve(lambda e: e.tensor_tensor(V["win"], V["sel"], V["later"], ALU.is_gt), a, sel)
            w_ = dve(lambda e: e.tensor_tensor(V["tmp"], V["win"], V["g"], ALU.mult), a)
            w_ = dve(lambda e: e.tensor_reduce(slot_w[:, :], V["tmp"].rearrange("p e t -> p t e"), AX.X, ALU.add), w_)
            b = dve(lambda e: e.tensor_tensor(V["tmp"], V["win"], V["pos"], ALU.mult), w_, pos)
            b = dve(lambda e: e.tensor_reduce(r16[:, :], V["tmp"].rearrange("p e t -> p t e"), AX.X, ALU.add), b)
            c = dve(lambda e: e.tensor_reduce(V["later"][:, 0, :], V["win"].rearrange("p e t -> p t e"), AX.X, ALU.add), a, b)
            put = sb("put", [P, NT], I32)
            c = dve(lambda e: e.tensor_scalar(V["later"][:, 0, :], V["later"][:, 0, :], -float(N), float(N), ALU.mult,
                                              ALU.add), c)
            c = dve(lambda e: e.tensor_tensor(V["later"][:, 0, :], V["later"][:, 0, :], r16[:, :], ALU.add), c)
            c = dve(lambda e: e.tensor_copy(put[:, :], V["later"][:, 0, :]), c)
            c1 = dve(lambda e: e.tensor_copy(slot_of[:, :], r16[:, :]), b)
            xr = sb("xr", [P, 2, D])
            used = {}
            for t in range(NT):
                q = t % 2
                l = f.dma(sp, f"xr{q}", lambda e: e.dma_start(xr[:, q, :], xn_rows[t * P:(t + 1) * P, :]), used.get(q))
                pool.wait(l, c, c1)
                used[q] = f.dma(pool, f"put{q}", lambda e: e.indirect_dma_start(
                    out=expert_in, out_offset=bass.IndirectOffsetOnAxis(ap=put[:, t:t + 1], axis=0),
                    in_=xr[:, q, :], in_offset=None, bounds_check=N - 1, oob_is_err=False))
            f.stage("experts")
            ew = sb("ew", [P, 2, KC, D])
            xe = sb("xe", [P, 2, D])
            xT = sb("xT", [P, 2, D])
            ye = sb("ye", [P, 2, D])
            wfree, ended = {}, {}
            loaded = {}

            def expert_tile(t):
                q, x = t % 2, t // 2
                was = ended.get(t - 2)
                if t % 2 == 0:
                    loaded[x] = f.dma(act, f"ew{x % 2}", lambda e: e.dma_start(ew[:, x % 2, :, :], rows(I["L1_ffn_experts"][x])),
                                      wfree.get(x - 2))
                l = f.dma(sp, f"xe{q}", lambda e: e.dma_start(xe[:, q, :], expert_in[t * P:(t + 1) * P, :]), was)
                yield
                B = bank[2 * q:2 * q + 2]
                for c in range(KC):
                    a = pe(lambda e: e.transpose(B[0][:, c * P:(c + 1) * P], xe[:, q, c * P:(c + 1) * P], ident), l, was)
                yield
                a = act(lambda e: e.activation(xT[:, q, :], B[0][:, :], ACT.Copy), a)
                yield
                for c in range(KC):
                    a = pe(lambda e: e.matmul(B[1][:, :], xT[:, q, c * P:(c + 1) * P], ew[:, x % 2, c, :], start=c == 0,
                                              stop=c == KC - 1), a, loaded[x])
                wfree[x] = a
                yield
                a = dve(lambda e: e.tensor_copy(ye[:, q, :], B[1][:, :]), a, was)
                ended[t] = [a, f.dma(sp, f"ye{q}", lambda e: e.dma_start(expert_out[t * P:(t + 1) * P, :], ye[:, q, :]), a)]

            interleave((expert_tile(t) for t in range(NT)), 2)
            f.stage("combine")
            used = {}
            for t in range(NT):
                q = t % 2
                pool.wait(used.get(q))
                l = f.dma(pool, f"in{q}", lambda e: e.indirect_dma_start(
                    out=xr[:, q, :], out_offset=None, in_=expert_out,
                    in_offset=bass.IndirectOffsetOnAxis(ap=slot_of[:, t:t + 1], axis=0)))
                used[q] = dve(lambda e: e.scalar_tensor_tensor(X[:, t, :], xr[:, q, :], slot_w[:, t:t + 1], X[:, t, :],
                                                               ALU.mult, ALU.add), l)
        f.stage("store")
        layer.close()
        write_out()


def kernel(**inputs):
    import concourse.bacc as _bacc
    from concourse.bass_utils import run_bass_kernel_spmd as _run

    nc = _bacc.Bacc("TRN2", target_bir_lowering=False, num_devices=1)
    table, const_at = constants()
    arrays, args = {}, {}
    for name, a in list(inputs.items()) + [("const", table), ("L0_mix_projT", np.asarray(inputs["L0_mix_proj"]).T),
                                        ("L1_mix_W_qkvT", np.asarray(inputs["L1_mix_W_qkv"]).T),
                                        ("L1_mix_W_projT", np.asarray(inputs["L1_mix_W_proj"]).T)]:
        a = np.asarray(a)
        if a.ndim == 0:
            a = a.reshape(1)
        a = np.ascontiguousarray(a)
        arrays[f"in_{name}"] = a
        args[name] = nc.dram_tensor(f"in_{name}", a.shape, mybir.dt.from_np(a.dtype), kind="ExternalInput").ap()
    out = nc.dram_tensor("out_0", (N, D), F32, kind="ExternalOutput").ap()
    program(nc, args, const_at, out, STOP)
    r = _run(nc, [arrays], core_ids=[0])
    return r.results[0]["out_0"]


STOP = 99
```

```python
import numpy as np
import concourse.bass as bass
from concourse import mybir
from contextlib import ExitStack

F32 = mybir.dt.float32
I32 = mybir.dt.int32
ALU = mybir.AluOpType
ACT = mybir.ActivationFunctionType
AX = mybir.AxisListType

P = 128
N, D = 2048, 512
NT = N // P
KC = D // P
H, HD = 8, 64
HV = HD + 2
G = 64
E = 32768
EC = E // P
TG = 2
GROUP_BITS = (TG * P).bit_length() - 1
EG = EC // TG + NT
ET = EG * TG
R0 = H + 2
R1 = 64 + 3
M = 266
MC = [(0, 128), (128, 128), (256, 10)]
EX = 4
SL = 2 * N
ST = SL // P
FE, CAP = 8, N // 8
LEVELS = [1, 2, 4, 8, 16, 32, 64]
EPS_LN = 1e-5
LIMIT = 8000
RESET = -1.0e4


def constants():
    r = np.arange(P)[:, None]
    c = np.arange(P)[None, :]
    parts = {
        "ident": (r == c),
        "ones": np.ones((P, P)),
        "before": (r < c),
        "upto": (r <= c),
        "after": (r > c),
        "lower": (r >= c),
        "iota": np.broadcast_to(c, (P, P)),
    }
    parts["same_half"] = (r // HD == c // HD)
    for b in LEVELS:
        parts[f"fill{b}"] = ((c // b) % 2 == 1) & (r // b == c // b - 1)
    parts["group_start"] = np.broadcast_to(np.arange(EG)[None, :] * TG * P, (P, EG))
    sel = np.zeros((P, KC, H))
    for k in range(KC):
        for p in range(P):
            sel[p, k, 2 * k + p // HD] = 1
    parts["head_of_row"] = sel.reshape(P, -1)
    parts["parity"] = np.stack([(np.arange(P) < HD), (np.arange(P) >= HD)], 1)
    parts["earlier"] = np.broadcast_to((np.arange(EX)[None, :] < np.arange(EX)[:, None]).reshape(1, -1), (P, EX * EX))
    at, n = {}, 0
    for name, a in parts.items():
        at[name] = (n, a.shape[1])
        n += a.shape[1]
    return np.ascontiguousarray(np.concatenate([np.asarray(a, np.float32) for a in parts.values()], 1)), at


class Lane:

    def __init__(self, flow, name, engine):
        self.flow, self.name, self.engine, self.sem, self.seen = flow, name, engine, None, {}
        self.issued, self.marked = [], []

    def wait(self, *events):
        for e in events:
            if e is None:
                continue
            if isinstance(e, list):
                self.wait(*e)
                continue
            sem, value, stage = e
            if value is None:
                value = self.flow.totals[sem] if stage == self.flow.number else 0
            elif stage == self.flow.number:
                value = sem.count_of(value)
                sem = sem.sem
            else:
                continue
            if self.seen.get(sem, 0) < value:
                self.seen[sem] = value
                self.engine.wait_ge(sem, value)

    def count_of(self, place):
        if not self.marked or self.marked[-1] < place:
            self.issued[place].then_inc(self.sem, 1)
            self.marked.append(place)
        count = len(self.marked)
        while count > 1 and self.marked[count - 2] >= place:
            count -= 1
        return count

    def __call__(self, build, *after):
        self.wait(*after)
        self.issued.append(build(self.engine))
        return (self, len(self.issued) - 1, self.flow.number)


class Flow:

    def __init__(self, nc, ctx):
        self.nc, self.ctx = nc, ctx
        self.lanes = [Lane(self, *x) for x in (("pe", nc.tensor), ("act", nc.scalar), ("dve", nc.vector),
                                               ("pool", nc.gpsimd), ("sp", nc.sync))]
        self.number, self.rings, self.totals, self.idle = 0, {}, {}, {True: [], False: []}

    def stage(self, name, pool_apart=False):
        lanes = [lane for lane in self.lanes if not (pool_apart and lane.name == "pool")]
        kept = {ring: sem for ring, sem in self.rings.items() if pool_apart and ring[0]}
        ends = [(lane, len(lane.issued) - 1, self.number) for lane in lanes if lane.issued]
        ends += [(sem, None, self.number) for ring, sem in self.rings.items() if ring not in kept]
        for lane in lanes:
            lane.wait(ends)
        for lane in lanes:
            if lane.sem is None or len(lane.marked) > LIMIT:
                lane.sem = self.ctx.enter_context(self.nc.semaphore(f"{lane.name}_from_{name}"))
                lane.issued, lane.marked = [], []
        for ring, sem in self.rings.items():
            if ring not in kept:
                self.idle[ring[0]].append(sem)
        self.number, self.rings, self.name = self.number + 1, kept, name

    def dma(self, lane, ring, build, *after):
        lane.wait(*after)
        ring = (lane.name == "pool", ring)
        if ring not in self.rings:
            idle = self.idle[ring[0]]
            if not idle:
                idle.append(self.ctx.enter_context(self.nc.semaphore(f"ring{len(self.totals)}")))
                self.totals[idle[-1]] = 0
            self.rings[ring] = idle.pop()
        sem = self.rings[ring]
        self.totals[sem] += 16
        build(lane.engine).then_inc(sem, 16)
        return (sem, None, self.number)


def interleave(steps, width, gap=0):
    steps = list(steps)
    live, beside, wait = [], [], 0
    while steps or live or beside:
        wait -= 1
        while steps and len(live) < width and wait <= 0:
            live.append(steps.pop(0))
            wait = gap
        for g in live + beside:
            said = next(g, StopIteration)
            if said is StopIteration:
                (live if g in live else beside).remove(g)
            elif said is not None and not isinstance(said, tuple):
                beside.append(said)


def mid(ap, n):
    return ap.unsqueeze(2).broadcast_to([ap.shape[0], ap.shape[1], n])


def rep(ap, n):
    return ap.unsqueeze(1).broadcast_to([ap.shape[0], n, ap.shape[1]])


def program(nc, I, const_at, out):
    ctx = ExitStack()
    with ctx:
        f = Flow(nc, ctx)
        pe, act, dve, pool, sp = f.lanes
        bank = [ctx.enter_context(nc.psum_tensor(f"bank{i}", [P, 512], F32)) for i in range(8)]

        def scratch(name, shape, dt=F32):
            return nc.dram_tensor(name, shape, dt, kind="Internal").ap()

        sorted_bias = scratch("sorted_bias", (P * ET, R0))
        sorted_edge = scratch("sorted_edge", (P * ET, R1))
        xn_rows = scratch("xn_rows", (N, D))
        gate_rows = scratch("gate_rows", (N, D))
        slot_qkv = scratch("slot_qkv", (SL, 3 * D))
        slot_gates = scratch("slot_gates", (SL, 2 * H))
        slot_out = scratch("slot_out", (SL, D))
        expert_in = scratch("expert_in", (N, D))
        expert_out = scratch("expert_out", (N, D))

        f.stage("start")
        cw = sum(w for _, w in const_at.values())
        C = ctx.enter_context(nc.sbuf_tensor("C", [P, cw], F32))
        X = ctx.enter_context(nc.sbuf_tensor("X", [P, NT, D], F32))
        bucket0 = ctx.enter_context(nc.sbuf_tensor("bucket0", [P, EG], I32))
        bucket1 = ctx.enter_context(nc.sbuf_tensor("bucket1", [P, EG], I32))
        neg_half = ctx.enter_context(nc.sbuf_tensor("neg_half", [P, P], F32))

        def const(name):
            a, w = const_at[name]
            return C[:, a:a + w]

        ident, ones = const("ident"), const("ones")
        f.dma(sp, "const", lambda e: e.dma_start(C[:, :], I["const"]))
        f.dma(sp, "x", lambda e: e.dma_start(X[:, :, :], I["x"].rearrange("(t p) d -> p t d", p=P)))
        pool(lambda e: e.memset(neg_half[:, :], -0.5))

        def tensors(s):
            def sb(name, shape, dt=F32):
                return s.enter_context(nc.sbuf_tensor(f"{f.name}_{name}", shape, dt))
            return sb

        def rows(ap):
            return ap.rearrange("(c p) n -> p c n", p=P)

        def vec_row(ap, parts, n):
            return ap.rearrange("(a n) -> a n", a=1).broadcast_to([parts, n])

        def rsqrt(dst, src, eps, scale, *after):
            a = dve(lambda e: e.tensor_scalar(dst, src, scale, eps, ALU.mult, ALU.add), *after)
            n = dst.shape[1]
            return pool(lambda e: e.tensor_tensor(dst, dst, neg_half[0:dst.shape[0], 0:n], ALU.pow), a)

        def edge_places(key, bkt, tmp, hot, run, sb, bucket_of_group, place, ranks, got, *after):
            small = sb("small", [P, 8, NT])
            ints = sb("ints", [P, 2, NT], I32)
            pos = sb("pos", [P, EC])
            tl = sb("tl", [P, EG])
            b = dve(lambda e: e.tensor_single_scalar(tmp[:, :], key[:, :], 7, ALU.logical_shift_right), got, *after)
            b = dve(lambda e: e.tensor_copy(bkt[:, :], tmp[:, :]), b)
            for i in range(NT):
                b1 = dve(lambda e: e.tensor_single_scalar(hot[:, i, :], bkt[:, :], float(i), ALU.is_equal), b)
            b = dve(lambda e: e.tensor_tensor_scan(run.rearrange("p b c -> p (b c)"), hot.rearrange("p b c -> p (b c)"),
                                                   hot.rearrange("p b c -> p (b c)"), 0.0, ALU.add, ALU.max), b1)
            b = dve(lambda e: e.tensor_copy(small[:, 0, :], run[:, :, EC - 1]), b)
            c1 = dve(lambda e: e.tensor_copy(small[:, 1, 0:1], small[:, 0, 0:1]), b)
            c2 = dve(lambda e: e.tensor_tensor(small[:, 1, 1:NT], small[:, 0, 1:NT], small[:, 0, 0:NT - 1],
                                               ALU.subtract), b)
            pe(lambda e: e.matmul(ranks[:, 0:NT], const("before"), small[:, 1, :], start=True, stop=True), c1, c2)
            c = pe(lambda e: e.matmul(ranks[:, NT:2 * NT], ones, small[:, 1, :], start=True, stop=True))
            c = dve(lambda e: e.tensor_scalar(small[:, 2, :], ranks[:, NT:2 * NT], TG * P - 1.0, None, ALU.add), c)
            c = dve(lambda e: e.tensor_copy(ints[:, 0, :], small[:, 2, :]), c)
            c = dve(lambda e: e.tensor_scalar(ints[:, 1, :], ints[:, 0, :], GROUP_BITS, GROUP_BITS, ALU.logical_shift_right,
                                              ALU.logical_shift_left), c)
            c = dve(lambda e: e.tensor_copy(small[:, 3, :], ints[:, 1, :]), c)
            c = dve(lambda e: e.tensor_tensor_scan(small[:, 4, :], small[:, 3, :], small[:, 3, :], 0.0,
                                                   ALU.add, ALU.max), c)
            d = dve(lambda e: e.tensor_tensor(small[:, 5, :], small[:, 4, :], small[:, 3, :], ALU.subtract), c)
            d = dve(lambda e: e.tensor_tensor(small[:, 5, :], small[:, 5, :], ranks[:, 0:NT], ALU.add), d)
            d = dve(lambda e: e.tensor_tensor(small[:, 5, :], small[:, 5, :], small[:, 0, :], ALU.subtract), d)
            d = dve(lambda e: e.tensor_tensor(small[:, 5, :], small[:, 5, :], small[:, 1, :], ALU.add), d)
            d = dve(lambda e: e.tensor_scalar(small[:, 5, :], small[:, 5, :], -1.0, None, ALU.add), d)
            for i in range(NT):
                d1 = dve(lambda e: e.scalar_tensor_tensor(run[:, i, :], run[:, i, :], small[:, 5, i:i + 1],
                                                          hot[:, i, :], ALU.add, ALU.mult), d)
            d = dve(lambda e: e.tensor_reduce(pos[:, :], run.rearrange("p b c -> p c b"), AX.X, ALU.add), d1)
            d = dve(lambda e: e.tensor_copy(place, pos[:, :]), d)
            d1 = dve(lambda e: e.tensor_single_scalar(tmp[:, :], place, 7, ALU.logical_shift_right), d)
            d2 = dve(lambda e: e.tensor_single_scalar(place, place, 127, ALU.bitwise_and), d1)
            d2 = dve(lambda e: e.tensor_copy(pos[:, :], place), d2)
            d2 = dve(lambda e: e.scalar_tensor_tensor(pos[:, :], pos[:, :], float(ET), tmp[:, :], ALU.mult,
                                                      ALU.add), d2)
            d2 = dve(lambda e: e.tensor_copy(place, pos[:, :]), d2)
            t = dve(lambda e: e.tensor_scalar(tl[:, :], const("group_start"), small[:, 4, 0:1], None, ALU.is_ge), c)
            for i in range(1, NT):
                t = dve(lambda e: e.scalar_tensor_tensor(tl[:, :], const("group_start"), small[:, 4, i:i + 1],
                                                         tl[:, :], ALU.is_ge, ALU.add), t)
            t = dve(lambda e: e.tensor_scalar(tl[:, :], tl[:, :], NT - 1.0, float(D), ALU.min, ALU.mult), t)
            t = dve(lambda e: e.tensor_copy(bucket_of_group[:, :], tl[:, :]), t)
            return [d2, t]

        def edge_bias(sb, rec, ea, eaT, we, be, loaded):
            z = dve(lambda e: e.memset(we[:, :, :], 0.0))
            lw = [f.dma(act, "we", lambda e: e.dma_start(we[16 * j:16 * j + 16, j, :], I["L0_gnn_We"]), z) for j in range(8)]
            lb = f.dma(act, "be", lambda e: e.dma_start(be[:, :], vec_row(I["L0_gnn_be"], P, H)))
            freeT, freeS = {}, {}
            for j in range(EC // 8):
                s = j % 2
                t = pe(lambda e: e.transpose(bank[s][:, 0:P], ea[:, 8 * j:8 * j + 8, :].rearrange("p a b -> p (a b)"),
                                             ident), loaded, freeT.get(s))
                freeT[s] = t = act(lambda e: e.activation(eaT[:, s, :], bank[s][:, 0:P], ACT.Copy), t)
                t = pe(lambda e: e.matmul(bank[2 + s][:, 0:64], eaT[:, s, :], we[:, :, :].rearrange("p a b -> p (a b)"),
                                          start=True, stop=True), t, lw, freeS.get(s))
                freeS[s] = dve(lambda e: e.tensor_tensor(
                    rec[:, 8 * j:8 * j + 8, 0:H], bank[2 + s][:, 0:64].rearrange("p (a b) -> p a b", b=H),
                    rep(be[:, :], 8), ALU.add), t, lb)
            return [freeT[0], freeT[1], freeS[0], freeS[1]]

        def layernorm(xnT, xn, store=None):
            with ExitStack() as s:
                sb = tensors(s)
                st = sb("st", [P, NT, 6])
                mv = sb("mv", [P, NT, 2])
                rs = sb("rs", [P, NT])
                for t in range(NT):
                    a = dve(lambda e: e.bn_stats(st[:, t, :], X[:, t, :]))
                    a = dve(lambda e: e.bn_aggr(mv[:, t, :], st[:, t, :]), a)
                a = rsqrt(rs[:, :], mv[:, :, 1], EPS_LN, 1.0, a)
                freed, copied = {}, {}
                for t in range(NT):
                    b = t % 2
                    n = dve(lambda e: e.tensor_scalar(xn[:, b, :], X[:, t, :], mv[:, t, 0:1], rs[:, t:t + 1],
                                                      ALU.subtract, ALU.mult), a, freed.get(b))
                    freed[b] = []
                    if store is not None:
                        freed[b].append(f.dma(sp, f"rows{b}", lambda e: e.dma_start(store[t * P:(t + 1) * P, :],
                                                                                    xn[:, b, :]), n))
                    for c in range(KC):
                        m = pe(lambda e: e.transpose(bank[b][:, c * P:(c + 1) * P], xn[:, b, c * P:(c + 1) * P], ident),
                               n, copied.get(b))
                    freed[b].append(m)
                    copied[b] = act(lambda e: e.activation(xnT[:, :, t * P:(t + 1) * P],
                                                           bank[b][:, :].rearrange("p (c n) -> p c n", c=KC), ACT.Copy), m)
                f.stage(f.name + "n")

        def project_back(o, oT, w, acc_bank, t_bank, t, *after):
            for c in range(KC):
                a = pe(lambda e: e.transpose(t_bank[:, c * P:(c + 1) * P], o[:, c * P:(c + 1) * P], ident), *after)
            yield
            a = act(lambda e: e.activation(oT, t_bank[:, :], ACT.Copy), a)
            yield
            for c in range(KC):
                b = pe(lambda e: e.matmul(acc_bank[:, :], oT[:, c * P:(c + 1) * P], w[:, c, :], start=c == 0,
                                          stop=c == KC - 1), a)
            yield
            yield dve(lambda e: e.tensor_tensor(X[:, t, :], X[:, t, :], acc_bank[:, :], ALU.add), b)

        f.stage("ln0")
        layer0 = ExitStack()
        xnT = layer0.enter_context(nc.sbuf_tensor("xnT0", [P, KC, N], F32))
        with ExitStack() as s:
            xn = s.enter_context(nc.sbuf_tensor("xn0", [P, 2, D], F32))
            layernorm(xnT, xn)

        def write_out():
            f.dma(sp, "out", lambda e: e.dma_start(out.rearrange("(t p) d -> p t d", p=P), X[:, :, :]))
            f.stage("end")

        order = ExitStack()
        CH, CB = 16, 3
        place = order.enter_context(nc.sbuf_tensor("place", [P, 2, EC], I32))
        rec0 = order.enter_context(nc.sbuf_tensor("rec0", [P, EC, R0], F32))
        rec1 = order.enter_context(nc.sbuf_tensor("rec1", [P, CB * CH, R1], F32))
        extra = order.enter_context(nc.sbuf_tensor("extra", [P, EC, 3], F32))

        def scatter_edges(ready0, ready1, blank):
            pool.wait(ready0, blank)
            for c in range(EC):
                f.dma(pool, "scatter0", lambda e: e.indirect_dma_start(
                    out=sorted_bias, out_offset=bass.IndirectOffsetOnAxis(ap=place[:, 0, c:c + 1], axis=0),
                    in_=rec0[:, c, :], in_offset=None))
            pool.wait(ready1)
            attr = I["edge_attr_64"].rearrange("(p c) w -> p c w", p=P)
            loaded, used = {}, {}

            def load(i):
                at = i % CB * CH
                loaded[i] = [
                    f.dma(pool, f"attr{i % CB}", lambda e: e.dma_start(rec1[:, at:at + CH, 0:64], attr[:, i * CH:(i + 1) * CH, :]),
                          used.get(i - CB)),
                    pool(lambda e: e.tensor_copy(rec1[:, at:at + CH, 64:67].bitcast(I32),
                                                 extra[:, i * CH:(i + 1) * CH, :].bitcast(I32)), used.get(i - CB))]

            load(0)
            for i in range(EC // CH):
                if i + 1 < EC // CH:
                    load(i + 1)
                pool.wait(loaded[i])
                for c in range(i * CH, (i + 1) * CH):
                    used[i] = f.dma(pool, f"scatter1_{i % CB}", lambda e: e.indirect_dma_start(
                        out=sorted_edge, out_offset=bass.IndirectOffsetOnAxis(ap=place[:, 1, c:c + 1], axis=0),
                        in_=rec1[:, c % (CB * CH), :], in_offset=None))

        f.stage("perf")
        with ExitStack() as s:
            sb = tensors(s)
            tT = sb("tT", [P, KC, N])
            va = sb("va", [P, NT, H, HV])
            w = sb("w", [P, KC, D])
            wv = sb("wv", [P, KC, D])
            prj = sb("prj", [P, 2, M])
            diag = sb("diag", [P, NT, H])
            mk = sb("mk", [P, NT, H])
            cx = sb("cx", [P, H, 3, HV])
            row = sb("row", [P, 4])
            dn = HD ** -0.25

            z = dve(lambda e: e.memset(prj[:, :, :], 0.0))
            with nc.allow_non_contiguous_dma(reason="projection laid out transposed"):
                lp = [f.dma(act, "prj", lambda e: e.dma_start(prj[j * HD:(j + 1) * HD, j, :], I["L0_mix_projT"]), z)
                      for j in range(2)]
            prj2 = prj[:, :, :].rearrange("p a b -> p (a b)")
            pd = dve(lambda e: e.tensor_scalar(prj2, prj2, dn, None, ALU.mult), lp)
            lk = f.dma(sp, "w", lambda e: e.dma_start(w[:, :, :], rows(I["L0_mix_Wk"])))
            lv = f.dma(sp, "wv", lambda e: e.dma_start(wv[:, :, :], rows(I["L0_mix_Wv"])))

            def to_features(loaded, freed=None):
                freed = freed or {}
                for m in range(KC):
                    for nb in range(4):
                        b = bank[(m * 4 + nb) % 4]
                        cols = slice(nb * 512, (nb + 1) * 512)
                        for c in range(KC):
                            a = pe(lambda e: e.matmul(b[:, :], w[:, c, m * P:(m + 1) * P], xnT[:, c, cols],
                                                      start=c == 0, stop=c == KC - 1), loaded, freed.get((m * 4 + nb) % 4))
                        freed[(m * 4 + nb) % 4] = a = act(lambda e: e.activation(tT[:, m, cols], b[:, :], ACT.Copy), a)
                return a

            def squares(sq, last):
                head_of_row = const("head_of_row").rearrange("p (c h) -> p c h", c=KC)
                dg, sqfree = bank[4], {}
                for t in range(NT):
                    q = t % 2
                    a = act(lambda e: e.activation(sq[:, q, :].rearrange("p (c n) -> p c n", c=KC),
                                                   tT[:, :, t * P:(t + 1) * P], ACT.Square), last, sqfree.get(q))
                    for c in range(KC):
                        b = pe(lambda e: e.matmul(dg[:, t * H:(t + 1) * H], sq[:, q, c * P:(c + 1) * P],
                                                  head_of_row[:, c, :], start=c == 0, stop=c == KC - 1), a)
                    sqfree[q] = b
                return [last, dve(lambda e: e.tensor_scalar(diag[:, :, :].rearrange("p t h -> p (t h)"),
                                                            dg[:, 0:NT * H], -0.5 * dn * dn, None, ALU.mult), b)]

            def scores(b, t, h, *after):
                return pe(lambda e: e.matmul(b[:, 0:M], tT[:, h // 2, t * P:(t + 1) * P], prj[:, h % 2, :],
                                             start=True, stop=True), *after)

            with ExitStack() as s2:
                sb2 = tensors(s2)
                eaT = sb2("eaT", [P, 2, P])
                we = sb2("we", [P, 8, H])
                be = sb2("be", [P, H])
                pad0 = sb2("pad0", [P, ET // 8, R0])
                ends = sb2("ends", [P, 2, EC], I32)
                bkt = sb2("bkt", [P, EC])
                tmp = sb2("tmp", [P, EC], I32)
                va2 = va[:, :, :, :].rearrange("p t h d -> p (t h d)")
                hot, run = (va2[:, i * NT * EC:(i + 1) * NT * EC].rearrange("p (b c) -> p b c", b=NT) for i in range(2))
                ea = va2[:, 0:EC * 16].rearrange("p (c w) -> p c w", w=16)
                lea = f.dma(sp, "ea", lambda e: e.dma_start(ea, I["edge_attr_16"].rearrange("(p c) w -> p c w", p=P)))
                le = [f.dma(sp, f"ends{i}", lambda e: e.dma_start(ends[:, i, :], I[n].rearrange("(p c) -> p c", p=P)))
                      for i, n in enumerate(("src", "dst"))]
                blank = []
                for pad, at, width, table in ((pad0[:, :, :], H, R0, sorted_bias), (rec1[:, 0:ET // 8, :], 65, R1, sorted_edge)):
                    a = pool(lambda e: e.memset(pad, 0.0))
                    a = pool(lambda e: e.memset(pad[:, :, at:at + 1], -1.0), a)
                    n = ET // 8
                    blank += [f.dma(sp, "blank", lambda e, i=i: e.dma_start(
                        table[i * n * P:(i + 1) * n * P, :].rearrange("(p n) w -> p n w", p=P), pad), a, lea, le, lk, lv) for i in range(8)]
                eb = edge_bias(sb2, rec0, ea, eaT, we, be, lea)
                features = to_features(lk, {i: eb for i in range(4)})
                src, dst = ends[:, 0, :], ends[:, 1, :]
                fields = []
                for key, mask, out_ in ((src, P - 1, rec0[:, :, H]), (dst, G - 1, rec0[:, :, H + 1]), (dst, P - 1, extra[:, :, 1])):
                    a = dve(lambda e: e.tensor_single_scalar(tmp[:, :], key, mask, ALU.bitwise_and), le, fields)
                    fields = [dve(lambda e: e.tensor_copy(out_, tmp[:, :]), a)]
                fields.append(dve(lambda e: e.memset(extra[:, :, 0:1], 1.0)))
                fields.append(dve(lambda e: e.tensor_copy(extra[:, :, 2].bitcast(I32), src), le))
                sorted0 = edge_places(src, bkt, tmp, hot, run, sb2, bucket0, place[:, 0, :], bank[7], le[0], fields, eb)
                f.name = "perf_dst"
                sorted1 = edge_places(dst, bkt, tmp, hot, run, sb2, bucket1, place[:, 1, :], bank[7], le[1], sorted0)
                scatter_edges([sorted0, fields, eb], [sorted1, fields], blank)
                vo = dve(lambda e: e.memset(va[:, :, :, HD:HV], 1.0), sorted1)
                f.stage("perfk", pool_apart=True)
            sq = sb("sq", [P, 2, D])
            ctx_t = sb("ctx_t", [HV, M])
            ex = sb("ex", [P, 4, M])
            qf = va2[:, 0:12 * P].rearrange("p (a b n) -> p a b n", a=4, b=3)
            o, oT = (va2[:, i * 2 * D:(i + 1) * 2 * D].rearrange("p (a n) -> p a n", a=2) for i in (2, 3))
            t1 = sb("t1", [P, 4, 4])
            rc = sb("rc", [P, 2, 4])
            ready = squares(sq, None)
            freed = {}
            for t in range(NT):
                b = bank[5 + t % 2]
                for c in range(KC):
                    a = pe(lambda e: e.matmul(b[:, :], xnT[:, c, t * P:(t + 1) * P], wv[:, c, :], start=c == 0,
                                              stop=c == KC - 1), lv, freed.get(t % 2))
                freed[t % 2] = vd = act(lambda e: e.activation(va[:, t, :, 0:HD], b[:, :].rearrange(
                    "p (h d) -> p h d", h=H), ACT.Copy), a)
            freed = {}
            for n in range(NT * H):
                t, h = n // H, n % H
                a = scores(bank[n % 4], t, h, ready, pd, freed.get(n % 4))
                freed[n % 4] = mkd = dve(lambda e: e.tensor_reduce(mk[:, t, h:h + 1], bank[n % 4][:, 0:M], AX.X,
                                                                   ALU.max), a)
            a = dve(lambda e: e.tensor_reduce(row[:, 0:1], mk[:, :, :].rearrange("p t h -> p (t h)"), AX.X, ALU.max), mkd)
            a = pe(lambda e: e.transpose(bank[7][0:1, 0:P], row[:, 0:1], ident), a)
            a = dve(lambda e: e.tensor_reduce(row[0:1, 1:2], bank[7][0:1, 0:P], AX.X, ALU.max), a)
            a = pe(lambda e: e.matmul(bank[7][:, P:P + 1], ones[0:1, :], row[0:1, 1:2], start=True, stop=True), a)
            a = dve(lambda e: e.tensor_copy(row[:, 2:3], bank[7][:, P:P + 1]), a)
            shift = dve(lambda e: e.tensor_scalar(mk[:, :, :], diag[:, :, :], row[:, 2:3], None, ALU.subtract), a)
            freed, used, cfree = {}, {}, None
            for h in range(H):
                held = bank[6 + h % 2]
                pend = []
                for t in range(NT):
                    n = h * NT + t
                    q = n % 4
                    a = scores(bank[q], t, h, freed.get(q), shift)
                    freed[q] = a = act(lambda e: e.activation(ex[:, q, :], bank[q][:, 0:M], ACT.Exp,
                                                              bias=mk[:, t, h:h + 1]), a, used.get(q))
                    a = dve(lambda e: e.tensor_scalar(ex[:, q, :], ex[:, q, :], 1e-4, None, ALU.add), a)
                    pend.append((t, q, a))
                    if len(pend) > 2 or t == NT - 1:
                        for t_, q_, a_ in (pend if t == NT - 1 else pend[:1]):
                            used[q_] = b = pe(lambda e: e.matmul(held[0:HV, 0:M], va[:, t_, h, :], ex[:, q_, :],
                                                                 start=t_ == 0, stop=t_ == NT - 1), a_, vd, vo)
                        pend = pend[1:]
                c = dve(lambda e: e.tensor_copy(ctx_t[:, :], held[0:HV, 0:M]), b, cfree)
                for j, (m0, mn) in enumerate(MC):
                    cfree = pe(lambda e: e.transpose(bank[4][0:mn, j * 128:j * 128 + HV], ctx_t[:, m0:m0 + mn],
                                                     ident[0:HV, 0:HV]), c)
                for j, (m0, mn) in enumerate(MC):
                    c = dve(lambda e: e.tensor_copy(cx[0:mn, h, j, :], bank[4][0:mn, j * 128:j * 128 + HV]), cfree)
                cfree = c
            f.stage("perfq", pool_apart=True)
            lq = f.dma(sp, "w", lambda e: e.dma_start(w[:, :, :], rows(I["L0_mix_Wq"])))
            lo = f.dma(sp, "wv", lambda e: e.dma_start(wv[:, :, :], rows(I["L0_mix_Wo"])))
            squares(sq, to_features(lq))
            f.stage("perfo", pool_apart=True)
            ended = {}

            scored, normed = {}, {}

            def perf_head(n):
                t, h = n // H, n % H
                k, q, B, nb = n % 4, t % 2, bank[n % 4], bank[4 + h // 4]
                was = scored.get(n - 4)
                a = scores(B, t, h, was)
                b = dve(lambda e: e.tensor_reduce(t1[:, k, 0:1], B[:, 0:M], AX.X, ALU.max), a)
                b = dve(lambda e: e.tensor_tensor(t1[:, k, 1:2], diag[:, t, h:h + 1], t1[:, k, 0:1], ALU.subtract), b)
                yield
                a = act(lambda e: e.activation(ex[:, k, :], B[:, 0:M], ACT.Exp, bias=t1[:, k, 1:2]), b)
                yield
                for j, (m0, mn) in enumerate(MC):
                    a = pe(lambda e: e.transpose(B[0:mn, j * P:(j + 1) * P], ex[:, k, m0:m0 + mn], ident), a)
                b1 = dve(lambda e: e.tensor_scalar(qf[:, k, 0:2, :].rearrange("p a b -> p (a b)"), B[:, 0:256],
                                                   1e-4, None, ALU.add), a)
                b = dve(lambda e: e.tensor_scalar(qf[0:MC[2][1], k, 2, :], B[0:MC[2][1], 256:384], 1e-4, None, ALU.add), a)
                yield
                at = (h % 4) * HV
                for j, (m0, mn) in enumerate(MC):
                    c = pe(lambda e: e.matmul(nb[:, at:at + HV], qf[0:mn, k, j, :], cx[0:mn, h, j, :],
                                              start=j == 0, stop=j == 2), b, normed.get((t - 1, h // 4)))
                scored[n] = c
                if h % 4 == 3:
                    n4 = nb[:, 0:4 * HV].rearrange("p (h d) -> p h d", h=4)
                    d = dve(lambda e: e.reciprocal(rc[:, q, :], n4[:, :, HD]), c, normed.get((t, 0)))
                    normed[(t, h // 4)] = norm = dve(lambda e: e.tensor_tensor(
                        o[:, q, (h - 3) * HD:(h + 1) * HD].rearrange("p (h d) -> p h d", h=4), n4[:, :, 0:HD],
                        mid(rc[:, q, :], HD), ALU.mult), d, ended.get(t - 2))
                if h == H - 1:
                    yield finish(t, norm)

            def finish(t, norm):
                for r in project_back(o[:, t % 2, :], oT[:, t % 2, :], wv, bank[7], bank[6], t, norm, lo, ended.get(t - 1)):
                    yield
                ended[t] = r

            interleave((perf_head(n) for n in range(NT * H)), 4)
            f.stage("perf_end", pool_apart=True)
        f.stage("sorted")
        order.close()
        def sum_edges(width, table, bucket_of_group, acc, acc_ready, local, rhs, depth, banks, gap):
            per, some = 16, 4
            with ExitStack() as s:
                sb = tensors(s)
                rec = sb("rec", [P, 3, per, width])
                hot = sb("hot", [P, 2, per, P])
                prepare_rhs, make = rhs(sb, per)
                flat = acc[:, :, :].rearrange("p t d -> p (t d)")
                table_p = table.rearrange("(p n) w -> p n w", p=P)
                loaded, ready, ended, starts, added = {}, {}, {}, {}, {}
                sums = [acc_ready]

                def users(i, n, ago):
                    return [ended[j] for j in range(i - ago, i - ago + n)] if i >= ago else None

                def load(g):
                    loaded[g] = f.dma(sp, f"rec{g % 3}", lambda e: e.dma_start(
                        rec[:, g % 3, :, :], table_p[:, g * per:(g + 1) * per, :]), users(g * per, per, 3 * per))

                def prepare(i):
                    g, ks = i // per, slice(i % per, i % per + some)
                    h = dve(lambda e: e.tensor_tensor(hot[:, g % 2, ks, :], rep(const("iota"), some),
                                                      mid(rec[:, g % 3, ks, local], P), ALU.is_equal),
                            loaded[g], users(i, some, 2 * per))
                    r = prepare_rhs(g % 2, ks, rec[:, g % 3, ks, :], loaded[g], users(i, some, 2 * per))
                    for j in range(i, i + some):
                        ready[j] = [loaded[g], h, r]

                def tile(i):
                    g, k, q = i // per, i % per, i % depth
                    if k == some and g + 1 < ET // per:
                        load(g + 1)
                    if k % some == 0 and i + 2 * some < ET:
                        prepare(i + 2 * some)
                    b, r = g % 2, rec[:, g % 3, k, :]
                    before = ended.get(i - depth)
                    for m in make(b, k, q, r, ready[i], before):
                        yield
                    n = i // TG
                    into = bank[n % banks]
                    ended[i] = [m[1], pe(lambda e: e.matmul(into[:, :], hot[:, b, k, :], m[0], start=i % TG == 0,
                                                            stop=i % TG == TG - 1), ready[i], m[1], before,
                                         added.get(n - banks))]
                    if i % TG < TG - 1:
                        return
                    yield
                    if n % 4 == 0:
                        for j in range(n, n + 4):
                            starts[j] = dve.engine.value_load(bucket_of_group[0:1, j:j + 1], min_val=0, max_val=(NT - 1) * D)
                    at = starts.pop(n)
                    added[n] = sums[0] = dve(lambda e: e.tensor_tensor(flat[:, bass.ds(at, D)], flat[:, bass.ds(at, D)],
                                                                       into[:, :], ALU.add), ended[i], sums[0])

                load(0)
                for i in range(0, 2 * some, some):
                    prepare(i)
                interleave((tile(i) for i in range(ET)), depth, gap)
                f.stage(f.name + "s")

        def bias_rhs(sb, per):
            col = sb("col", [P, 2, per, G])
            prod = sb("prod", [P, 8, H, G])

            def prepare(b, ks, rec, loaded, used):
                return dve(lambda e: e.tensor_tensor(col[:, b, ks, :], rep(const("iota")[:, 0:G], ks.stop - ks.start),
                                                     mid(rec[:, :, H + 1], G), ALU.is_equal), loaded, used)

            def make(b, k, q, r, ready, before):
                yield (prod[:, q, :, :].rearrange("p h j -> p (h j)"),
                       pool(lambda e: e.tensor_tensor(prod[:, q, :, :], rep(col[:, b, k, :], H), mid(r[:, 0:H], G),
                                                      ALU.mult), ready, before))
            return prepare, make

        f.stage("bias")
        biased = ExitStack()
        bias = biased.enter_context(nc.sbuf_tensor("bias", [P, NT, D], F32))
        wq, wk, wv, wo = (biased.enter_context(nc.sbuf_tensor(f"att_{n}", [P, KC, D], F32)) for n in ("wq", "wk", "wv", "wo"))
        for w_, n in zip((wq, wk, wv, wo), "qkvo"):
            f.dma(act, "w", lambda e: e.dma_start(w_[:, :, :], rows(I[f"L0_gnn_W{n}"])))
        cleared = [pool(lambda e: e.memset(bias[:, 0:NT // 2, :], 0.0)), dve(lambda e: e.memset(bias[:, NT // 2:NT, :], 0.0))]
        sum_edges(R0, sorted_bias, bucket0, bias, cleared, H, bias_rhs, 8, 4, 1)

        f.stage("att")
        with ExitStack() as s:
            sb = tensors(s)
            loads = []
            bq, bk = sb("bq", [P, KC]), sb("bk", [P, KC])
            bkp = sb("bkp", [P, 2, KC])
            bv = sb("bv", [G, D])
            bo = sb("bo", [P, 2, D])
            with nc.allow_non_contiguous_dma(reason="small bias columns"):
                loads.append(f.dma(act, "b", lambda e: e.dma_start(bq[:, :], I["L0_gnn_bq"].rearrange("(c p) -> p c", p=P))))
                loads.append(f.dma(act, "b", lambda e: e.dma_start(bk[:, :], I["L0_gnn_bk"].rearrange("(c p) -> p c", p=P))))
            loads.append(f.dma(act, "b", lambda e: e.dma_start(bv[:, :], vec_row(I["L0_gnn_bv"], G, D))))
            loads.append(f.dma(act, "b", lambda e: e.dma_start(bo[:, 0, :], vec_row(I["L0_gnn_bo"], P, D))))
            loads.append(f.dma(act, "b", lambda e: e.dma_start(bo[:, 1, :], vec_row(I["L0_mix_bo"], P, D))))
            par = const("parity")
            for j in range(2):
                bkd = dve(lambda e: e.tensor_scalar(bkp[:, j, :], bk[:, :], par[:, j:j + 1], None, ALU.mult), loads)
            bod = dve(lambda e: e.tensor_tensor(bo[:, 0, :], bo[:, 0, :], bo[:, 1, :], ALU.add), loads)
            qT = sb("qT", [P, 2, KC, P])
            kT = sb("kT", [P, 2, 2, KC, P])
            v = sb("v", [G, 2, 2, D])
            sc = sb("sc", [P, 2, D])
            pT = sb("pT", [G, 2, H, P])
            o = sb("o", [P, 2, D])
            oT = sb("oT", [P, 2, D])
            mx = sb("mx", [P, 2, 3, H])
            ended = {}

            def att_tile(t):
                q = t % 2
                B = bank[4 * q:4 * q + 4]
                was = ended.get(t - 2)
                nodes = slice(t * P, (t + 1) * P)
                bx = pool(lambda e: e.tensor_tensor(X[:, t, :], X[:, t, :], bo[:, 0, :], ALU.add), bod)
                for w, b in ((wq, B[0]), (wk, B[1])):
                    for m in range(KC):
                        for c in range(KC):
                            a = pe(lambda e: e.matmul(b[:, m * P:(m + 1) * P], w[:, c, m * P:(m + 1) * P],
                                                      xnT[:, c, nodes], start=c == 0, stop=c == KC - 1), loads, was)
                    yield
                for g in range(2):
                    for c in range(KC):
                        av = pe(lambda e: e.matmul(B[2 + g][0:G, :], xnT[:, c, t * P + g * G:t * P + (g + 1) * G],
                                                   wv[:, c, :], start=c == 0, stop=c == KC - 1))
                B0 = B[0][:, :].rearrange("p (c n) -> p c n", c=KC)
                B1 = B[1][:, :].rearrange("p (c n) -> p c n", c=KC)
                qd = dve(lambda e: e.tensor_tensor(qT[:, q, :, :], B0, mid(bq[:, :], P), ALU.add), a, was)
                for j in range(2):
                    kd = dve(lambda e: e.scalar_tensor_tensor(kT[:, q, j, :, :], B1, par[:, j:j + 1],
                                                              mid(bkp[:, j, :], P), ALU.mult, ALU.add), bkd)
                for g in range(2):
                    vd = dve(lambda e: e.tensor_tensor(v[:, q, g, :], B[2 + g][0:G, :], bv[:, :], ALU.add), av)
                yield
                for h in range(H):
                    for g in range(2):
                        cols = slice(g * G, (g + 1) * G)
                        a = pe(lambda e: e.matmul(B[0][cols, h * G:(h + 1) * G], qT[:, q, h // 2, cols],
                                                  kT[:, q, h % 2, h // 2, cols], start=True, stop=True), kd)
                yield
                s3 = sc[:, q, :].rearrange("p (h j) -> p h j", h=H)
                a = dve(lambda e: e.scalar_tensor_tensor(sc[:, q, :], B[0][:, :], HD ** -0.5, bias[:, t, :],
                                                         ALU.mult, ALU.add), a)
                a = dve(lambda e: e.tensor_reduce(mx[:, q, 0, :], s3, AX.X, ALU.max), a)
                yield
                a = dve(lambda e: e.tensor_tensor(s3, s3, mid(mx[:, q, 0, :], G), ALU.subtract), a)
                x = act(lambda e: e.activation(sc[:, q, :], sc[:, q, :], ACT.Exp), a)
                yield
                for h in range(H):
                    a = pe(lambda e: e.transpose(B[1 + h // 4][0:G, (h % 4) * P:(h % 4 + 1) * P],
                                                 s3[:, h, :], ident), x, vd)
                b = dve(lambda e: e.tensor_reduce(mx[:, q, 1, :], s3, AX.X, ALU.add), x)
                b = dve(lambda e: e.reciprocal(mx[:, q, 2, :], mx[:, q, 1, :]), b)
                yield
                for j in range(2):
                    a = act(lambda e: e.activation(pT[:, q, 4 * j:4 * j + 4, :].rearrange("p h n -> p (h n)"),
                                                   B[1 + j][0:G, :], ACT.Copy), a)
                yield
                for h in range(H):
                    for g in range(2):
                        cols = slice(g * G, (g + 1) * G)
                        m = pe(lambda e: e.matmul(B[3][cols, h * HD:(h + 1) * HD], pT[:, q, h, cols],
                                                  v[:, q, g, h * HD:(h + 1) * HD], start=True, stop=True), a, vd)
                yield
                a = dve(lambda e: e.tensor_tensor(o[:, q, :].rearrange("p (h j) -> p h j", h=H),
                                                  B[3][:, :].rearrange("p (h j) -> p h j", h=H),
                                                  mid(mx[:, q, 2, :], HD), ALU.mult), m, b)
                yield
                for r in project_back(o[:, q, :], oT[:, q, :], wo, B[1], B[0], t, a, bx):
                    yield
                ended[t] = r

            interleave((att_tile(t) for t in range(NT)), 2)
            f.stage("att_end")
        biased.close()

        layer0.close()
        f.stage("ln1")
        layer, normed = ExitStack(), ExitStack()
        slot_of = layer.enter_context(nc.sbuf_tensor("slot_of", [P, 2, NT], I32))
        slot_w = layer.enter_context(nc.sbuf_tensor("slot_w", [P, 2, NT], F32))
        xnT = normed.enter_context(nc.sbuf_tensor("xnT1", [P, KC, N], F32))
        wts = [normed.enter_context(nc.sbuf_tensor(f"ffn_w{n}", [P, KC, D], F32)) for n in "qkvg"]
        for w_, n in zip(wts, "qkvg"):
            f.dma(sp, "w", lambda e: e.dma_start(w_[:, :, :], rows(I[f"L0_ffn_W{n}"])))
        with ExitStack() as s:
            xn = s.enter_context(nc.sbuf_tensor("xn1", [P, 2, D], F32))
            layernorm(xnT, xn)

        def slots_of(sel, pos, base, tot, groups, *after):
            n = groups * NT
            pe(lambda e: e.matmul(bank[0][:, 0:n], const("before"), sel, start=True, stop=True), *after)
            a = pe(lambda e: e.matmul(bank[1][:, 0:n], ones, sel, start=True, stop=True))
            b = dve(lambda e: e.tensor_copy(tot, bank[1][:, 0:n]), a)
            c = dve(lambda e: e.tensor_tensor_scan(base, tot, tot, 0.0, ALU.add, ALU.max), b)
            c = dve(lambda e: e.tensor_tensor(base, base, tot, ALU.subtract), c)
            return dve(lambda e: e.tensor_tensor(pos, base, bank[0][:, 0:n], ALU.add), c)

        f.stage("route")
        with ExitStack() as s:
            sb = tensors(s)
            ws = sb("ws", [P, KC, 20])
            lw = [f.dma(sp, "w", lambda e: e.dma_start(ws[:, :, a:b], rows(I[f"L0_ffn_W{n}"])))
                  for n, a, b in (("gate", 0, 4), ("b", 4, 12), ("a", 12, 20))]
            dtb, alog = sb("dtb", [P, H]), sb("alog", [P, H])
            lb = [f.dma(act, "b", lambda e: e.dma_start(dtb[:, :], vec_row(I["L0_ffn_dt_bias"], P, H))),
                  f.dma(act, "b", lambda e: e.dma_start(alog[:, :], vec_row(I["L0_ffn_A_log"], P, H)))]
            sm = sb("sm", [P, NT, 20])
            for t in range(NT):
                for c in range(KC):
                    a = pe(lambda e: e.matmul(bank[2][:, t * 20:(t + 1) * 20], xnT[:, c, t * P:(t + 1) * P],
                                              ws[:, c, :], start=c == 0, stop=c == KC - 1), lw)
            sm2 = sm[:, :, :].rearrange("p t n -> p (t n)")
            a = dve(lambda e: e.tensor_copy(sm2, bank[2][:, 0:NT * 20]), a)
            big = {n: sb(n, [P, EX, NT]) for n in ("lg", "pr", "sel", "w", "prev", "pos", "base", "tot", "first", "tmp",
                                                   "reset")}
            V = {n: t[:, :, :] for n, t in big.items()}
            flat = {n: v.rearrange("p e t -> p (e t)") for n, v in V.items()}
            cmp = sb("cmp", [P, EX, EX, NT])
            equal = sb("equal", [P, EX, EX, NT])
            mx = sb("mx", [P, NT])
            a = dve(lambda e: e.tensor_copy(V["lg"], sm[:, :, 0:EX].rearrange("p t e -> p e t")), a)
            b = dve(lambda e: e.tensor_reduce(mx[:, :], V["lg"].rearrange("p e t -> p t e"), AX.X, ALU.max), a)
            lg = dve(lambda e: e.tensor_tensor(V["lg"], V["lg"], rep(mx[:, :], EX), ALU.subtract), b)
            pr = act(lambda e: e.activation(flat["pr"], flat["lg"], ACT.Exp), lg)
            other = V["lg"].unsqueeze(1).broadcast_to([P, EX, EX, NT])
            own = V["lg"].unsqueeze(2).broadcast_to([P, EX, EX, NT])
            a = dve(lambda e: e.tensor_tensor(cmp[:, :, :, :], other, own, ALU.is_gt), lg)
            b = dve(lambda e: e.tensor_tensor(equal[:, :, :, :], other, own, ALU.is_equal), lg)
            eq3 = equal[:, :, :, :].rearrange("p e i t -> p (e i) t")
            b = dve(lambda e: e.tensor_tensor(eq3, eq3, mid(const("earlier"), NT), ALU.mult), b)
            a = dve(lambda e: e.tensor_tensor(cmp[:, :, :, :], cmp[:, :, :, :], equal[:, :, :, :], ALU.add), a, b)
            for x in range(EX):
                a1 = dve(lambda e: e.tensor_reduce(V["sel"][:, x, :], cmp[:, x, :, :].rearrange("p i t -> p t i"), AX.X,
                                                   ALU.add), a)
            sel = dve(lambda e: e.tensor_scalar(flat["sel"], flat["sel"], 1.5, None, ALU.is_lt), a1)
            a = dve(lambda e: e.tensor_tensor(V["w"], V["pr"], V["sel"], ALU.mult), sel, pr)
            b = dve(lambda e: e.tensor_reduce(mx[:, :], V["w"].rearrange("p e t -> p t e"), AX.X, ALU.add), a)
            b = dve(lambda e: e.reciprocal(mx[:, :], mx[:, :]), b)
            w_ = dve(lambda e: e.tensor_tensor(V["w"], V["w"], rep(mx[:, :], EX), ALU.mult), b)
            a = dve(lambda e: e.memset(V["prev"][:, 0, :], 0.0))
            for x in range(1, EX):
                a = dve(lambda e: e.tensor_tensor(V["prev"][:, x, :], V["prev"][:, x - 1, :], V["sel"][:, x - 1, :],
                                                  ALU.add), a, sel)
            prev = a
            pos = slots_of(flat["sel"], flat["pos"], flat["base"], flat["tot"], EX, sel)
            rs = dve(lambda e: e.tensor_tensor(V["reset"], V["pos"], mid(V["base"][:, :, 0], NT), ALU.is_equal), pos)
            picked = sb("picked", [P, 2, 3, NT])
            a = None
            for j in range(2):
                if j == 0:
                    c = dve(lambda e: e.tensor_tensor(V["first"], V["sel"], V["prev"], ALU.mult), prev)
                    c = dve(lambda e: e.tensor_tensor(V["first"], V["sel"], V["first"], ALU.subtract), c)
                else:
                    c = dve(lambda e: e.tensor_tensor(V["first"], V["sel"], V["prev"], ALU.mult), a)
                a = c
                for k, n in enumerate(("pos", "w", "reset")):
                    a = dve(lambda e: e.tensor_tensor(V["tmp"], V["first"], V[n], ALU.mult), c, a, pos, w_, rs)
                    a = dve(lambda e: e.tensor_reduce(picked[:, j, k, :], V["tmp"].rearrange("p e t -> p t e"), AX.X,
                                                      ALU.add), a)
            for j in range(2):
                dve(lambda e: e.tensor_copy(slot_of[:, j, :], picked[:, j, 0, :]), a)
                pk = dve(lambda e: e.tensor_copy(slot_w[:, j, :], picked[:, j, 1, :]), a)
            gt = sb("gt", [P, 6, NT, H])
            ga = sb("ga", [P, 2, NT, 2 * H])
            al = sb("al", [P, 2, NT])
            a = act(lambda e: e.activation(gt[:, 0, :, :], sm[:, :, 4:12], ACT.Exp, scale=-1.0), pk)
            a = dve(lambda e: e.tensor_scalar(gt[:, 0, :, :], gt[:, 0, :, :], 1.0, None, ALU.add), a)
            beta = dve(lambda e: e.reciprocal(gt[:, 0, :, :], gt[:, 0, :, :]), a)
            a = act(lambda e: e.activation(alog[:, :], alog[:, :], ACT.Exp), lb)
            na = dve(lambda e: e.tensor_scalar(alog[:, :], alog[:, :], -1.0, None, ALU.mult), a)
            z = dve(lambda e: e.tensor_tensor(gt[:, 1, :, :], sm[:, :, 12:20], rep(dtb[:, :], NT), ALU.add), lb)
            a = dve(lambda e: e.scalar_tensor_tensor(gt[:, 2, :, :], gt[:, 1, :, :], -1.0, gt[:, 1, :, :], ALU.mult,
                                                     ALU.max), z)
            a = act(lambda e: e.activation(gt[:, 3, :, :], gt[:, 2, :, :], ACT.Exp, scale=-1.0), a)
            a = dve(lambda e: e.tensor_scalar(gt[:, 3, :, :], gt[:, 3, :, :], 1.0, None, ALU.add), a)
            a = act(lambda e: e.activation(gt[:, 3, :, :], gt[:, 3, :, :], ACT.Ln), a)
            a = dve(lambda e: e.scalar_tensor_tensor(gt[:, 4, :, :], gt[:, 1, :, :], 0.0, gt[:, 3, :, :], ALU.max,
                                                     ALU.add), a)
            g = dve(lambda e: e.tensor_tensor(gt[:, 4, :, :], gt[:, 4, :, :], rep(alog[:, :], NT), ALU.mult), a, na)
            for j in range(2):
                a = dve(lambda e: e.tensor_scalar(al[:, j, :], picked[:, j, 1, :], 0.0, None, ALU.is_gt), pk)
                dve(lambda e: e.tensor_tensor(ga[:, j, :, 0:H], gt[:, 0, :, :], mid(al[:, j, :], H), ALU.mult), a, beta)
                b = dve(lambda e: e.tensor_tensor(gt[:, 5, :, :], gt[:, 4, :, :], mid(al[:, j, :], H), ALU.mult), a, g)
                g = dve(lambda e: e.scalar_tensor_tensor(ga[:, j, :, H:2 * H], mid(picked[:, j, 2, :], H), RESET,
                                                         gt[:, 5, :, :], ALU.mult, ALU.add), b)
            f.stage("qkv")
            rw = sb("rw", [P, 2, 3 * D])
            gr = sb("gr", [P, 2, D])
            sq = sb("sq", [P, 2, 2 * D])
            ss = sb("ss", [P, 2, 2 * H])
            ended = {}

            def qkv_tile(t):
                q = t % 2
                B = bank[4 * q:4 * q + 4]
                was = ended.get(t - 2)
                for i in range(4):
                    for c in range(KC):
                        a = pe(lambda e: e.matmul(B[i][:, :], xnT[:, c, t * P:(t + 1) * P], wts[i][:, c, :], start=c == 0,
                                                  stop=c == KC - 1), was)
                    if i < 3:
                        b = act(lambda e: e.activation(rw[:, q, i * D:(i + 1) * D], B[i][:, :], ACT.Silu), a, was)
                    else:
                        g = act(lambda e: e.activation(gr[:, q, :], B[i][:, :], ACT.Silu), a, was)
                    yield
                sg = f.dma(sp, f"gate{q}", lambda e: e.dma_start(gate_rows[t * P:(t + 1) * P, :], gr[:, q, :]), g)
                a = pool(lambda e: e.tensor_tensor(sq[:, q, :], rw[:, q, 0:2 * D], rw[:, q, 0:2 * D], ALU.mult), b)
                yield
                a = dve(lambda e: e.tensor_reduce(ss[:, q, :], sq[:, q, :].rearrange("p (h d) -> p h d", d=HD), AX.X,
                                                  ALU.add), a)
                a = rsqrt(ss[:, q, :], ss[:, q, :], 1e-6, 1.0, a)
                yield
                a = dve(lambda e: e.tensor_scalar(ss[:, q, 0:H], ss[:, q, 0:H], HD ** -0.5, None, ALU.mult), a)
                qk = rw[:, q, 0:2 * D].rearrange("p (h d) -> p h d", d=HD)
                a = dve(lambda e: e.tensor_tensor(qk, qk, mid(ss[:, q, :], HD), ALU.mult), a)
                yield
                pool.wait(a)
                for j in range(2):
                    off = bass.IndirectOffsetOnAxis(ap=slot_of[:, j, t:t + 1], axis=0)
                    s1 = f.dma(pool, f"slots{q}", lambda e: e.indirect_dma_start(
                        out=slot_qkv, out_offset=off, in_=rw[:, q, :], in_offset=None))
                    f.dma(pool, "slotg", lambda e: e.indirect_dma_start(
                        out=slot_gates, out_offset=off, in_=ga[:, j, t, :], in_offset=None))
                ended[t] = [s1, sg, a]

            interleave((qkv_tile(t) for t in range(NT)), 2, 4)
            f.stage("qkv_end")
        normed.close()

        f.stage("gates")
        deltas = ExitStack()
        sb = tensors(deltas)
        gt = sb("gt", [P, ST, 2 * H])
        eg = sb("eg", [P, 3, ST, H])
        bg = sb("bg", [P, ST, H])
        l2 = f.dma(sp, "gt", lambda e: e.dma_start(gt[:, :, :], slot_gates.rearrange("(t p) n -> p t n", p=P)))
        for i, n in enumerate(("upto", "ones", "after")):
            a = pe(lambda e: e.matmul(bank[i][:, 0:ST * H], const(n), gt[:, :, H:2 * H], start=True, stop=True), l2)
            x = act(lambda e: e.activation(eg[:, i, :, :].rearrange("p t h -> p (t h)"), bank[i][:, 0:ST * H], ACT.Exp), a)
        dve(lambda e: e.tensor_tensor(bg[:, :, :], gt[:, :, 0:H], eg[:, 0, :, :], ALU.mult), x)
        f.stage("delta")
        with deltas:
            sb = tensors(deltas)
            HG = H // 2
            W = HG * HD
            B8 = [P, 2, H, P]
            PR = H // 2
            state = sb("state", [P, 2, PR, P])
            decayed = sb("decayed", [P, PR, P])
            rw = sb("rw", [P, 4, 3, D])
            dec, A, X_, Z, T, att = (sb(n, B8) for n in ("dec", "A", "X", "Z", "T", "att"))
            kT, qT = (sb(n, [P, 2, PR, P]) for n in ("kT", "qT"))
            kT1 = sb("kT1", [P, 2, PR, 2, P])
            kd, vb, r_, u, o = (sb(n, [P, 2, H, HD]) for n in ("kd", "vb", "r", "u", "o"))
            ds = sb("ds", [P, PR, P])
            zero = pool(lambda e: e.memset(state[:, :, :, :], 0.0))
            ended, loaded = {}, {}
            chain = [{"state": zero, "read": None, "n": 0} for _ in range(2)]

            def flat4(ap):
                return ap.rearrange("p h n -> p (h n)")

            def load(t):
                loaded[t] = f.dma(sp, f"rw{t % 4}", lambda e: e.dma_start(
                    rw[:, t % 4, :, :], slot_qkv[t * P:(t + 1) * P, :].rearrange("p (a d) -> p a d", a=3)),
                    ended.get((t - 4, 0)), ended.get((t - 4, 1)))

            def delta_tile(t, g):
                q, hs, ps = t % 2, slice(g * HG, (g + 1) * HG), slice(g * HG // 2, (g + 1) * HG // 2)
                heads, pairs = range(g * HG, (g + 1) * HG), range(g * HG // 2, (g + 1) * HG // 2)
                left, right = bank[2 * (2 * q + g)], bank[2 * (2 * q + g) + 1]
                was = ended.get((t - 2, g))
                link = chain[g]
                if g == 0 and t + 2 < ST:
                    load(t + 2)
                l1 = loaded[t]
                Q, K, Vv = (rw[:, t % 4, i, g * W:(g + 1) * W].rearrange("p (h d) -> p h d", d=HD) for i in range(3))
                beta, lg = gt[:, t, hs], gt[:, t, H + g * HG:H + (g + 1) * HG]
                up, total, rest = (eg[:, i, t, hs] for i in range(3))

                def full(b, i):
                    return b[:, i * P:(i + 1) * P]

                def four(b):
                    return b[:, :].rearrange("p (h n) -> p h n", h=HG)

                def wide(b, at=0):
                    return b[:, at:at + W].rearrange("p (h d) -> p h d", h=HG)

                gu = pool(lambda e: e.tensor_tensor(Z[:, q, hs, :], rep(const("after"), HG), mid(lg, P), ALU.mult), was)
                for i, p_ in enumerate(pairs):
                    for j, src in enumerate((K, Q)):
                        a = pe(lambda e: e.transpose(full(left, 2 * j + i), flat4(src[:, 2 * i:2 * i + 2, :]), ident),
                               l1, was)
                kk = act(lambda e: e.activation(flat4(kT[:, q, ps, :]), left[:, 0:W], ACT.Copy), a, was)
                qq = act(lambda e: e.activation(flat4(qT[:, q, ps, :]), left[:, W:2 * W], ACT.Copy))
                kdd = pool(lambda e: e.tensor_tensor(kd[:, q, hs, :], K, mid(rest, HD), ALU.mult), l1, was)
                vd = pool(lambda e: e.tensor_tensor(vb[:, q, hs, :], Vv, mid(beta, HD), ALU.mult))
                yield
                for j in range(2):
                    k1 = dve(lambda e: e.tensor_scalar(kT1[:, q, ps, j, :], kT[:, q, ps, :], const("parity")[:, j:j + 1],
                                                       None, ALU.mult), kk, was)
                a = pe(lambda e: e.matmul(right[:, :], const("upto"), flat4(Z[:, q, hs, :]), start=True, stop=True), gu, was)
                ed = act(lambda e: e.activation(flat4(dec[:, q, hs, :]), right[:, :], ACT.Exp), a, was)
                yield
                for i, p_ in enumerate(pairs):
                    a = pe(lambda e: e.matmul(left[:, 2 * i * P:2 * (i + 1) * P], kT[:, q, p_, :], flat4(kT1[:, q, p_, :, :]),
                                              start=True, stop=True), k1, qq)
                for i, h in enumerate(heads):
                    ad = dve(lambda e: e.scalar_tensor_tensor(A[:, q, h, :], full(left, i), gt[:, t, h:h + 1],
                                                              dec[:, q, h, :], ALU.mult, ALU.mult), a, ed, was)
                yield
                for i, p_ in enumerate(pairs):
                    a = pe(lambda e: e.matmul(right[:, 2 * i * P:2 * (i + 1) * P], qT[:, q, p_, :],
                                              flat4(kT1[:, q, p_, :, :]), start=True, stop=True), ed)
                md = dve(lambda e: e.tensor_tensor(dec[:, q, hs, :], dec[:, q, hs, :], four(right), ALU.mult), a, ad)
                lo = pool(lambda e: e.tensor_tensor(dec[:, q, hs, :], dec[:, q, hs, :], rep(const("lower"), HG), ALU.mult), md)
                for i, h in enumerate(heads):
                    a = pe(lambda e: e.transpose(full(left, i), A[:, q, h, :], ident), ad)
                z_used = [gu, a]
                for b_ in LEVELS:
                    if b_ > 1:
                        for i, h in enumerate(heads):
                            a = pe(lambda e: e.matmul(full(left, i), A[:, q, h, :], T[:, q, h, :], start=True, stop=True), td)
                    zd = dve(lambda e: e.tensor_tensor(Z[:, q, hs, :], four(left), rep(const(f"fill{b_}"), HG), ALU.mult),
                             a, z_used)
                    yield
                    if b_ == 1:
                        td = pool(lambda e: e.tensor_tensor(T[:, q, hs, :], rep(ident, HG), Z[:, q, hs, :], ALU.subtract),
                                  zd, was)
                    else:
                        for i, h in enumerate(heads):
                            a = pe(lambda e: e.matmul(full(right, i), X_[:, q, h, :], Z[:, q, h, :], start=True, stop=True),
                                   zd, xd)
                        z_used = a
                        td = dve(lambda e: e.tensor_tensor(T[:, q, hs, :], T[:, q, hs, :], four(right), ALU.subtract), a)
                    yield
                    if b_ < LEVELS[-1]:
                        for i, h in enumerate(heads):
                            a = pe(lambda e: e.transpose(full(right, i), T[:, q, h, :], ident), td, md)
                        xd = act(lambda e: e.activation(flat4(X_[:, q, hs, :]), right[:, :], ACT.Copy), a, z_used, was)
                        if b_ == 1:
                            z_used = td
                        yield
                for i, h in enumerate(heads):
                    a = pe(lambda e: e.transpose(full(left, i), dec[:, q, h, :], ident), lo, zd)
                mt = act(lambda e: e.activation(flat4(att[:, q, hs, :]), left[:, :], ACT.Copy), a, was)
                old, new = state[:, link["n"] % 2, :, :], state[:, (link["n"] + 1) % 2, :, :]
                link["n"] += 1
                dc = pool(lambda e: e.tensor_tensor(flat4(decayed[:, ps, :]).rearrange("p (h d) -> p h d", d=HD),
                                                    flat4(old[:, ps, :]).rearrange("p (h d) -> p h d", d=HD),
                                                    mid(total, HD), ALU.mult), link["state"])
                for j, rows_ in enumerate((kT, qT)):
                    for i, p_ in enumerate(pairs):
                        a = pe(lambda e: e.matmul(full(right, 2 * j + i), rows_[:, q, p_, :], old[:, p_, :], start=True,
                                                  stop=True), td, link["state"])
                b = dve(lambda e: e.tensor_tensor(r_[:, q, hs, :], wide(right), mid(bg[:, t, hs], HD), ALU.mult), a, was)
                b = dve(lambda e: e.tensor_tensor(r_[:, q, hs, :], vb[:, q, hs, :], r_[:, q, hs, :], ALU.subtract), b, vd)
                od = dve(lambda e: e.tensor_tensor(o[:, q, hs, :], wide(right, W), mid(up, HD), ALU.mult), a, was)
                yield
                for i, h in enumerate(heads):
                    a = pe(lambda e: e.matmul(left[:, i * HD:(i + 1) * HD], T[:, q, h, :], r_[:, q, h, :], start=True,
                                              stop=True), b, mt)
                ud = act(lambda e: e.activation(u[:, q, hs, :], wide(left), ACT.Copy), a, was)
                yield
                for i, p_ in enumerate(pairs):
                    a = pe(lambda e: e.matmul(full(right, i), flat4(kd[:, q, 2 * p_:2 * p_ + 2, :]),
                                              flat4(u[:, q, 2 * p_:2 * p_ + 2, :]), start=True, stop=True), ud, kdd, od)
                for i, h in enumerate(heads):
                    c = pe(lambda e: e.matmul(left[:, i * HD:(i + 1) * HD], att[:, q, h, :], u[:, q, h, :], start=True,
                                              stop=True))
                ns = dve(lambda e: e.tensor_tensor(ds[:, ps, :], right[:, 0:W].rearrange("p (i n) -> p i n", n=P),
                                                   rep(const("same_half"), HG // 2), ALU.mult), a, link["state"])
                ns = dve(lambda e: e.tensor_tensor(new[:, ps, :], decayed[:, ps, :], ds[:, ps, :], ALU.add),
                         ns, dc, link["read"])
                link["state"], link["read"] = ns, c
                od = dve(lambda e: e.tensor_tensor(o[:, q, hs, :], o[:, q, hs, :], wide(left), ALU.add), c, od)
                ended[(t, g)] = [od, ns, f.dma(sp, f"out{q}{g}", lambda e: e.dma_start(
                    slot_out[t * P:(t + 1) * P, g * W:(g + 1) * W], flat4(o[:, q, hs, :])), od)]

            load(0)
            load(1)
            interleave((delta_tile(t, g) for t in range(ST) for g in range(2)), 4, 7)
            f.stage("delta_end")

        f.stage("merge")
        with ExitStack() as s:
            sb = tensors(s)
            wo = sb("wo", [P, KC, D])
            onw = sb("onw", [P, HD])
            ab = sb("ab", [P, 4, 3, D])
            ss = sb("ss", [P, 4, H])
            oT = sb("oT", [P, 4, D])
            lw = f.dma(sp, "w", lambda e: e.dma_start(wo[:, :, :], rows(I["L0_ffn_Wo"])))
            ln = f.dma(sp, "n", lambda e: e.dma_start(onw[:, :], vec_row(I["L0_ffn_o_norm_weight"], P, HD)))
            ended = {}

            def merge_tile(t):
                q = t % 4
                B = bank[2 * q:2 * q + 2]
                was = ended.get(t - 4)
                pool.wait(was)
                for j in range(2):
                    g = f.dma(pool, f"in{q}", lambda e: e.indirect_dma_start(
                        out=ab[:, q, j, :], out_offset=None, in_=slot_out,
                        in_offset=bass.IndirectOffsetOnAxis(ap=slot_of[:, j, t:t + 1], axis=0)))
                g2 = f.dma(sp, f"gate{q}", lambda e: e.dma_start(ab[:, q, 2, :], gate_rows[t * P:(t + 1) * P, :]), was)
                yield
                o = ab[:, q, 0, :]
                a = dve(lambda e: e.tensor_scalar(o, o, slot_w[:, 0, t:t + 1], None, ALU.mult), g)
                a = dve(lambda e: e.scalar_tensor_tensor(o, ab[:, q, 1, :], slot_w[:, 1, t:t + 1], o, ALU.mult, ALU.add), a)
                b = pool(lambda e: e.tensor_tensor(ab[:, q, 1, :], o, o, ALU.mult), a)
                yield
                b = dve(lambda e: e.tensor_reduce(ss[:, q, :], ab[:, q, 1, :].rearrange("p (h d) -> p h d", d=HD), AX.X,
                                                  ALU.add), b, was)
                b = rsqrt(ss[:, q, :], ss[:, q, :], 1e-5, 1.0 / HD, b)
                o3 = o.rearrange("p (h d) -> p h d", d=HD)
                a = dve(lambda e: e.tensor_tensor(o, o, ab[:, q, 2, :], ALU.mult), g2, a, b)
                a = dve(lambda e: e.tensor_tensor(o3, o3, mid(ss[:, q, :], HD), ALU.mult), a, b)
                a = dve(lambda e: e.tensor_tensor(o3, o3, rep(onw[:, :], H), ALU.mult), a, ln)
                yield
                for r in project_back(o, oT[:, q, :], wo, B[1], B[0], t, a, lw, was):
                    yield
                ended[t] = [r, a]

            interleave((merge_tile(t) for t in range(NT)), 4, 2)
            f.stage("merge_end")
        layer.close()
        f.stage("ln2")
        layer = ExitStack()
        xnT = layer.enter_context(nc.sbuf_tensor("xnT2", [P, KC, N], F32))
        wq, wk, wv, wo = (layer.enter_context(nc.sbuf_tensor(f"lin_{n}", [P, KC, D], F32)) for n in ("wq", "wk", "wv", "wo"))
        for i, w_ in enumerate((wq, wk, wv)):
            f.dma(sp, "w", lambda e: e.dma_start(w_[:, :, :], rows(I["L1_mix_W_qkvT"])[:, :, i * D:(i + 1) * D]))
        f.dma(sp, "w", lambda e: e.dma_start(wo[:, :, :], rows(I["L1_mix_W_projT"])))
        with ExitStack() as s:
            xn = s.enter_context(nc.sbuf_tensor("xn2", [P, 2, D], F32))
            layernorm(xnT, xn, xn_rows)
        f.stage("lin")
        with ExitStack() as s:
            sb = tensors(s)
            bo = sb("bo", [P, D])
            lb = f.dma(act, "b", lambda e: e.dma_start(bo[:, :], vec_row(I["L1_mix_b_proj"], P, D)))
            k = sb("k", [P, 2, D])
            va = sb("va", [P, 2, H, HV])
            kv = sb("kv", [P, KC, 2, HV])
            qT = sb("qT", [P, 2, KC, P])
            o = sb("o", [P, 2, D])
            oT = sb("oT", [P, 2, D])
            rc = sb("rc", [P, 2, H])
            z = pool(lambda e: e.memset(kv[:, :, :, :], 0.0))
            on = pool(lambda e: e.memset(va[:, :, :, HD:HV], 1.0))
            ended = {}

            def kv_tile(t):
                q = t % 2
                B = bank[2 * q:2 * q + 2]
                was = ended.get(t - 2)
                for b, w in ((B[0], wk), (B[1], wv)):
                    for c in range(KC):
                        a = pe(lambda e: e.matmul(b[:, :], xnT[:, c, t * P:(t + 1) * P], w[:, c, :], start=c == 0,
                                                  stop=c == KC - 1), was)
                    if w is wk:
                        x = dve(lambda e: e.tensor_scalar(k[:, q, :], b[:, :], 0.0, HD ** -0.5, ALU.max, ALU.add), a, was)
                    else:
                        y = act(lambda e: e.activation(va[:, q, :, 0:HD], b[:, :].rearrange("p (h d) -> p h d", h=H),
                                                       ACT.Copy), a, was)
                    yield
                for p_ in range(KC):
                    a = pe(lambda e: e.matmul(bank[4 + p_][:, 0:2 * HV], k[:, q, p_ * P:(p_ + 1) * P],
                                              va[:, q, 2 * p_:2 * p_ + 2, :].rearrange("p h d -> p (h d)"),
                                              start=t == 0, stop=t == NT - 1), x, y, on)
                ended[t] = a

            interleave((kv_tile(t) for t in range(NT)), 2)
            for p_ in range(KC):
                for j in range(2):
                    half = slice(j * HD, (j + 1) * HD)
                    kd = dve(lambda e: e.tensor_copy(kv[half, p_, j, :], bank[4 + p_][half, j * HV:(j + 1) * HV]),
                             ended[NT - 1], z)
            f.stage("lino")
            ended = {}

            def lin_tile(t):
                q = t % 2
                B = bank[4 * q:4 * q + 4]
                was = ended.get(t - 2)
                bx = pool(lambda e: e.tensor_tensor(X[:, t, :], X[:, t, :], bo[:, :], ALU.add), lb)
                for m in range(KC):
                    for c in range(KC):
                        a = pe(lambda e: e.matmul(B[0][:, m * P:(m + 1) * P], wq[:, c, m * P:(m + 1) * P],
                                                  xnT[:, c, t * P:(t + 1) * P], start=c == 0, stop=c == KC - 1), was)
                yield
                a = dve(lambda e: e.tensor_scalar(qT[:, q, :, :].rearrange("p c n -> p (c n)"), B[0][:, :], 0.0, HD ** -0.5,
                                                  ALU.max, ALU.add), a, was)
                yield
                for p_ in range(KC):
                    b = pe(lambda e: e.matmul(B[1 + p_ // 2][:, (p_ % 2) * 2 * HV:(p_ % 2 + 1) * 2 * HV], qT[:, q, p_, :],
                                              kv[:, p_, :, :].rearrange("p h d -> p (h d)"), start=True, stop=True), a)
                yield
                for j in range(2):
                    n4 = B[1 + j][:, 0:4 * HV].rearrange("p (h d) -> p h d", h=4)
                    a = dve(lambda e: e.tensor_scalar(rc[:, q, 4 * j:4 * j + 4], n4[:, :, HD], 1e-6, None, ALU.add), b, was)
                    a = dve(lambda e: e.reciprocal(rc[:, q, 4 * j:4 * j + 4], rc[:, q, 4 * j:4 * j + 4]), a)
                    a = dve(lambda e: e.tensor_tensor(o[:, q, j * 256:(j + 1) * 256].rearrange("p (h d) -> p h d", h=4),
                                                      n4[:, :, 0:HD], mid(rc[:, q, 4 * j:4 * j + 4], HD), ALU.mult), a)
                yield
                for r in project_back(o[:, q, :], oT[:, q, :], wo, B[3], B[0], t, a, bx):
                    yield
                ended[t] = [r, a]

            interleave((lin_tile(t) for t in range(NT)), 2)
            f.stage("lin_end")
        layer.close()

        f.stage("conv")
        layer = ExitStack()
        acc = layer.enter_context(nc.sbuf_tensor("acc", [P, NT, D], F32))
        epsr = layer.enter_context(nc.sbuf_tensor("epsr", [P, 1], F32))
        a = f.dma(sp, "xn", lambda e: e.dma_start(acc[:, :, :], xn_rows.rearrange("(t p) d -> p t d", p=P)))
        b = f.dma(sp, "eps", lambda e: e.dma_start(epsr[:, :], vec_row(I["L1_gnn_eps"], P, 1)))
        b = dve(lambda e: e.tensor_scalar(epsr[:, :], epsr[:, :], 1.0, None, ALU.add), b)
        for t in range(NT):
            scaled = dve(lambda e: e.tensor_scalar(acc[:, t, :], acc[:, t, :], epsr[:, 0:1], None, ALU.mult), a, b)
        wes = ExitStack()
        we = wes.enter_context(nc.sbuf_tensor("we", [65, D], F32))
        lwe = [f.dma(sp, "we", lambda e: e.dma_start(we[0:64, :], I["L1_gnn_W_e"])),
               f.dma(sp, "we", lambda e: e.dma_start(we[64:65, :], vec_row(I["L1_gnn_b_e"], 1, D)))]

        def message_rhs(sb, per):
            src = sb("src", [P, 6, D])
            msg = sb("msg", [P, 6, D])
            eT = sb("eT", [65, 6, P])

            def make(b, k, q, r, ready, before):
                pool.wait(ready, before)
                g = f.dma(pool, f"src{q}", lambda e: e.indirect_dma_start(
                    out=src[:, q, :], out_offset=None, in_=xn_rows,
                    in_offset=bass.IndirectOffsetOnAxis(ap=r[:, 66:67].bitcast(I32), axis=0)))
                a = pe(lambda e: e.transpose(bank[2 + q][0:65, 0:P], r[:, 0:65], ident), ready, before)
                yield
                a = act(lambda e: e.activation(eT[:, q, :], bank[2 + q][0:65, 0:P], ACT.Copy), a)
                yield
                a = pe(lambda e: e.matmul(bank[2 + q][:, :], eT[:, q, :], we[:, :], start=True, stop=True), a, lwe)
                yield
                a = dve(lambda e: e.tensor_tensor(msg[:, q, :], bank[2 + q][:, :], src[:, q, :], ALU.add), a, g)
                yield
                a = act(lambda e: e.activation(msg[:, q, :], msg[:, q, :], ACT.Relu), a)
                yield (msg[:, q, :], a)
            return lambda *x: None, make

        sum_edges(R1, sorted_edge, bucket1, acc, scaled, 65, message_rhs, 6, 2, 1)
        wes.close()

        f.stage("mlp")
        NB = N // 512
        with ExitStack() as s:
            sb = tensors(s)
            hT = sb("hT", [P, KC, N])
            freed = {}
            for t in range(NT):
                b = bank[t % 2]
                for c in range(KC):
                    a = pe(lambda e: e.transpose(b[:, c * P:(c + 1) * P], acc[:, t, c * P:(c + 1) * P], ident), freed.get(t % 2))
                freed[t % 2] = act(lambda e: e.activation(hT[:, :, t * P:(t + 1) * P],
                                                          b[:, :].rearrange("p (c n) -> p c n", c=KC), ACT.Copy), a)
            f.stage("mlp1")
            h1 = sb("h1", [P, 2 * KC, N])
            w2 = sb("w2", [P, 2 * KC, D])
            w1 = acc[:, :, :].rearrange("p a b -> p (a b)")[:, 0:KC * 2 * D].rearrange("p (c n) -> p c n", c=KC)
            st = sb("st", [P, 2 * KC, NB, 6])
            mv = sb("mv", [P, 2 * KC, 2])
            vec = sb("vec", [P, 6, 2 * KC])
            l1 = f.dma(sp, "w1", lambda e: e.dma_start(w1, rows(I["L1_gnn_W1"])))
            l2 = f.dma(sp, "w2", lambda e: e.dma_start(w2[:, :, :], rows(I["L1_gnn_W2"])))
            with nc.allow_non_contiguous_dma(reason="small columns"):
                lb = [f.dma(act, "v", lambda e: e.dma_start(vec[:, i, 0:w], I["L1_gnn_" + n].rearrange("(c p) -> p c", p=P)))
                      for i, (n, w) in enumerate((("b1", 8), ("g1", 8), ("beta1", 8), ("b2", 4), ("g2", 4), ("beta2", 4)))]

            def norm_layer(tag, n_out, w, src, n_in, dst, v, loaded):
                freed, i = {}, 0
                for m in range(n_out):
                    for nb in range(NB):
                        b = bank[i % 4]
                        cols = slice(nb * 512, (nb + 1) * 512)
                        for c in range(n_in):
                            a = pe(lambda e: e.matmul(b[:, :], w[:, c, m * P:(m + 1) * P], src[:, c, cols],
                                                      start=c == 0, stop=c == n_in - 1), loaded, freed.get(i % 4))
                        freed[i % 4] = a = act(lambda e: e.activation(dst[:, m, cols], b[:, :], ACT.Identity,
                                                                      bias=vec[:, v, m:m + 1]), a, lb)
                        a = dve(lambda e: e.bn_stats(st[:, m, nb, :], dst[:, m, cols]), a)
                        i += 1
                    a = dve(lambda e: e.bn_aggr(mv[:, m, :], st[:, m, :, :].rearrange("p a b -> p (a b)")), a)
                f.stage(tag + "n")
                r = rsqrt(mv[:, 0:n_out, 1], mv[:, 0:n_out, 1], 1e-5, 1.0)
                sc = dve(lambda e: e.tensor_tensor(mv[:, 0:n_out, 1], mv[:, 0:n_out, 1], vec[:, v + 1, 0:n_out], ALU.mult), r)
                a = dve(lambda e: e.tensor_tensor(mv[:, 0:n_out, 0], mv[:, 0:n_out, 0], mv[:, 0:n_out, 1], ALU.mult), sc)
                a = dve(lambda e: e.tensor_tensor(mv[:, 0:n_out, 0], vec[:, v + 2, 0:n_out], mv[:, 0:n_out, 0],
                                                  ALU.subtract), a)
                for m in range(n_out):
                    a = act(lambda e: e.activation(dst[:, m, :], dst[:, m, :], ACT.Silu, bias=mv[:, m, 0:1],
                                                   scale=mv[:, m, 1:2]), a)
                f.stage(tag + "e")

            norm_layer("bn1", 2 * KC, w1, hT, KC, h1, 0, l1)
            norm_layer("bn2", KC, w2, h1, 2 * KC, hT, 3, None)
            freed = {}
            for t in range(NT):
                b = bank[t % 2]
                for c in range(KC):
                    a = pe(lambda e: e.transpose(b[:, c * P:(c + 1) * P], hT[:, c, t * P:(t + 1) * P], ident), freed.get(t % 2))
                freed[t % 2] = dve(lambda e: e.tensor_tensor(X[:, t, :], X[:, t, :], b[:, :], ALU.add), a)
            f.stage("mlp_end")
        layer.close()

        f.stage("ln3")
        layer = ExitStack()
        xnT = layer.enter_context(nc.sbuf_tensor("xnT3", [P, KC, N], F32))
        slot_of = layer.enter_context(nc.sbuf_tensor("slot_of3", [P, NT], I32))
        slot_w = layer.enter_context(nc.sbuf_tensor("slot_w3", [P, NT], F32))
        ew = layer.enter_context(nc.sbuf_tensor("ew", [P, 4, KC, D], F32))
        for x in range(4):
            f.dma(act, "ew", lambda e: e.dma_start(ew[:, x, :, :], rows(I["L1_ffn_experts"][x])))
        with ExitStack() as s:
            sb = tensors(s)
            xn = sb("xn", [P, 2, D])
            zero = sb("zero", [P, D])
            a = pool(lambda e: e.memset(zero[:, :], 0.0))
            for t in range(NT):
                f.dma(sp, "zero", lambda e: e.dma_start(expert_in[t * P:(t + 1) * P, :], zero[:, :]), a)
            layernorm(xnT, xn, xn_rows)
        f.stage("sink")
        with ExitStack() as s:
            sb = tensors(s)
            wg = sb("wg", [P, KC, FE])
            lw = f.dma(sp, "w", lambda e: e.dma_start(wg[:, :, :], rows(I["L1_ffn_gate_weight"][0])))
            big = {n: sb(n, [P, FE, NT]) for n in ("g", "sel", "w", "later", "pos", "base", "tot", "win", "tmp")}
            V = {n: t[:, :, :] for n, t in big.items()}
            flat = {n: v.rearrange("p e t -> p (e t)") for n, v in V.items()}
            r8 = sb("r8", [P, FE])
            r16 = sb("r16", [P, NT])
            for t in range(NT):
                for c in range(KC):
                    a = pe(lambda e: e.matmul(bank[2][:, t * FE:(t + 1) * FE], xnT[:, c, t * P:(t + 1) * P], wg[:, c, :],
                                              start=c == 0, stop=c == KC - 1), lw)
            a = dve(lambda e: e.tensor_scalar(V["g"], bank[2][:, 0:NT * FE].rearrange("p (t e) -> p e t", e=FE), 1e-6, None,
                                              ALU.max), a)
            for it in range(8):
                a = dve(lambda e: e.tensor_reduce(r8[:, :], V["g"], AX.X, ALU.add), a)
                a = pe(lambda e: e.matmul(bank[3][:, 0:FE], ones, r8[:, :], start=True, stop=True), a)
                a = dve(lambda e: e.reciprocal(r8[:, :], bank[3][:, 0:FE]), a)
                a = dve(lambda e: e.tensor_tensor(V["g"], V["g"], mid(r8[:, :], NT), ALU.mult), a)
                a = dve(lambda e: e.tensor_reduce(r16[:, :], V["g"].rearrange("p e t -> p t e"), AX.X, ALU.add), a)
                a = dve(lambda e: e.reciprocal(r16[:, :], r16[:, :]), a)
                a = dve(lambda e: e.tensor_tensor(V["g"], V["g"], rep(r16[:, :], FE), ALU.mult), a)
            def count(*after):
                b = dve(lambda e: e.tensor_reduce(r8[:, :], V["tmp"], AX.X, ALU.add), *after)
                return pe(lambda e: e.matmul(bank[3][:, 0:FE], ones, r8[:, :], start=True, stop=True), b)

            least, tried, step = (sb(n, [P, FE]) for n in ("least", "tried", "step"))
            gd = [a, dve(lambda e: e.memset(least[:, :], 0.0))]
            a = gd
            for k in range(29, -1, -1):
                a = dve(lambda e: e.tensor_single_scalar(tried[:, :].bitcast(I32), least[:, :].bitcast(I32), 1 << k,
                                                         ALU.bitwise_or), a)
                a = dve(lambda e: e.tensor_tensor(V["tmp"], V["g"], mid(tried[:, :], NT), ALU.is_ge), a)
                a = dve(lambda e: e.tensor_scalar(step[:, :].bitcast(I32), bank[3][:, 0:FE], CAP - 0.5, float(1 << k),
                                                  ALU.is_ge, ALU.mult), count(a))
                a = dve(lambda e: e.tensor_tensor(least[:, :].bitcast(I32), least[:, :].bitcast(I32),
                                                  step[:, :].bitcast(I32), ALU.bitwise_or), a)
            above = dve(lambda e: e.tensor_tensor(V["tmp"], V["g"], mid(least[:, :], NT), ALU.is_gt), a)
            missing = dve(lambda e: e.tensor_scalar(r8[:, :], bank[3][:, 0:FE], -1.0, float(CAP), ALU.mult, ALU.add),
                          count(above))
            equal = dve(lambda e: e.tensor_tensor(V["win"], V["g"], mid(least[:, :], NT), ALU.is_equal), a)
            a = slots_of(flat["win"], flat["pos"], flat["base"], flat["tot"], FE, equal)
            a = dve(lambda e: e.tensor_tensor(V["pos"], V["pos"], mid(V["base"][:, :, 0], NT), ALU.subtract), a)
            a = dve(lambda e: e.tensor_tensor(V["pos"], V["pos"], mid(r8[:, :], NT), ALU.is_lt), a, missing)
            a = dve(lambda e: e.tensor_tensor(V["pos"], V["pos"], V["win"], ALU.mult), a, equal)
            sel = dve(lambda e: e.tensor_tensor(V["sel"], V["tmp"], V["pos"], ALU.add), a, above)
            pos = slots_of(flat["sel"], flat["pos"], flat["base"], flat["tot"], FE, sel)
            a = dve(lambda e: e.memset(V["later"][:, FE - 1, :], 0.0))
            for x in range(FE - 2, -1, -1):
                a = dve(lambda e: e.tensor_tensor(V["later"][:, x, :], V["later"][:, x + 1, :], V["sel"][:, x + 1, :],
                                                  ALU.max), a, sel)
            a = dve(lambda e: e.tensor_tensor(V["win"], V["sel"], V["later"], ALU.is_gt), a, sel)
            w_ = dve(lambda e: e.tensor_tensor(V["tmp"], V["win"], V["g"], ALU.mult), a)
            w_ = dve(lambda e: e.tensor_reduce(slot_w[:, :], V["tmp"].rearrange("p e t -> p t e"), AX.X, ALU.add), w_)
            b = dve(lambda e: e.tensor_tensor(V["tmp"], V["win"], V["pos"], ALU.mult), w_, pos)
            b = dve(lambda e: e.tensor_reduce(r16[:, :], V["tmp"].rearrange("p e t -> p t e"), AX.X, ALU.add), b)
            c = dve(lambda e: e.tensor_reduce(V["later"][:, 0, :], V["win"].rearrange("p e t -> p t e"), AX.X, ALU.add), a, b)
            put = sb("put", [P, NT], I32)
            c = dve(lambda e: e.tensor_scalar(V["later"][:, 0, :], V["later"][:, 0, :], -float(N), float(N), ALU.mult,
                                              ALU.add), c)
            c = dve(lambda e: e.tensor_tensor(V["later"][:, 0, :], V["later"][:, 0, :], r16[:, :], ALU.add), c)
            c = dve(lambda e: e.tensor_copy(put[:, :], V["later"][:, 0, :]), c)
            c1 = dve(lambda e: e.tensor_copy(slot_of[:, :], r16[:, :]), b)
            xr = sb("xr", [P, 4, D])
            used = {}
            for t in range(NT):
                q = t % 4
                l = f.dma(sp, f"xr{q}", lambda e: e.dma_start(xr[:, q, :], xn_rows[t * P:(t + 1) * P, :]), used.get(q))
                pool.wait(l, c, c1)
                used[q] = f.dma(pool, f"put{q}", lambda e: e.indirect_dma_start(
                    out=expert_in, out_offset=bass.IndirectOffsetOnAxis(ap=put[:, t:t + 1], axis=0),
                    in_=xr[:, q, :], in_offset=None, bounds_check=N - 1, oob_is_err=False))
            f.stage("experts")
            xe = sb("xe", [P, 4, D])
            xT = sb("xT", [P, 4, D])
            ye = sb("ye", [P, 4, D])
            wfree, ended = {}, {}
            loaded = {}

            def expert_tile(t):
                q, x = t % 4, t // 2
                was = ended.get(t - 4)
                if t % 2 == 1 and x >= 2 and x + 2 < FE:
                    loaded[x + 2] = f.dma(act, f"ew{(x + 2) % 4}", lambda e: e.dma_start(
                        ew[:, (x + 2) % 4, :, :], rows(I["L1_ffn_experts"][x + 2])), wfree[x - 2])
                l = f.dma(sp, f"xe{q}", lambda e: e.dma_start(xe[:, q, :], expert_in[t * P:(t + 1) * P, :]), was)
                yield
                B = bank[2 * q:2 * q + 2]
                for c in range(KC):
                    a = pe(lambda e: e.transpose(B[0][:, c * P:(c + 1) * P], xe[:, q, c * P:(c + 1) * P], ident), l, was)
                yield
                a = act(lambda e: e.activation(xT[:, q, :], B[0][:, :], ACT.Copy), a)
                yield
                for c in range(KC):
                    a = pe(lambda e: e.matmul(B[1][:, :], xT[:, q, c * P:(c + 1) * P], ew[:, x % 4, c, :], start=c == 0,
                                              stop=c == KC - 1), a, loaded.get(x))
                wfree[x] = a
                yield
                a = dve(lambda e: e.tensor_copy(ye[:, q, :], B[1][:, :]), a, was)
                ended[t] = [a, f.dma(sp, f"ye{q}", lambda e: e.dma_start(expert_out[t * P:(t + 1) * P, :], ye[:, q, :]), a)]

            interleave((expert_tile(t) for t in range(NT)), 4, 2)
            f.stage("combine")
            used = {}
            for t in range(NT):
                q = t % 4
                pool.wait(used.get(q))
                l = f.dma(pool, f"in{q}", lambda e: e.indirect_dma_start(
                    out=xr[:, q, :], out_offset=None, in_=expert_out,
                    in_offset=bass.IndirectOffsetOnAxis(ap=slot_of[:, t:t + 1], axis=0)))
                used[q] = dve(lambda e: e.scalar_tensor_tensor(X[:, t, :], xr[:, q, :], slot_w[:, t:t + 1], X[:, t, :],
                                                               ALU.mult, ALU.add), l)
        f.stage("store")
        layer.close()
        write_out()


def kernel(**inputs):
    import concourse.bacc as _bacc
    from concourse.bass_utils import run_bass_kernel_spmd as _run

    nc = _bacc.Bacc("TRN2", target_bir_lowering=False, num_devices=1)
    table, const_at = constants()
    arrays, args = {}, {}
    for name, a in list(inputs.items()) + [("const", table), ("L0_mix_projT", np.asarray(inputs["L0_mix_proj"]).T),
                                        ("L1_mix_W_qkvT", np.asarray(inputs["L1_mix_W_qkv"]).T),
                                        ("L1_mix_W_projT", np.asarray(inputs["L1_mix_W_proj"]).T)]:
        a = np.asarray(a)
        if a.ndim == 0:
            a = a.reshape(1)
        a = np.ascontiguousarray(a)
        arrays[f"in_{name}"] = a
        args[name] = nc.dram_tensor(f"in_{name}", a.shape, mybir.dt.from_np(a.dtype), kind="ExternalInput").ap()
    out = nc.dram_tensor("out_0", (N, D), F32, kind="ExternalOutput").ap()
    program(nc, args, const_at, out)
    r = _run(nc, [arrays], core_ids=[0])
    return r.results[0]["out_0"]
```
